# Optimizing a Trainium2 kernel written in Bass

```python
import numpy as np
import jax
import jax.numpy as jnp

def _softmax(x, axis=-1):
    return jax.nn.softmax(x, axis=axis)

def _gelu(x):
    return jax.nn.gelu(x, approximate=True)

def _silu(x):
    return jax.nn.silu(x)

def _sigmoid(x):
    return jax.nn.sigmoid(x)

def _layernorm(x, axis=-1, eps=1e-05):
    m = jnp.mean(x, axis=axis, keepdims=True)
    v = jnp.var(x, axis=axis, keepdims=True)
    return (x - m) / jnp.sqrt(v + eps)

def _scatter_add(tgt, idx, src, axis=0):
    return tgt.at[idx].add(src)

def _segment_sum(src, seg, n):
    return jax.ops.segment_sum(src, seg, n)
kernel_name = 'mk_adaln_attn_ffn_d1_seqx_r4_358874'

def setup_inputs(seed: int=0):
    np.random.seed(seed)
    _w = jnp.asarray

    def _rec_inputs():
        import jax
        import jax.numpy as jnp
        _rk = jax.random.key(seed)
        x = 7.22e-05 + 1 * jax.random.normal(jax.random.fold_in(_rk, 1), (8, 256, 256), jnp.float32)
        _lenS = 256 - jax.random.randint(jax.random.fold_in(_rk, 7), (8,), 0, max(1, 256 // 4) + 1, jnp.int32)
        _lenS2 = 256 - jax.random.randint(jax.random.fold_in(_rk, 8), (8,), 0, max(1, 256 // 4) + 1, jnp.int32)
        itok_BxS_0_999 = jax.random.randint(jax.random.fold_in(_rk, 11), (8, 256), 0, 250, jnp.int32)
        itok_BxS_0_4 = jax.random.randint(jax.random.fold_in(_rk, 12), (8, 256), 0, 5, jnp.int32)
        cond_512 = 0.00199304 + 1.00034 * jax.random.normal(jax.random.fold_in(_rk, 14), (8, 128), jnp.float32)
        cond_64 = 0.0990542 + 1.04422 * jax.random.normal(jax.random.fold_in(_rk, 15), (8, 64), jnp.float32)
        fside_Bx32_0 = -0.136436 + 0.990155 * jax.random.normal(jax.random.fold_in(_rk, 16), (8, 32), jnp.float32)
        _validS = jnp.arange(256)[None, :] < _lenS[:, None]
        _validS2 = jnp.arange(256)[None, :] < _lenS2[:, None]
        _causal = jnp.tril(jnp.ones((256, 256), dtype=bool))
        mask_BxS_ik0 = jnp.where(jnp.broadcast_to(_validS[:, :], (8, 256)), 0, 1).astype(jnp.int32)
        return (x, itok_BxS_0_999, itok_BxS_0_4, cond_512, cond_64, fside_Bx32_0, mask_BxS_ik0)
    x, itok_BxS_0_999, itok_BxS_0_4, cond_512, cond_64, fside_Bx32_0, mask_BxS_ik0 = _rec_inputs()

    def _L0_cond_setup():
        import jax, jax.numpy as jnp
        import numpy as np
        EPS = 1e-05

        def _ln(x, g, b):
            m = jnp.mean(x, axis=-1, keepdims=True)
            v = jnp.mean((x - m) ** 2, axis=-1, keepdims=True)
            return (x - m) * jax.lax.rsqrt(v + EPS) * g + b

        def _mlp_ln(s, W1, b1, W2, b2, g, b):
            h = jax.nn.silu(s @ W1 + b1) @ W2 + b2
            return _ln(h, g, b)
        key = jax.random.key(seed)
        B, S, D = (4, 512, 256)
        MEM, NOI, RES = (128, 64, 32)
        ks = jax.random.split(key, 40)
        ki = iter(range(40))

        def nrm(shape, scale=0.02):
            return jax.random.normal(ks[next(ki)], shape, jnp.float32) * scale

        def gamma(shape):
            return jnp.ones(shape, jnp.float32) + nrm(shape)
        inp = {'x': jax.random.normal(ks[next(ki)], (B, S, D), jnp.float32), 'pathway_ids': jax.random.randint(ks[next(ki)], (B, S), 0, 250), 'compartment_ids': jax.random.randint(ks[next(ki)], (B, S), 0, 5), 'time_steps': jax.random.randint(ks[next(ki)], (B, S), 0, 5), 'scale_type': jax.random.randint(ks[next(ki)], (B, S), 0, 3), 'memory_state': jax.random.normal(ks[next(ki)], (B, MEM), jnp.float32), 'noise_state': jax.random.normal(ks[next(ki)], (B, NOI), jnp.float32), 'resource_state': jax.random.normal(ks[next(ki)], (B, RES), jnp.float32), 'pw_g': gamma((250, D)), 'pw_b': nrm((250, D)), 'cp_g': gamma((5, D)), 'cp_b': nrm((5, D)), 'tm_g': gamma((5, D)), 'tm_b': nrm((5, D)), 'ms_g': gamma((3, D)), 'ms_b': nrm((3, D)), 'mem_W1': nrm((MEM, D)), 'mem_b1': jnp.zeros((D,)), 'mem_W2': nrm((D, D)), 'mem_b2': jnp.zeros((D,)), 'mem_g': gamma((D,)), 'mem_be': jnp.zeros((D,)), 'noi_W1': nrm((NOI, D)), 'noi_b1': jnp.zeros((D,)), 'noi_W2': nrm((D, D)), 'noi_b2': jnp.zeros((D,)), 'noi_g': gamma((D,)), 'noi_be': jnp.zeros((D,)), 'res_W1': nrm((RES, D)), 'res_b1': jnp.zeros((D,)), 'res_W2': nrm((D, D)), 'res_b2': jnp.zeros((D,)), 'res_g': gamma((D,)), 'res_be': jnp.zeros((D,)), 'int_W1': nrm((6 * D, D)), 'int_b1': jnp.zeros((D,)), 'int_W2': nrm((D, D)), 'int_b2': jnp.zeros((D,)), 'int_g': gamma((D,)), 'int_be': jnp.zeros((D,)), 'aw': jnp.ones((6,), jnp.float32) / 6.0}
        return inp
    _L0_cond_all = _L0_cond_setup()
    _L0_cond_in = {k: v for k, v in _L0_cond_all.items() if k in ('pw_g', 'pw_b', 'cp_g', 'cp_b', 'tm_g', 'tm_b', 'ms_g', 'ms_b', 'mem_W1', 'mem_b1', 'mem_W2', 'mem_b2', 'mem_g', 'mem_be', 'noi_W1', 'noi_b1', 'noi_W2', 'noi_b2', 'noi_g', 'noi_be', 'res_W1', 'res_b1', 'res_W2', 'res_b2', 'res_g', 'res_be', 'int_W1', 'int_b1', 'int_W2', 'int_b2', 'int_g', 'int_be', 'aw')}
    del _L0_cond_all

    def _L0_attn_setup():
        import jax, jax.numpy as jnp
        import numpy as np
        ALPHA = 1.0
        N_HEADS = 16
        key = jax.random.key(seed)
        ks = jax.random.split(key, 3)
        B, N, D = (2, 512, 256)
        x = jax.random.normal(ks[0], (B, N, D), dtype=jnp.float32)
        W_qkv = jax.random.normal(ks[1], (D, 3 * D), dtype=jnp.float32) * D ** (-0.5)
        b_qkv = jnp.zeros((3 * D,), dtype=jnp.float32)
        W_proj = jax.random.normal(ks[2], (D, D), dtype=jnp.float32) * D ** (-0.5)
        b_proj = jnp.zeros((D,), dtype=jnp.float32)
        return {'x': x, 'W_qkv': W_qkv, 'b_qkv': b_qkv, 'W_proj': W_proj, 'b_proj': b_proj}
    _L0_attn_all = _L0_attn_setup()
    _L0_attn_in = {k: v for k, v in _L0_attn_all.items() if k in ('W_qkv', 'b_qkv', 'W_proj', 'b_proj')}
    del _L0_attn_all

    def _L0_cond2_setup():
        import jax, jax.numpy as jnp
        import numpy as np
        import math
        HEAD_NUM = 16
        EPS = 1e-08

        def modulated_linear(x, s, aff_w, aff_b, w, b):
            style = s @ aff_w.T + aff_b
            w_mod = w[None, :, :] * style[:, None, :]
            demod = jax.lax.rsqrt(jnp.sum(w_mod * w_mod, axis=2) + EPS)
            w_mod = w_mod * demod[:, :, None]
            return jnp.einsum('bni,boi->bno', x, w_mod) + b
        key = jax.random.key(seed)
        ks = jax.random.split(key, 6)
        B, N, F, S = (8, 256, 256, 128)
        return {'x': jax.random.normal(ks[0], (B, N, F), dtype=jnp.float32), 's': jax.random.normal(ks[1], (B, S), dtype=jnp.float32), 'k_aff_w': jax.random.normal(ks[2], (F, S), dtype=jnp.float32) * 0.02, 'k_aff_b': jnp.ones((F,), dtype=jnp.float32), 'k_w': jax.random.normal(ks[3], (F, F), dtype=jnp.float32) * 0.02, 'k_b': jnp.zeros((F,), dtype=jnp.float32), 'o_aff_w': jax.random.normal(ks[4], (F, S), dtype=jnp.float32) * 0.02, 'o_aff_b': jnp.ones((F,), dtype=jnp.float32), 'o_w': jax.random.normal(ks[5], (F, F), dtype=jnp.float32) * 0.02, 'o_b': jnp.zeros((F,), dtype=jnp.float32)}
    _L0_cond2_all = _L0_cond2_setup()
    _L0_cond2_in = {k: v for k, v in _L0_cond2_all.items() if k in ('k_aff_w', 'k_aff_b', 'k_w', 'k_b', 'o_aff_w', 'o_aff_b', 'o_w', 'o_b')}
    del _L0_cond2_all

    def _L0_ffn_setup():
        import jax, jax.numpy as jnp
        import numpy as np
        DIM = 256
        DEPTH = 6
        HEADS = 16
        DIM_HEAD = 64
        WINDOW = 64
        INNER = HEADS * DIM_HEAD
        DIM_INNER = int(DIM * 4 * 2 / 3)
        QK_SCALE = 8.0

        def shift_tokens(t):
            a, s = jnp.split(t, 2, -1)
            s = jnp.pad(s, ((0, 0), (1, 0), (0, 0)))[:, :-1]
            return jnp.concatenate([a, s], -1)

        def l2norm(t):
            return t / jnp.maximum(jnp.linalg.norm(t, axis=-1, keepdims=True), 1e-12)

        def rotate_half(x):
            x1, x2 = jnp.split(x, 2, -1)
            return jnp.concatenate([-x2, x1], -1)

        def rotary_tables(n):
            half = jnp.arange(0, DIM_HEAD, 2, dtype=jnp.float32)
            inv_freq = 1.0 / 10000.0 ** (half / DIM_HEAD)
            t = jnp.arange(n, dtype=jnp.float32)
            freqs = t[:, None] * inv_freq[None, :]
            freqs = jnp.concatenate([freqs, freqs], -1)
            base_scale = (half + 0.4 * DIM_HEAD) / (1.4 * DIM_HEAD)
            power = (t - n // 2) / (WINDOW // 2)
            scale = base_scale[None, :] ** power[:, None]
            scale = jnp.concatenate([scale, scale], -1)
            return (freqs, scale)

        def local_attention(q, k, v):
            b, h, n, d = q.shape
            w = WINDOW
            nw = n // w
            bq = q.reshape(b, h, nw, w, d)
            bk = k.reshape(b, h, nw, w, d)
            bv = v.reshape(b, h, nw, w, d)

            def look(t):
                p = jnp.pad(t, ((0, 0), (0, 0), (1, 0), (0, 0), (0, 0)))
                return jnp.concatenate([p[:, :, :nw], p[:, :, 1:]], axis=3)
            bk2, bv2 = (look(bk), look(bv))
            seq = jnp.arange(n).reshape(nw, w)
            seq_p = jnp.pad(seq, ((1, 0), (0, 0)), constant_values=-1)
            jt = jnp.concatenate([seq_p[:nw], seq_p[1:]], axis=1)
            it = seq[:, :, None]
            jb = jt[:, None, :]
            mask = (it < jb) | (it > jb + w) | (jb == -1)
            sim = jnp.einsum('bhwie,bhwje->bhwij', bq, bk2) * QK_SCALE
            sim = jnp.where(mask, -jnp.finfo(sim.dtype).max, sim)
            attn = jax.nn.softmax(sim, -1)
            out = jnp.einsum('bhwij,bhwje->bhwie', attn, bv2)
            return out.reshape(b, h, n, d)

        def attn_layer(x, Wqkv, qs, ksc, Wo):
            b, n, _ = x.shape
            qkv = x @ Wqkv
            q, k, v = jnp.split(qkv, 3, -1)
            sh = lambda t: t.reshape(b, n, HEADS, DIM_HEAD).transpose(0, 2, 1, 3)
            q, k, v = (sh(q), sh(k), sh(v))
            q = l2norm(q) * qs
            k = l2norm(k) * ksc
            freqs, scale = rotary_tables(n)
            cos, sin = (jnp.cos(freqs), jnp.sin(freqs))
            q = q * cos * scale + rotate_half(q) * sin * scale
            inv = 1.0 / scale
            k = k * cos * inv + rotate_half(k) * sin * inv
            out = local_attention(q, k, v)
            out = out.transpose(0, 2, 1, 3).reshape(b, n, INNER)
            return out @ Wo

        def ffn_layer(x, g, bln, W1, b1, W2, b2):
            mu = x.mean(-1, keepdims=True)
            var = ((x - mu) ** 2).mean(-1, keepdims=True)
            xn = (x - mu) / jnp.sqrt(var + 1e-05) * g + bln
            hg = xn @ W1 + b1
            a, gate = jnp.split(hg, 2, -1)
            return a * jax.nn.gelu(gate, approximate=False) @ W2 + b2
        key = jax.random.key(seed)
        ks = jax.random.split(key, 8)
        B, N = (2, 512)
        init = lambda k, shape: jax.random.normal(k, shape, jnp.float32) * 0.02
        return {'x': jax.random.normal(ks[0], (B, N, DIM), jnp.float32), 'Wqkv': init(ks[1], (DEPTH, DIM, 3 * INNER)), 'q_scale': jnp.ones((DEPTH, DIM_HEAD), jnp.float32), 'k_scale': jnp.ones((DEPTH, DIM_HEAD), jnp.float32), 'Wo': init(ks[2], (DEPTH, INNER, DIM)), 'ln_g': jnp.ones((DEPTH, DIM), jnp.float32), 'ln_b': jnp.zeros((DEPTH, DIM), jnp.float32), 'W1': init(ks[3], (DEPTH, DIM, 2 * DIM_INNER)), 'b1': jnp.zeros((DEPTH, 2 * DIM_INNER), jnp.float32), 'W2': init(ks[4], (DEPTH, DIM_INNER, DIM)), 'b2': jnp.zeros((DEPTH, DIM), jnp.float32)}
    _L0_ffn_all = _L0_ffn_setup()
    _L0_ffn_in = {k: v for k, v in _L0_ffn_all.items() if k in ('Wqkv', 'q_scale', 'k_scale', 'Wo', 'ln_g', 'ln_b', 'W1', 'b1', 'W2', 'b2')}
    del _L0_ffn_all
    return {'x': x, 'itok_BxS_0_999': itok_BxS_0_999, 'itok_BxS_0_4': itok_BxS_0_4, 'cond_512': cond_512, 'cond_64': cond_64, 'fside_Bx32_0': fside_Bx32_0, 'mask_BxS_ik0': mask_BxS_ik0, 'L0_cond_pw_g': _L0_cond_in['pw_g'], 'L0_cond_pw_b': _L0_cond_in['pw_b'], 'L0_cond_cp_g': _L0_cond_in['cp_g'], 'L0_cond_cp_b': _L0_cond_in['cp_b'], 'L0_cond_tm_g': _L0_cond_in['tm_g'], 'L0_cond_tm_b': _L0_cond_in['tm_b'], 'L0_cond_ms_g': _L0_cond_in['ms_g'], 'L0_cond_ms_b': _L0_cond_in['ms_b'], 'L0_cond_mem_W1': _L0_cond_in['mem_W1'], 'L0_cond_mem_b1': _L0_cond_in['mem_b1'], 'L0_cond_mem_W2': _L0_cond_in['mem_W2'], 'L0_cond_mem_b2': _L0_cond_in['mem_b2'], 'L0_cond_mem_g': _L0_cond_in['mem_g'], 'L0_cond_mem_be': _L0_cond_in['mem_be'], 'L0_cond_noi_W1': _L0_cond_in['noi_W1'], 'L0_cond_noi_b1': _L0_cond_in['noi_b1'], 'L0_cond_noi_W2': _L0_cond_in['noi_W2'], 'L0_cond_noi_b2': _L0_cond_in['noi_b2'], 'L0_cond_noi_g': _L0_cond_in['noi_g'], 'L0_cond_noi_be': _L0_cond_in['noi_be'], 'L0_cond_res_W1': _L0_cond_in['res_W1'], 'L0_cond_res_b1': _L0_cond_in['res_b1'], 'L0_cond_res_W2': _L0_cond_in['res_W2'], 'L0_cond_res_b2': _L0_cond_in['res_b2'], 'L0_cond_res_g': _L0_cond_in['res_g'], 'L0_cond_res_be': _L0_cond_in['res_be'], 'L0_cond_int_W1': _L0_cond_in['int_W1'], 'L0_cond_int_b1': _L0_cond_in['int_b1'], 'L0_cond_int_W2': _L0_cond_in['int_W2'], 'L0_cond_int_b2': _L0_cond_in['int_b2'], 'L0_cond_int_g': _L0_cond_in['int_g'], 'L0_cond_int_be': _L0_cond_in['int_be'], 'L0_cond_aw': _L0_cond_in['aw'], 'L0_attn_W_qkv': _L0_attn_in['W_qkv'], 'L0_attn_b_qkv': _L0_attn_in['b_qkv'], 'L0_attn_W_proj': _L0_attn_in['W_proj'], 'L0_attn_b_proj': _L0_attn_in['b_proj'], 'L0_cond2_k_aff_w': _L0_cond2_in['k_aff_w'], 'L0_cond2_k_aff_b': _L0_cond2_in['k_aff_b'], 'L0_cond2_k_w': _L0_cond2_in['k_w'], 'L0_cond2_k_b': _L0_cond2_in['k_b'], 'L0_cond2_o_aff_w': _L0_cond2_in['o_aff_w'], 'L0_cond2_o_aff_b': _L0_cond2_in['o_aff_b'], 'L0_cond2_o_w': _L0_cond2_in['o_w'], 'L0_cond2_o_b': _L0_cond2_in['o_b'], 'L0_ffn_Wqkv': _L0_ffn_in['Wqkv'], 'L0_ffn_q_scale': _L0_ffn_in['q_scale'], 'L0_ffn_k_scale': _L0_ffn_in['k_scale'], 'L0_ffn_Wo': _L0_ffn_in['Wo'], 'L0_ffn_ln_g': _L0_ffn_in['ln_g'], 'L0_ffn_ln_b': _L0_ffn_in['ln_b'], 'L0_ffn_W1': _L0_ffn_in['W1'], 'L0_ffn_b1': _L0_ffn_in['b1'], 'L0_ffn_W2': _L0_ffn_in['W2'], 'L0_ffn_b2': _L0_ffn_in['b2']}

def reference(x, itok_BxS_0_999, itok_BxS_0_4, cond_512, cond_64, fside_Bx32_0, mask_BxS_ik0, L0_cond_pw_g, L0_cond_pw_b, L0_cond_cp_g, L0_cond_cp_b, L0_cond_tm_g, L0_cond_tm_b, L0_cond_ms_g, L0_cond_ms_b, L0_cond_mem_W1, L0_cond_mem_b1, L0_cond_mem_W2, L0_cond_mem_b2, L0_cond_mem_g, L0_cond_mem_be, L0_cond_noi_W1, L0_cond_noi_b1, L0_cond_noi_W2, L0_cond_noi_b2, L0_cond_noi_g, L0_cond_noi_be, L0_cond_res_W1, L0_cond_res_b1, L0_cond_res_W2, L0_cond_res_b2, L0_cond_res_g, L0_cond_res_be, L0_cond_int_W1, L0_cond_int_b1, L0_cond_int_W2, L0_cond_int_b2, L0_cond_int_g, L0_cond_int_be, L0_cond_aw, L0_attn_W_qkv, L0_attn_b_qkv, L0_attn_W_proj, L0_attn_b_proj, L0_cond2_k_aff_w, L0_cond2_k_aff_b, L0_cond2_k_w, L0_cond2_k_b, L0_cond2_o_aff_w, L0_cond2_o_aff_b, L0_cond2_o_w, L0_cond2_o_b, L0_ffn_Wqkv, L0_ffn_q_scale, L0_ffn_k_scale, L0_ffn_Wo, L0_ffn_ln_g, L0_ffn_ln_b, L0_ffn_W1, L0_ffn_b1, L0_ffn_W2, L0_ffn_b2):
    import jax
    import jax.numpy as jnp

    def _L0_cond_ref(x, pathway_ids, compartment_ids, time_steps, scale_type, memory_state, noise_state, resource_state, pw_g, pw_b, cp_g, cp_b, tm_g, tm_b, ms_g, ms_b, mem_W1, mem_b1, mem_W2, mem_b2, mem_g, mem_be, noi_W1, noi_b1, noi_W2, noi_b2, noi_g, noi_be, res_W1, res_b1, res_W2, res_b2, res_g, res_be, int_W1, int_b1, int_W2, int_b2, int_g, int_be, aw):
        import jax, jax.numpy as jnp
        import numpy as np
        EPS = 1e-05

        def _ln(x, g, b):
            m = jnp.mean(x, axis=-1, keepdims=True)
            v = jnp.mean((x - m) ** 2, axis=-1, keepdims=True)
            return (x - m) * jax.lax.rsqrt(v + EPS) * g + b

        def _mlp_ln(s, W1, b1, W2, b2, g, b):
            h = jax.nn.silu(s @ W1 + b1) @ W2 + b2
            return _ln(h, g, b)
        h = _ln(x, pw_g[pathway_ids], pw_b[pathway_ids])
        h = _ln(h, cp_g[compartment_ids], cp_b[compartment_ids])
        t = _ln(x, tm_g[time_steps], tm_b[time_steps])
        m = x + _mlp_ln(memory_state, mem_W1, mem_b1, mem_W2, mem_b2, mem_g, mem_be)[:, None, :]
        n = x + _mlp_ln(noise_state, noi_W1, noi_b1, noi_W2, noi_b2, noi_g, noi_be)[:, None, :]
        r = x + _mlp_ln(resource_state, res_W1, res_b1, res_W2, res_b2, res_g, res_be)[:, None, :]
        s = _ln(x, ms_g[scale_type], ms_b[scale_type])
        w = jax.nn.softmax(aw)
        cat = jnp.concatenate([w[0] * h, w[1] * t, w[2] * m, w[3] * n, w[4] * r, w[5] * s], axis=-1)
        return _mlp_ln(cat, int_W1, int_b1, int_W2, int_b2, int_g, int_be)

    def _L0_attn_ref(x, W_qkv, b_qkv, W_proj, b_proj):
        import jax, jax.numpy as jnp
        import numpy as np
        ALPHA = 1.0
        N_HEADS = 16
        B, N, D = x.shape
        H = N_HEADS
        hd = D // H
        qkv = (x @ W_qkv + b_qkv).reshape(B, N, 3, H, hd).transpose(2, 0, 3, 1, 4)
        q, k, v = (qkv[0], qkv[1], qkv[2])
        q_row_2 = jnp.max(jnp.sum(jnp.abs(q), axis=-1), axis=-1) ** 2
        k_col_2 = jnp.max(jnp.sum(jnp.abs(k), axis=-2), axis=-1) ** 2
        fro_q = jnp.sqrt(jnp.sum(q * q, axis=(-2, -1)))
        inf_xt = jnp.max(jnp.sum(jnp.abs(x), axis=-2), axis=-1)
        denom = fro_q * inf_xt[:, None]
        qk = jnp.einsum('bhnd,bhmd->bhnm', q, k)
        sim = -ALPHA * (q_row_2[:, :, None, None] - 2.0 * qk + k_col_2[:, :, None, None]) / denom[:, :, None, None]
        attn = jax.nn.softmax(sim, axis=-1)
        weighted = jnp.einsum('bhnm,bhmd->bhnd', attn, v)
        weighted = weighted.transpose(0, 2, 1, 3).reshape(B, N, D)
        return weighted @ W_proj + b_proj

    def _L0_cond2_ref(x, s, k_aff_w, k_aff_b, k_w, k_b, o_aff_w, o_aff_b, o_w, o_b):
        import jax, jax.numpy as jnp
        import numpy as np
        import math
        HEAD_NUM = 16
        EPS = 1e-08

        def modulated_linear(x, s, aff_w, aff_b, w, b):
            style = s @ aff_w.T + aff_b
            w_mod = w[None, :, :] * style[:, None, :]
            demod = jax.lax.rsqrt(jnp.sum(w_mod * w_mod, axis=2) + EPS)
            w_mod = w_mod * demod[:, :, None]
            return jnp.einsum('bni,boi->bno', x, w_mod) + b
        B, N, F = x.shape
        H = HEAD_NUM
        D = F // H
        kx = modulated_linear(x, s, k_aff_w, k_aff_b, k_w, k_b)
        kx = kx.reshape(B, N, H, D)
        q = k = v = kx
        scores = jnp.einsum('bnhd,bnjd->bnhj', q, k) / math.sqrt(D)
        A = jax.nn.softmax(scores, axis=-1)
        out = jnp.einsum('bnhj,bnjd->bnhd', A, v).reshape(B, N, F)
        out = modulated_linear(out, s, o_aff_w, o_aff_b, o_w, o_b)
        return out

    def _L0_ffn_ref(x, Wqkv, q_scale, k_scale, Wo, ln_g, ln_b, W1, b1, W2, b2):
        import jax, jax.numpy as jnp
        import numpy as np
        DIM = 256
        DEPTH = 6
        HEADS = 16
        DIM_HEAD = 64
        WINDOW = 64
        INNER = HEADS * DIM_HEAD
        DIM_INNER = int(DIM * 4 * 2 / 3)
        QK_SCALE = 8.0

        def shift_tokens(t):
            a, s = jnp.split(t, 2, -1)
            s = jnp.pad(s, ((0, 0), (1, 0), (0, 0)))[:, :-1]
            return jnp.concatenate([a, s], -1)

        def l2norm(t):
            return t / jnp.maximum(jnp.linalg.norm(t, axis=-1, keepdims=True), 1e-12)

        def rotate_half(x):
            x1, x2 = jnp.split(x, 2, -1)
            return jnp.concatenate([-x2, x1], -1)

        def rotary_tables(n):
            half = jnp.arange(0, DIM_HEAD, 2, dtype=jnp.float32)
            inv_freq = 1.0 / 10000.0 ** (half / DIM_HEAD)
            t = jnp.arange(n, dtype=jnp.float32)
            freqs = t[:, None] * inv_freq[None, :]
            freqs = jnp.concatenate([freqs, freqs], -1)
            base_scale = (half + 0.4 * DIM_HEAD) / (1.4 * DIM_HEAD)
            power = (t - n // 2) / (WINDOW // 2)
            scale = base_scale[None, :] ** power[:, None]
            scale = jnp.concatenate([scale, scale], -1)
            return (freqs, scale)

        def local_attention(q, k, v):
            b, h, n, d = q.shape
            w = WINDOW
            nw = n // w
            bq = q.reshape(b, h, nw, w, d)
            bk = k.reshape(b, h, nw, w, d)
            bv = v.reshape(b, h, nw, w, d)

            def look(t):
                p = jnp.pad(t, ((0, 0), (0, 0), (1, 0), (0, 0), (0, 0)))
                return jnp.concatenate([p[:, :, :nw], p[:, :, 1:]], axis=3)
            bk2, bv2 = (look(bk), look(bv))
            seq = jnp.arange(n).reshape(nw, w)
            seq_p = jnp.pad(seq, ((1, 0), (0, 0)), constant_values=-1)
            jt = jnp.concatenate([seq_p[:nw], seq_p[1:]], axis=1)
            it = seq[:, :, None]
            jb = jt[:, None, :]
            mask = (it < jb) | (it > jb + w) | (jb == -1)
            sim = jnp.einsum('bhwie,bhwje->bhwij', bq, bk2) * QK_SCALE
            sim = jnp.where(mask, -jnp.finfo(sim.dtype).max, sim)
            attn = jax.nn.softmax(sim, -1)
            out = jnp.einsum('bhwij,bhwje->bhwie', attn, bv2)
            return out.reshape(b, h, n, d)

        def attn_layer(x, Wqkv, qs, ksc, Wo):
            b, n, _ = x.shape
            qkv = x @ Wqkv
            q, k, v = jnp.split(qkv, 3, -1)
            sh = lambda t: t.reshape(b, n, HEADS, DIM_HEAD).transpose(0, 2, 1, 3)
            q, k, v = (sh(q), sh(k), sh(v))
            q = l2norm(q) * qs
            k = l2norm(k) * ksc
            freqs, scale = rotary_tables(n)
            cos, sin = (jnp.cos(freqs), jnp.sin(freqs))
            q = q * cos * scale + rotate_half(q) * sin * scale
            inv = 1.0 / scale
            k = k * cos * inv + rotate_half(k) * sin * inv
            out = local_attention(q, k, v)
            out = out.transpose(0, 2, 1, 3).reshape(b, n, INNER)
            return out @ Wo

        def ffn_layer(x, g, bln, W1, b1, W2, b2):
            mu = x.mean(-1, keepdims=True)
            var = ((x - mu) ** 2).mean(-1, keepdims=True)
            xn = (x - mu) / jnp.sqrt(var + 1e-05) * g + bln
            hg = xn @ W1 + b1
            a, gate = jnp.split(hg, 2, -1)
            return a * jax.nn.gelu(gate, approximate=False) @ W2 + b2
        for i in range(DEPTH):
            x = attn_layer(shift_tokens(x), Wqkv[i], q_scale[i], k_scale[i], Wo[i]) + x
            x = ffn_layer(shift_tokens(x), ln_g[i], ln_b[i], W1[i], b1[i], W2[i], b2[i]) + x
        return x
    x = x + _L0_attn_ref(_L0_cond_ref(x, itok_BxS_0_999, itok_BxS_0_4, itok_BxS_0_4, mask_BxS_ik0, cond_512, cond_64, fside_Bx32_0, L0_cond_pw_g, L0_cond_pw_b, L0_cond_cp_g, L0_cond_cp_b, L0_cond_tm_g, L0_cond_tm_b, L0_cond_ms_g, L0_cond_ms_b, L0_cond_mem_W1, L0_cond_mem_b1, L0_cond_mem_W2, L0_cond_mem_b2, L0_cond_mem_g, L0_cond_mem_be, L0_cond_noi_W1, L0_cond_noi_b1, L0_cond_noi_W2, L0_cond_noi_b2, L0_cond_noi_g, L0_cond_noi_be, L0_cond_res_W1, L0_cond_res_b1, L0_cond_res_W2, L0_cond_res_b2, L0_cond_res_g, L0_cond_res_be, L0_cond_int_W1, L0_cond_int_b1, L0_cond_int_W2, L0_cond_int_b2, L0_cond_int_g, L0_cond_int_be, L0_cond_aw), L0_attn_W_qkv, L0_attn_b_qkv, L0_attn_W_proj, L0_attn_b_proj)
    x = x + _L0_ffn_ref(_L0_cond2_ref(x, cond_512, L0_cond2_k_aff_w, L0_cond2_k_aff_b, L0_cond2_k_w, L0_cond2_k_b, L0_cond2_o_aff_w, L0_cond2_o_aff_b, L0_cond2_o_w, L0_cond2_o_b), L0_ffn_Wqkv, L0_ffn_q_scale, L0_ffn_k_scale, L0_ffn_Wo, L0_ffn_ln_g, L0_ffn_ln_b, L0_ffn_W1, L0_ffn_b1, L0_ffn_W2, L0_ffn_b2)
    return x

_drawn_inputs = setup_inputs


def setup_inputs(seed=0):
    import zlib

    import numpy as np

    out = dict(_drawn_inputs(seed))
    spreads = {'L0_cond_mem_b1': (0.0, 0.8),
     'L0_cond_mem_b2': (0.0, 0.1),
     'L0_cond_mem_be': (0.0, 0.8),
     'L0_cond_noi_b1': (0.0, 0.8),
     'L0_cond_noi_b2': (0.0, 0.1),
     'L0_cond_noi_be': (0.0, 0.8),
     'L0_cond_res_b1': (0.0, 0.8),
     'L0_cond_res_b2': (0.0, 0.1),
     'L0_cond_res_be': (0.0, 0.8),
     'L0_cond_int_b1': (0.0, 0.1),
     'L0_cond_int_b2': (0.0, 0.1),
     'L0_cond_int_be': (0.0, 0.1),
     'L0_cond_aw': (0.1666666716337204, 0.6),
     'L0_attn_b_qkv': (0.0, 0.1),
     'L0_attn_b_proj': (0.0, 0.1),
     'L0_cond2_k_aff_b': (1.0, 0.2),
     'L0_cond2_k_b': (0.0, 0.1),
     'L0_cond2_o_aff_b': (1.0, 0.2),
     'L0_cond2_o_b': (0.0, 0.1),
     'L0_ffn_q_scale': (1.0, 0.6),
     'L0_ffn_k_scale': (1.0, 0.6),
     'L0_ffn_ln_g': (1.0, 0.6),
     'L0_ffn_ln_b': (0.0, 0.8),
     'L0_ffn_b1': (0.0, 0.467),
     'L0_ffn_b2': (0.0, 0.1)}
    factors = {'cond_64': 3.742,
     'fside_Bx32_0': 5.454,
     'L0_cond_pw_g': 8.0,
     'L0_cond_pw_b': 8.0,
     'L0_cond_cp_g': 8.0,
     'L0_cond_cp_b': 8.0,
     'L0_cond_tm_g': 8.0,
     'L0_cond_tm_b': 8.0,
     'L0_cond_ms_g': 8.0,
     'L0_cond_ms_b': 8.0,
     'L0_cond_mem_W1': 2.729,
     'L0_cond_mem_W2': 2.673,
     'L0_cond_mem_g': 8.0,
     'L0_cond_noi_W1': 3.683,
     'L0_cond_noi_W2': 2.848,
     'L0_cond_noi_g': 8.0,
     'L0_cond_res_W1': 5.563,
     'L0_cond_res_W2': 4.522,
     'L0_cond_res_g': 8.0,
     'L0_cond_int_g': 4.098}
    for name, (base, spread) in spreads.items():
        noise = np.random.default_rng([zlib.crc32(name.encode()), seed]).standard_normal(out[name].shape)
        drawn = base * np.exp(spread * noise) if base else spread * noise
        out[name] = jnp.asarray(drawn.astype(out[name].dtype))
    for name, factor in factors.items():
        out[name] = (out[name] * factor).astype(out[name].dtype)
    return out
```

```python
from contextlib import ExitStack

import numpy as np
import concourse.bass as bass
import concourse.mybir as mybir
from concourse.alu_op_type import AluOpType as ALU

F32 = mybir.dt.float32
BF16 = mybir.dt.bfloat16
I32 = mybir.dt.int32
ACT = mybir.ActivationFunctionType
AX = mybir.AxisListType

P = 128
B, N, D = 8, 256, 256
NU = N // P
KT = D // P
LANES = ("pe", "act", "dve", "pool", "sp")


class Stretch:

    def __init__(self, nc, ctx, name, counts, steps):
        self.name, self.steps, self.new = name, steps, {}
        self.old = counts.get(name, {})
        self.eng = dict(zip(LANES, (nc.tensor, nc.scalar, nc.vector, nc.gpsimd, nc.sync)))
        self.carrier = ctx.enter_context(nc.semaphore(f"{name}_carrier"))
        self.sem = {lane: ctx.enter_context(nc.semaphore(f"{name}_{lane}")) for lane in LANES}
        self.per = {lane: self.old.get(("per", lane), 1) for lane in LANES}
        self.base, self.count, self.seen = {}, {}, {}
        if steps:
            for lane in LANES:
                self.eng[lane].sem_inc(self.sem[lane], self.per[lane])

    def begin(self, step=0):
        self.step, self.base, self.seen = step, {}, {}
        self.count = {lane: 0 for lane in LANES}

    def mark(self, lane, instruction, *name):
        self.count[lane] += 1
        assert name not in self.new or self.new[name] == (lane, self.count[lane]), name
        self.new[name] = (lane, self.count[lane])
        instruction.then_inc(self.sem[lane], 1)
        return instruction

    def wait(self, lane, *name, back=0):
        maker, at = self.old.get(name, ("pe", 1))
        at -= back * self.per[maker]
        if self.old and self.seen.get((lane, maker), -10**9) >= at:
            return
        self.seen[lane, maker] = at
        if (lane, maker) not in self.base:
            self.base[lane, maker] = (self.eng[lane].snap((self.step + 1) * self.per[maker])
                                      if self.steps else 0)
        self.eng[lane].wait_ge(self.sem[maker], self.base[lane, maker] + at)

    def carry(self, lane):
        self.eng[lane].sem_inc(self.carrier, 1)

    def wait_unit(self, lane, name, unit, units):
        if unit < 0:
            if self.steps:
                self.wait(lane, name, unit + units, back=1)
        else:
            self.wait(lane, name, unit)

    def end(self):
        for lane in LANES:
            self.new["per", lane] = max(self.count[lane], 1)
        Stretch.made[self.name] = self.new


NH, HD = 16, 16
NTILE = 4
SLOT = 32
INT_IN = 6
FQ = NTILE * P


def conditioned_blocks(nc, ctx, counts, io, ident, eps_ln, state, resid):
    def sb(name, shape, dt=F32):
        return ctx.enter_context(nc.sbuf_tensor(name, shape, dt))

    banks = [ctx.enter_context(nc.psum_tensor(f"bank{k}", [P, 512], F32)) for k in range(8)]

    ids = sb("ids", [P, 3, NU * B], I32)
    w_int1 = sb("w_int1", [P, 2 * INT_IN, D])
    w_mix = sb("w_mix", [P, 8, D])
    w_int2 = sb("w_int2", [P, KT, D])
    w_qk = sb("w_qk", [P, KT, 2 * FQ])
    w_v = sb("w_v", [P, KT, D])
    w_proj = sb("w_proj", [P, KT, D])
    k_w, o_w = sb("k_w", [P, KT, D]), sb("o_w", [P, KT, D])
    rows = sb("rows", [P, 5, D])
    fcols = sb("fcols", [P, 16 + 2 * NTILE])
    aw = sb("aw", [P, INT_IN])
    s_t = [sb(f"s_t{m}", [w, B]) for m, w in enumerate((128, 64, 32))]
    m_w1 = [sb(f"m_w1{m}", [w, D]) for m, w in enumerate((128, 64, 32))]
    m_w2 = [sb(f"m_w2{m}", [P, KT, D]) for m in range(3)]
    m_rows = sb("m_rows", [B, 3, 3, D])
    aff = [sb(f"aff{m}", [P, D]) for m in range(2)]
    ones = sb("ones", [P, P])
    slots = sb("slots", [P, P // SLOT])
    nhalf = sb("nhalf", [P, NH])
    mix = sb("mix", [P, INT_IN])
    amax, esum, erec = sb("amax", [P, 1]), sb("esum", [P, 1]), sb("erec", [P, 1])
    m_hid = sb("m_hid", [P, KT, B])
    m_out, m_norm = sb("m_out", [B, D]), sb("m_norm", [B, D])
    m_stat, m_mv, m_sd, m_rs = sb("m_stat", [B, 6]), sb("m_mv", [B, 2]), sb("m_sd", [B, 1]), sb("m_rs", [B, 1])
    m_t = sb("m_t", [P, 3, KT, B])
    int_bias = sb("int_bias", [P, KT, B])
    style = sb("style", [P, 4, B])
    k_sq, o_sq = sb("k_sq", [P, KT, D]), sb("o_sq", [P, KT, D])
    eps_mod = sb("eps_mod", [P, 1])

    dma = ctx.enter_context(nc.semaphore("dma_front"))
    pre = Stretch(nc, ctx, "front_setup", counts, 0)
    body = Stretch(nc, ctx, "front", counts, B)

    pre.begin()
    n = 0
    flat = {2: None, 3: "p a b -> p (a b)", 4: "p a b c -> p (a b c)"}
    for dst, src in (
        [(ids, "ids"), (w_int1, "w_int1"), (w_int2, "w_int2"), (w_qk, "w_qk"), (w_v, "w_v"),
         (w_proj, "w_proj"), (k_w, "k_w"), (o_w, "o_w"), (fcols, "fcols")]
        + [(s_t[m], f"s_t{m}") for m in range(3)] + [(m_w1[m], f"m_w1{m}") for m in range(3)]
        + [(m_w2[m], f"m_w2{m}") for m in range(3)] + [(aff[m], f"aff{m}") for m in range(2)]
    ):
        d = dst[:, :] if len(dst.shape) == 2 else dst.ap().rearrange(flat[len(dst.shape)])
        nc.sync.dma_start(d, io[src]).then_inc(dma, 16)
        n += 16
    for dst, src, w in ((rows, "rows", P), (aw, "aw", P), (m_rows, "m_rows", B)):
        d = dst[:, :] if len(dst.shape) == 2 else dst.ap().rearrange(flat[len(dst.shape)])
        nc.scalar.dma_start(d, io[src].broadcast_to([w, io[src].shape[1]])).then_inc(dma, 16)
        n += 16
    pre.mark("pool", nc.gpsimd.memset(ones[:, :], 1.0), "ones")
    pre.mark("pool", nc.gpsimd.memset(nhalf[:, :], -0.5), "nhalf")
    pre.mark("pool", nc.gpsimd.memset(eps_mod[:, :], 1e-8), "eps_mod")
    pre.mark("dve", nc.vector.memset(slots[:, :], 0.0), "slots0")
    pre.wait("dve", "slots0")
    for g in range(P // SLOT):
        m = nc.vector.memset(slots[g * SLOT:(g + 1) * SLOT, g:g + 1], 1.0)
    pre.mark("dve", m, "slots")
    for lane in ("pe", "act", "dve", "pool"):
        pre.eng[lane].wait_ge(dma, n)
    pre.mark("dve", nc.vector.tensor_reduce(amax[:, :], aw[:, :], AX.X, ALU.max, negate=True), "amax")
    pre.wait("act", "amax")
    pre.mark("act", nc.scalar.activation(mix[:, :], aw[:, :], ACT.Exp, bias=amax[:, :], accum_out=esum[:, :]),
             "mix_exp")
    pre.wait("dve", "mix_exp")
    pre.mark("dve", nc.vector.reciprocal(erec[:, :], esum[:, :]), "erec")
    pre.wait("dve", "erec")
    pre.mark("dve", nc.vector.tensor_scalar(mix[:, :], mix[:, :], erec[:, 0:1], None, ALU.mult), "mix")
    pre.wait("dve", "mix")
    for dst, blk in ((0, 0), (2, 1), (6, 5)):
        nc.vector.tensor_scalar(w_mix[:, dst:dst + 2, :], w_int1[:, 2 * blk:2 * blk + 2, :],
                                mix[:, blk:blk + 1], None, ALU.mult)
    pre.mark("dve", nc.vector.tensor_scalar(w_mix[:, 4:6, :], w_int1[:, 4:6, :], mix[:, 2:3], None, ALU.mult),
             "w_mix", 2)
    for blk in (3, 4):
        pre.wait("dve", "w_mix", blk - 1)
        for kt in range(KT):
            m = nc.vector.scalar_tensor_tensor(out=w_mix[:, 4 + kt, :], in0=w_int1[:, 2 * blk + kt, :],
                                               scalar=mix[:, blk:blk + 1], in1=w_mix[:, 4 + kt, :],
                                               op0=ALU.mult, op1=ALU.add)
        pre.mark("dve", m, "w_mix", blk)
    for m3 in range(3):
        if m3:
            pre.wait("pe", "m_hid", m3 - 1)
        for mt in range(KT):
            m = nc.tensor.matmul(banks[0][:, mt * B:(mt + 1) * B], m_w1[m3][:, mt * P:(mt + 1) * P],
                                 s_t[m3][:, :], start=True, stop=True)
        pre.mark("pe", m, "m_h", m3)
        pre.wait("act", "m_h", m3)
        if m3:
            pre.wait("act", "m_o", m3 - 1)
        for mt in range(KT):
            m = nc.scalar.activation(m_hid[:, mt, :], banks[0][:, mt * B:(mt + 1) * B], ACT.Silu,
                                     bias=fcols[:, 2 * m3 + mt:2 * m3 + mt + 1])
        pre.mark("act", m, "m_hid", m3)
        pre.wait("pe", "m_hid", m3)
        if m3:
            pre.wait("pe", "m_out", m3 - 1)
        for kt in range(KT):
            m = nc.tensor.matmul(banks[1][0:B, 0:D], m_hid[:, kt, :], m_w2[m3][:, kt, :],
                                 start=kt == 0, stop=kt == KT - 1)
        pre.mark("pe", m, "m_o", m3)
        pre.wait("dve", "m_o", m3)
        pre.mark("dve", nc.vector.tensor_tensor(m_out[:, :], banks[1][0:B, 0:D], m_rows[:, m3, 0, :], ALU.add),
                 "m_out", m3)
        pre.wait("dve", "m_out", m3)
        pre.mark("dve", nc.vector.bn_stats(m_stat[:, :], m_out[:, :]), "m_stat", m3)
        pre.wait("dve", "m_stat", m3)
        pre.mark("dve", nc.vector.bn_aggr(m_mv[:, :], m_stat[:, :]), "m_mv", m3)
        pre.wait("act", "m_mv", m3)
        pre.mark("act", nc.scalar.activation(m_sd[:, :], m_mv[:, 1:2], ACT.Sqrt, bias=eps_ln[0:B, :]), "m_sd", m3)
        pre.wait("dve", "m_sd", m3)
        pre.mark("dve", nc.vector.reciprocal(m_rs[:, :], m_sd[:, :]), "m_rs", m3)
        pre.wait("dve", "m_rs", m3)
        pre.mark("dve", nc.vector.tensor_scalar(m_norm[:, :], m_out[:, :], m_mv[:, 0:1], m_rs[:, 0:1],
                                                ALU.subtract, ALU.mult), "m_n0", m3)
        pre.wait("dve", "m_n0", m3)
        pre.mark("dve", nc.vector.tensor_tensor(m_norm[:, :], m_norm[:, :], m_rows[:, m3, 1, :], ALU.mult),
                 "m_n1", m3)
        pre.wait("dve", "m_n1", m3)
        pre.mark("dve", nc.vector.tensor_tensor(m_norm[:, :], m_norm[:, :], m_rows[:, m3, 2, :], ALU.add),
                 "m_n2", m3)
        pre.wait("pe", "m_n2", m3)
        if m3:
            pre.wait("pe", "m_t", m3 - 1)
        for kt in range(KT):
            m = nc.tensor.transpose(banks[2][:, kt * B:(kt + 1) * B], m_norm[:, kt * P:(kt + 1) * P],
                                    ident[0:B, 0:B])
        pre.mark("pe", m, "m_tp", m3)
        pre.wait("dve", "m_tp", m3)
        pre.mark("dve", nc.vector.tensor_scalar(m_t[:, m3, :, :].rearrange("p a b -> p (a b)"),
                                                banks[2][:, 0:KT * B], mix[:, 2 + m3:3 + m3], None, ALU.mult),
                 "m_t", m3)
    pre.wait("pe", "m_t", 2)
    for mt in range(KT):
        for m3 in range(3):
            for kt in range(KT):
                m = nc.tensor.matmul(banks[3][:, mt * B:(mt + 1) * B],
                                     w_int1[:, 4 + 2 * m3 + kt, mt * P:(mt + 1) * P], m_t[:, m3, kt, :],
                                     start=m3 + kt == 0, stop=m3 == 2 and kt == KT - 1)
    pre.mark("pe", m, "int_bias_ps")
    pre.wait("dve", "int_bias_ps")
    for mt in range(KT):
        m = nc.vector.tensor_scalar(int_bias[:, mt, :], banks[3][:, mt * B:(mt + 1) * B],
                                    fcols[:, 6 + mt:7 + mt], None, ALU.add)
    pre.mark("dve", m, "int_bias")
    for m2 in range(2):
        for mt in range(KT):
            c = 2 * m2 + mt
            m = nc.tensor.matmul(banks[4][:, c * B:(c + 1) * B], aff[m2][:, mt * P:(mt + 1) * P], s_t[0][:, :],
                                 start=True, stop=True)
    pre.mark("pe", m, "style_ps")
    pre.wait("dve", "style_ps")
    for c in range(4):
        m = nc.vector.tensor_scalar(style[:, c, :], banks[4][:, c * B:(c + 1) * B], fcols[:, 8 + c:9 + c], None,
                                    ALU.add)
    pre.mark("dve", m, "style")
    nc.scalar.activation(k_sq.ap(), k_w.ap(), ACT.Square)
    pre.mark("act", nc.scalar.activation(o_sq.ap(), o_w.ap(), ACT.Square), "w_sq")
    pre.end()
    nc.all_engine_barrier()

    x_tok = sb("x_tok", [P, NU, D])
    idc = sb("idc", [P, 3, NU], I32)
    pw = sb("pw", [P, NU, 2 * D])
    ct = sb("ct", [P, NU, 4 * D])
    ms = sb("ms", [P, NU, 2 * D])
    stat, mv = sb("stat", [P, NU, 6]), sb("mv", [P, NU, 2])
    rs = sb("rs", [P, NU])
    xh, hh, tt, ss = (sb(q, [P, NU, D]) for q in ("xh", "hh", "tt", "ss"))
    cat = sb("cat", [P, 8, N])
    ibc = sb("ibc", [P, KT])
    hid = sb("hid_t", [P, KT, N])
    y, y_t = sb("y", [P, NU, D]), sb("y_t", [P, KT, N])
    q_t, k_t = sb("q_t", [P, NTILE, N]), sb("k_t", [P, NTILE, N])
    v = sb("v_rows", [P, NU, D])
    junk = sb("junk", [P, N])
    qsq, kab, yab = sb("qsq", [P, NTILE]), sb("kab", [P, NTILE]), sb("yab", [P, KT])
    ymax, yinf, yrec = sb("ymax", [P, 1]), sb("yinf", [P, 1]), sb("yrec", [P, 1])
    qmask, fro = sb("qmask", [P, NH]), sb("fro", [P, NH])
    scl = sb("scl", [P, NH])
    rmax, rbias = sb("rmax", [P, 2, 2]), sb("rbias", [P, 2, 2])
    pr, pr_t = sb("pr", [P, 2, 2, N]), sb("pr_t", [P, 2, 2, NU, P])
    psm, pri = sb("psm", [P, NU, NH]), sb("pri", [P, NU, NH])
    o, o_t = sb("o", [P, NU, D]), sb("o_t", [P, KT, N])
    x_t = sb("x_t", [P, KT, N])
    x1 = sb("x1_t", [P, KT, N])
    stc, stc2 = sb("stc", [P, 4]), sb("stc2", [P, 4])
    stw = sb("stw", [P, 4, P])
    dem, demr = sb("dem", [P, 2, D]), sb("demr", [P, 2, D])
    w_m = sb("w_m", [P, 2, KT, D])
    kx = sb("kx", [P, NU, D])
    prod = sb("prod", [P, NH, NH, HD])
    sc, scm, scs, scr = sb("sc", [P, NH, NH]), sb("scm", [P, NH]), sb("scs", [P, NH]), sb("scr", [P, NH])
    o2, o2_t = sb("o2", [P, NU, D]), sb("o2_t", [P, KT, N])
    dma_x = ctx.enter_context(nc.semaphore("dma_x"))
    dma_g = [ctx.enter_context(nc.semaphore(f"dma_g{k}")) for k in range(3)]

    def W(lane, *name, **kw):
        body.wait(lane, *name, **kw)

    def M(lane, m, *name):
        body.mark(lane, m, *name)

    def dve(m, *name):
        M("dve", m, *name)
        W("dve", *name)

    T = lambda a: slice(a * P, (a + 1) * P)
    two = lambda bank: bank[:, :].rearrange("p (a n) -> p a n", a=2)
    V, A, G, E = nc.vector, nc.scalar, nc.gpsimd, nc.tensor
    VT, TS = V.tensor_tensor, V.tensor_scalar

    def flip(src, bank, name, need, free):
        for w in need + free:
            W("pe", *w[:-1], back=w[-1])
        for kt in range(KT):
            for u in range(NU):
                m = E.transpose(bank[:, kt * N + u * P:][:, 0:P], src[:, u, T(kt)], ident[:, :])
        M("pe", m, name)

    def norm_stats(src, name):
        for u in range(NU):
            m = V.bn_stats(stat[:, u, :], src[:, u, :])
        dve(m, name, "stat")
        body.carry("dve")
        for u in range(NU):
            m = V.bn_aggr(mv[:, u, :], stat[:, u, :])
        dve(m, name, "mv")
        dve(TS(mv[:, :, 1], mv[:, :, 1], 1e-5, None, ALU.add), name, "var")
        W("pool", name, "var")
        M("pool", G.tensor_tensor(rs[:, :], mv[:, :, 1], nhalf[:, 0:NU], ALU.pow), name, "rs")
        W("dve", name, "rs")

    def normalise(dst, src, name):
        for u in range(NU):
            m = TS(dst[:, u, :], src[:, u, :], mv[:, u, 0:1], rs[:, u:u + 1], ALU.subtract, ALU.mult)
        M("dve", m, name, "norm")

    with nc.Fori(0, B) as b:
        body.begin(b)
        W("sp", "xflip", back=1)
        W("sp", "xstat", "norm", back=1)
        nc.sync.dma_start(x_tok.ap(), io["x"][bass.ds(b, 1), :, :].rearrange("o (u p) d -> p (o u) d", p=P)
                          ).then_inc(dma_x, 16)
        W("pool", "s_add", back=1)
        W("pool", "h_add", back=1)
        M("pool", G.tensor_copy(idc.ap(), ids[:, :, bass.ds(b * NU, NU)]), "idc")
        W("pool", "idc")
        body.carry("pool")
        for k, (dst, tab) in enumerate(((pw, "t_pw"), (ct, "t_ct"), (ms, "t_ms"))):
            for u in range(NU):
                G.indirect_dma_start(dst[:, u, :], None, io[tab],
                                     bass.IndirectOffsetOnAxis(ap=idc[:, k, u:u + 1], axis=0)
                                     ).then_inc(dma_g[k], 16)
        V.wait_ge(dma_x, (b + 1) * 16)
        W("dve", "xflip", back=1)
        norm_stats(x_tok, "xstat")
        W("dve", "s_mul", back=1)
        normalise(xh, x_tok, "xstat")
        W("dve", "xstat", "norm")
        V.wait_ge(dma_g[0], (b + 1) * (16 * NU))
        W("dve", "hflip", back=1)
        dve(VT(hh.ap(), xh.ap(), pw[:, :, 0:D], ALU.mult), "h_mul0")
        dve(VT(hh.ap(), hh.ap(), pw[:, :, D:2 * D], ALU.add), "h_add0")
        G.wait_ge(dma_g[1], (b + 1) * (16 * NU))
        W("pool", "xstat", "norm")
        W("pool", "tflip", back=1)
        M("pool", G.tensor_tensor(tt.ap(), xh.ap(), ct[:, :, 2 * D:3 * D], ALU.mult), "t_mul")
        W("pool", "t_mul")
        M("pool", G.tensor_tensor(tt.ap(), tt.ap(), ct[:, :, 3 * D:4 * D], ALU.add), "t_add")
        G.wait_ge(dma_g[2], (b + 1) * (16 * NU))
        W("pool", "sflip", back=1)
        M("pool", G.tensor_tensor(ss.ap(), xh.ap(), ms[:, :, 0:D], ALU.mult), "s_mul")
        W("pool", "s_mul")
        M("pool", G.tensor_tensor(ss.ap(), ss.ap(), ms[:, :, D:2 * D], ALU.add), "s_add")
        norm_stats(hh, "hstat")
        normalise(hh, hh, "hstat")
        W("dve", "hstat", "norm")
        V.wait_ge(dma_g[1], (b + 1) * (16 * NU))
        dve(VT(hh.ap(), hh.ap(), ct[:, :, 0:D], ALU.mult), "h_mul")
        M("dve", VT(hh.ap(), hh.ap(), ct[:, :, D:2 * D], ALU.add), "h_add")
        E.wait_ge(dma_x, (b + 1) * 16)
        flip(x_tok, banks[0], "xflip", [], [("o_t", 1)])
        W("act", "xflip")
        W("act", "resid", back=1)
        W("act", "hid_ps", back=1)
        M("act", A.activation(x_t.ap(), two(banks[0]), ACT.Copy), "x_t")
        M("act", A.activation(cat[:, 4:6, :], two(banks[0]), ACT.Copy), "cat_x")
        for n, (src, ready) in enumerate(((tt, "t_add"), (ss, "s_add"), (hh, "h_add"))):
            name, c = ("tflip", "sflip", "hflip")[n], (2, 6, 0)[n]
            flip(src, banks[1 + n], name, [(ready, 0)], [(("x1", "dem", "kx")[n], 1)])
            W("act", name)
            M("act", A.activation(cat[:, c:c + 2, :], two(banks[1 + n]), ACT.Copy), "cat", n)
        W("act", "hid", back=1)
        M("act", A.activation(ibc[:, :], int_bias[:, :, bass.ds(b, 1)].rearrange("p a o -> p (a o)"), ACT.Copy),
          "ibc")
        W("act", "ibc")
        W("pe", "cat", 2)
        W("pe", "cat_x")
        W("pe", "o2_t", back=1)
        for mt in range(KT):
            for c in range(8):
                m = E.matmul(banks[4][:, mt * N:(mt + 1) * N], w_mix[:, c, T(mt)], cat[:, c, :],
                             start=c == 0, stop=c == 7)
        M("pe", m, "hid_ps")
        W("act", "hid_ps")
        W("act", "y_ps", back=1)
        for mt in range(KT):
            m = A.activation(hid[:, mt, :], banks[4][:, mt * N:(mt + 1) * N], ACT.Silu, bias=ibc[:, mt:mt + 1])
        M("act", m, "hid")
        W("pe", "hid")
        W("pe", "y_b", back=1)
        for u in range(NU):
            for kt in range(KT):
                m = E.matmul(banks[5][:, u * D:(u + 1) * D], hid[:, kt, T(u)], w_int2[:, kt, :],
                             start=kt == 0, stop=kt == KT - 1)
        M("pe", m, "y_ps")
        row = lambda r: rows[:, r, :].unsqueeze(1).broadcast_to([P, NU, D])
        W("dve", "y_ps")
        W("dve", "yflip", back=1)
        dve(VT(y.ap(), two(banks[5]), row(0), ALU.add), "y_b")
        norm_stats(y, "ystat")
        normalise(y, y, "ystat")
        W("dve", "ystat", "norm")
        dve(VT(y.ap(), y.ap(), row(1), ALU.mult), "y_g")
        M("dve", VT(y.ap(), y.ap(), row(2), ALU.add), "y")
        flip(y, banks[0], "yflip", [("y", 0)], [("cat_x", 0), ("x_t", 0)])
        W("act", "yflip")
        W("act", "v_ps", back=1)
        W("act", "junk", NTILE + KT - 1, back=1)
        M("act", A.activation(y_t.ap(), two(banks[0]), ACT.Copy), "y_t")
        W("pe", "y_t")
        for half, (dst, nm) in enumerate(((q_t, "q"), (k_t, "k"))):
            for c in range(2):
                bank = banks[1 + 2 * half + c] if half == 0 else banks[(3, 6)[c]]
                if half == 0:
                    W("pe", "cat", c)
                else:
                    W("pe", "cat", 2)
                    W("pe", "o", back=1)
                for t2 in range(2):
                    t = 2 * c + t2
                    for kt in range(KT):
                        m = E.matmul(bank[:, t2 * N:(t2 + 1) * N],
                                     w_qk[:, kt, half * FQ + t * P:][:, 0:P], y_t[:, kt, :],
                                     start=kt == 0, stop=kt == KT - 1)
                M("pe", m, nm + "_ps", c)
                W("act", nm + "_ps", c)
                W("act", "sc_ps", NH - 1, back=1)
                for t2 in range(2):
                    t = 2 * c + t2
                    m = A.activation(dst[:, t, :], bank[:, t2 * N:(t2 + 1) * N], ACT.Identity,
                                     bias=fcols[:, 16 + half * NTILE + t:][:, 0:1])
                M("act", m, nm, c)
        for u in range(NU):
            if u == 0:
                W("pe", "ostate", back=1)
            for kt in range(KT):
                m = E.matmul(banks[7][:, u * D:(u + 1) * D], y_t[:, kt, T(u)], w_v[:, kt, :],
                             start=kt == 0, stop=kt == KT - 1)
        M("pe", m, "v_ps")
        W("dve", "v_ps")
        W("dve", "av", NH - 1, back=1)
        M("dve", VT(v.ap(), two(banks[7]), row(3), ALU.add), "v")
        W("act", "q", 1)
        W("act", "qmask", back=1)
        W("act", "ymax", back=1)
        for t in range(NTILE):
            W("act", "junk", t - 1) if t else W("act", "junk", NTILE + KT - 1, back=1)
            M("act", A.activation(junk[:, :], q_t[:, t, :], ACT.Square, accum_out=qsq[:, t:t + 1]), "junk", t)
        for kt in range(KT):
            W("act", "junk", NTILE + kt - 1)
            M("act", A.activation(junk[:, :], y_t[:, kt, :], ACT.Abs, accum_out=yab[:, kt:kt + 1]),
              "junk", NTILE + kt)
        W("dve", "junk", NTILE + KT - 1)
        W("dve", "yinf", back=1)
        W("dve", "fro_ps", back=1)
        M("dve", V.tensor_reduce(ymax[:, :], yab[:, :], AX.X, ALU.max), "ymax")
        M("dve", VT(qmask[:, :].rearrange("p (t g) -> p t g", g=4), qsq[:, :].unsqueeze(2).broadcast_to([P, 4, 4]),
                    slots[:, :].unsqueeze(1).broadcast_to([P, 4, 4]), ALU.mult), "qmask")
        W("pool", "ymax")
        W("pool", "yrec", back=1)
        body.carry("pool")
        M("pool", G.partition_all_reduce(yinf[:, :], ymax[:, :], P, bass.bass_isa.ReduceOp.max), "yinf")
        W("pe", "qmask")
        W("pe", "v")
        M("pe", E.matmul(banks[7][:, 0:NH], ones[:, :], qmask[:, :], start=True, stop=True), "fro_ps")
        W("dve", "fro_ps")
        W("dve", "yinf")
        W("dve", "scl0", back=1)
        M("dve", V.tensor_copy(fro[:, :], banks[7][:, 0:NH]), "fro")
        dve(V.reciprocal(yrec[:, :], yinf[:, :]), "yrec")
        W("pool", "fro")
        W("pool", "exp", NH - 1, back=1)
        M("pool", G.tensor_tensor(scl[:, :], fro[:, :], nhalf[:, :], ALU.pow), "scl0")
        W("dve", "scl0")
        dve(TS(scl[:, :], scl[:, :], yrec[:, 0:1], 2.0, ALU.mult, ALU.mult), "scl")
        AU = NH
        SB = (banks[1], banks[2])
        PB = (banks[3], banks[4])
        OB = banks[6]

        def head(hp, e):
            return 4 * (2 * (hp // 4) + e) + hp % 4

        def scores(i):
            hp, u = divmod(i, NU)
            W("pe", "q", 1); W("pe", "k", 1)
            if i >= 2:
                W("pe", "exp", i - 2)
                W("pe", "rmax", i - 2)
            for e in range(2):
                h = head(hp, e)
                t, r = h // 4, slice(SLOT * (h % 4), SLOT * (h % 4) + SLOT)
                m = E.matmul(SB[i % 2][:, e * N:(e + 1) * N], q_t[r, t, T(u)], k_t[r, t, :], start=True, stop=True)
            M("pe", m, "sc_ps", i)

        def softmax(i):
            hp, u = divmod(i, NU)
            s = i % 2
            W("dve", "sc_ps", i)
            if i >= 2:
                W("dve", "exp", i - 2)
            elif i == 0:
                W("dve", "exp", NH - 1, back=1)
            M("dve", V.tensor_reduce(rmax[:, s, :], two(SB[s]), AX.X, ALU.max, negate=True), "rmax", i)
            W("dve", "rmax", i)
            W("dve", "scl")
            M("dve", VT(rbias[:, s, :], rmax[:, s, :], scl[:, head(hp, 0):head(hp, 1) + 1:4], ALU.mult), "rbias", i)
            W("act", "rbias", i)
            if i >= 2:
                W("act", "prt_ps", i - 2)
            else:
                W("act", "prt_ps", NH - 2 + i, back=1)
                W("act", "pri", back=1)
            for e in range(2):
                h = head(hp, e)
                m = A.activation(pr[:, s, e, :], SB[s][:, e * N:(e + 1) * N], ACT.Exp, bias=rbias[:, s, e:e + 1],
                                 scale=scl[:, h:h + 1], accum_out=psm[:, u, h:h + 1])
            M("act", m, "exp", i)

        def flip_p(i):
            s = i % 2
            W("pe", "exp", i)
            if i >= 2:
                W("pe", "prt", i - 2)
            else:
                W("pe", "k", 0); W("pe", "hid")
            for e in range(2):
                for c in range(NU):
                    m = E.transpose(PB[s][:, (2 * e + c) * P:][:, 0:P], pr[:, s, e, T(c)], ident[:, :])
            M("pe", m, "prt_ps", i)
            W("act", "prt_ps", i)
            if i >= 2:
                W("act", "av", i - 2)
            else:
                W("act", "av", NH - 2 + i, back=1)
            M("act", A.activation(pr_t[:, s, :, :, :].rearrange("p a b c -> p (a b c)"), PB[s][:, :], ACT.Copy),
              "prt", i)

        def weigh(i):
            hp, u = divmod(i, NU)
            s = i % 2
            W("pe", "prt", i)
            W("pe", "v")
            if i == 0:
                W("pe", "k", 1)
            for e in range(2):
                h = head(hp, e)
                for c in range(NU):
                    m = E.matmul(OB[:, u * D + h * HD:][:, 0:HD], pr_t[:, s, e, c, :], v[:, c, h * HD:(h + 1) * HD],
                                 start=c == 0, stop=c == NU - 1)
            M("pe", m, "av", i)

        stages = (scores, softmax, flip_p, weigh)
        for t in range(AU + 3):
            for s in reversed(range(4)):
                if 0 <= t - s < AU:
                    stages[s](t - s)
        W("dve", "exp", NH - 1)
        W("dve", "o", back=1)
        dve(V.reciprocal(pri.ap(), psm.ap()), "pri")
        W("dve", "av", NH - 1)
        W("dve", "oflip", back=1)
        M("dve", VT(o.ap().rearrange("p u (h d) -> p u h d", d=HD),
                    two(OB).rearrange("p u (h d) -> p u h d", d=HD),
                    pri.ap().unsqueeze(3).broadcast_to([P, NU, NH, HD]), ALU.mult), "o")
        flip(o, banks[0], "oflip", [("o", 0)], [("y_t", 0)])
        W("act", "oflip")
        W("act", "x1_ps", back=1)
        M("act", A.activation(o_t.ap(), two(banks[0]), ACT.Copy), "o_t")
        W("pe", "o_t")
        W("pe", "exp", NH - 1)
        for mt in range(KT):
            for kt in range(KT):
                m = E.matmul(SB[0][:, mt * N:(mt + 1) * N], w_proj[:, kt, T(mt)], o_t[:, kt, :],
                             start=kt == 0, stop=kt == KT - 1)
        M("pe", m, "x1_ps")
        W("dve", "x1_ps")
        W("dve", "x_t")
        W("dve", "kx_ps", back=1)
        W("dve", "resid", back=1)
        for mt in range(KT):
            m = V.scalar_tensor_tensor(out=x1[:, mt, :], in0=SB[0][:, mt * N:(mt + 1) * N],
                                       scalar=fcols[:, 12 + mt:13 + mt], in1=x_t[:, mt, :],
                                       op0=ALU.add, op1=ALU.add)
        M("dve", m, "x1")
        W("act", "x1")
        M("act", A.activation(resid[:, bass.ds(b, 1), :].rearrange("p o n -> p (o n)"),
                              x1.ap().rearrange("p a n -> p (a n)"), ACT.Copy), "resid")
        W("dve", "w_m", back=1)
        dve(V.tensor_copy(stc[:, :], style[:, :, bass.ds(b, 1)].rearrange("p a o -> p (a o)")), "stc")
        dve(VT(stc2[:, :], stc[:, :], stc[:, :], ALU.mult), "stc2")
        W("dve", "dem_ps", back=1)
        for c in range(4):
            m = TS(stw[:, c, :], ones[:, :], stc2[:, c:c + 1], None, ALU.mult)
        M("dve", m, "stw")
        W("pe", "stw")
        W("pe", "exp", NH - 1)
        for m2, w2 in enumerate((k_sq, o_sq)):
            for kt in range(KT):
                m = E.matmul(SB[1][:, m2 * D:(m2 + 1) * D], stw[:, 2 * m2 + kt, :], w2[:, kt, :],
                             start=kt == 0, stop=kt == KT - 1)
        M("pe", m, "dem_ps")
        W("act", "dem_ps")
        W("act", "demr", back=1)
        M("act", A.activation(dem.ap(), two(SB[1]), ACT.Sqrt, bias=eps_mod[:, :]), "dem")
        W("dve", "dem")
        dve(V.reciprocal(demr.ap(), dem.ap()), "demr")
        W("dve", "x2_ps", back=1)
        for m2, w in enumerate((k_w, o_w)):
            for kt in range(KT):
                m = V.scalar_tensor_tensor(out=w_m[:, m2, kt, :], in0=demr[:, m2, :],
                                           scalar=stc[:, 2 * m2 + kt:2 * m2 + kt + 1], in1=w[:, kt, :],
                                           op0=ALU.mult, op1=ALU.mult)
        M("dve", m, "w_m")
        W("pe", "w_m")
        W("pe", "x1")
        W("pe", "prt", NH - 2)
        for u in range(NU):
            for kt in range(KT):
                m = E.matmul(PB[0][:, u * D:(u + 1) * D], x1[:, kt, T(u)], w_m[:, 0, kt, :],
                             start=kt == 0, stop=kt == KT - 1)
        M("pe", m, "kx_ps")
        W("dve", "kx_ps")
        dve(VT(kx.ap(), two(PB[0]), row(4), ALU.add), "kx")
        W("dve", "o2flip", back=1)
        for u in range(NU):
            kh = kx[:, u, :].rearrange("p (h d) -> p h d", d=HD)
            dve(VT(prod.ap(), kh.unsqueeze(2).broadcast_to([P, NH, NH, HD]),
                   kh.unsqueeze(1).broadcast_to([P, NH, NH, HD]), ALU.mult), "hp", u)
            dve(V.tensor_reduce(sc.ap(), prod.ap(), AX.X, ALU.add), "hs", u)
            dve(V.tensor_reduce(scm[:, :], sc.ap(), AX.X, ALU.max), "hm", u)
            dve(VT(sc.ap(), sc.ap(), scm[:, :].unsqueeze(2).broadcast_to([P, NH, NH]), ALU.subtract), "hd", u)
            W("act", "hd", u)
            M("act", A.activation(sc.ap(), sc.ap(), ACT.Exp, scale=float(HD) ** -0.5), "he", u)
            W("dve", "he", u)
            dve(V.tensor_reduce(scs[:, :], sc.ap(), AX.X, ALU.add), "hsum", u)
            dve(V.reciprocal(scr[:, :], scs[:, :]), "hrec", u)
            dve(VT(sc.ap(), sc.ap(), scr[:, :].unsqueeze(2).broadcast_to([P, NH, NH]), ALU.mult), "hw", u)
            kd = kx[:, u, :].rearrange("p (j d) -> p d j", d=HD)
            dve(VT(prod.ap(), sc.ap().unsqueeze(2).broadcast_to([P, NH, HD, NH]),
                   kd.unsqueeze(1).broadcast_to([P, NH, HD, NH]), ALU.mult), "hq", u)
            dve(V.tensor_reduce(o2[:, u, :].rearrange("p (h d) -> p h d", d=HD), prod.ap(), AX.X, ALU.add),
                "ho", u)
        flip(o2, PB[1], "o2flip", [("ho", NU - 1, 0)], [("prt", NH - 1, 0)])
        W("act", "o2flip")
        W("act", "x2_ps", back=1)
        M("act", A.activation(o2_t.ap(), two(PB[1]), ACT.Copy), "o2_t")
        W("pe", "o2_t")
        W("pe", "o")
        for mt in range(KT):
            for kt in range(KT):
                m = E.matmul(banks[7][:, mt * N:(mt + 1) * N], w_m[:, 1, kt, T(mt)], o2_t[:, kt, :],
                             start=kt == 0, stop=kt == KT - 1)
        M("pe", m, "x2_ps")
        W("act", "x2_ps")
        for mt in range(KT):
            m = A.activation(state[:, bass.ds(b, 1), mt * PAD + 1:(mt + 1) * PAD].rearrange("p o n -> p (o n)"),
                             banks[7][:, mt * N:(mt + 1) * N], ACT.Identity, bias=fcols[:, 14 + mt:15 + mt])
        M("act", m, "ostate")
        body.end()
    nc.all_engine_barrier()


def write_out(nc, ctx, counts, out, ident, state, resid):
    def sb(name, shape, dt=F32):
        return ctx.enter_context(nc.sbuf_tensor(name, shape, dt))

    total = sb("total", [P, 2, KT, N])
    rows_out = sb("rows_out", [P, 2, NU, D])
    bank = [ctx.enter_context(nc.psum_tensor(f"out_bank{k}", [P, 512], F32)) for k in range(2)]
    dma_o = [ctx.enter_context(nc.semaphore(f"dma_o{k}")) for k in range(2)]
    last = Stretch(nc, ctx, "write_out", counts, 0)
    last.begin()
    for b in range(B):
        s = b % 2
        if b >= 2:
            last.wait("dve", "flip", b - 2)
        last.mark("dve", nc.vector.tensor_tensor(
            total[:, s, :, :], resid[:, b, :].rearrange("p (k n) -> p k n", k=KT),
            state[:, b, :].rearrange("p (k n) -> p k n", k=KT)[:, :, 1:PAD], ALU.add), "total", b)
        last.wait("pe", "total", b)
        if b >= 2:
            last.wait("pe", "rows", b - 2)
        for u in range(NU):
            for kt in range(KT):
                m = nc.tensor.transpose(bank[s][:, u * D + kt * P:][:, 0:P], total[:, s, kt, u * P:(u + 1) * P],
                                        ident[:, :])
        last.mark("pe", m, "flip", b)
        last.wait("act", "flip", b)
        if b >= 2:
            nc.scalar.wait_ge(dma_o[s], 16 * (b // 2))
        last.mark("act", nc.scalar.activation(rows_out[:, s, :, :].rearrange("p u d -> p (u d)"), bank[s][:, :],
                                              ACT.Copy), "rows", b)
        last.wait("sp", "rows", b)
        nc.sync.dma_start(out[b:b + 1, :, :].rearrange("o (u p) d -> p (o u) d", p=P), rows_out[:, s, :, :]
                          ).then_inc(dma_o[s], 16)
    for s in range(2):
        nc.sync.wait_ge(dma_o[s], 16 * (B // 2))
    last.end()
DEPTH, HEADS, DH, WIN = 6, 16, 64, 64
INNER = HEADS * DH
DI = int(D * 4 * 2 / 3)
NJ = -(-DI // P)
GH = 4
NG = HEADS // GH
UNITS = NG * NU
GC = GH * DH
PAD = N + 1
VR = 6
QK_SCALE = 8.0
NCOL = 2 * KT + 2 * NJ + KT


def local_layers(nc, ctx, counts, io, state, ident, eps_ln):
    def sb(name, shape, dt=F32):
        return ctx.enter_context(nc.sbuf_tensor(name, shape, dt))

    w_qkv = [sb(f"w_qkv{k}", [P, KT, NG, 3 * GC]) for k in range(2)]
    w_o = [sb(f"w_o{k}", [P, INNER // P, D]) for k in range(2)]
    w_1 = [sb(f"w_1{k}", [P, KT, 2 * DI]) for k in range(2)]
    w_2 = [sb(f"w_2{k}", [P, NJ, D]) for k in range(2)]
    cols = [sb(f"cols{k}", [P, NCOL]) for k in range(2)]
    qk_gain = [sb(f"qk_gain{k}", [P, 2, DH]) for k in range(2)]
    rot_cos, rot_sin = sb("rot_cos", [P, NU, 2, DH]), sb("rot_sin", [P, NU, 2, DH])
    cos_t, sin_t = sb("cos_t", [P, NU, 2, DH]), sb("sin_t", [P, NU, 2, DH])
    band = sb("band", [P, NU, P], BF16)
    ident_bf = sb("ident_bf", [P, P], BF16)
    mean_w = sb("mean_w", [P, P])
    half = sb("half", [P, 2 * GH])

    xa = sb("xa", [P, KT * PAD])
    sq = sb("sq", [P, 2, 2 * GC])
    norm2 = sb("norm2", [P, 2, 2 * GH])
    rnorm = sb("rnorm", [P, 2, 2 * GH])
    by_cos, by_sin = sb("by_cos", [P, 2, 2 * GC]), sb("by_sin", [P, 2, 2 * GC])
    turned = sb("turned", [P, 2, 2 * GC])
    qk_t = sb("qk_t", [P, 4, 4, P])
    v_tok = sb("v_tok", [P, VR, GC])
    v_shift = sb("v_shift", [P, NG, GC])
    negmax = sb("negmax", [P, 2, GH])
    escale, ebias = sb("escale", [P, 2, GH]), sb("ebias", [P, 2, GH])
    prob = sb("prob", [P, 2, GH, P])
    rsum, rinv = sb("rsum", [P, 2, GH]), sb("rinv", [P, 2, GH])
    prob_t = sb("prob_t", [P, 2, GH, P])
    attn_t = sb("attn_t", [P, INNER // P, N])
    x1 = sb("x1", [P, KT * PAD])
    cent, cent2 = sb("cent", [P, KT, N]), sb("cent2", [P, KT, N])
    sdev = sb("sdev", [P, N])
    lin_in = sb("lin_in", [P, KT, N])
    gate = sb("gate", [P, 2, N])
    hidden = sb("hidden", [P, NJ, N])

    def ps(name):
        return ctx.enter_context(nc.psum_tensor(name, [P, 512], F32))

    ps_qk = [ps("ps_qk0"), ps("ps_qk1")]
    ps_v = ps("ps_v")
    ps_t = ps("ps_t")
    ps_s = [ps("ps_s0"), ps("ps_s1")]
    ps_f = [ps("ps_f0"), ps("ps_f1")]
    ps_av, ps_pt = ps_f

    dma_w = [ctx.enter_context(nc.semaphore(f"dma_w{k}")) for k in range(2)]
    dma_c = ctx.enter_context(nc.semaphore("dma_c"))
    ready = Stretch(nc, ctx, "layer_setup", counts, 0)
    sec = Stretch(nc, ctx, "layer", counts, DEPTH)
    body = Stretch(nc, ctx, "layer_batch", counts, DEPTH * B)

    W_DMAS = 6

    def load_layer(k, layer):
        one = bass.ds(layer, 1)
        for dst, src in ((w_qkv[k], io["w_qkv"]), (w_o[k], io["w_o"]), (w_1[k], io["w_1"]),
                         (w_2[k], io["w_2"]), (cols[k], io["cols"])):
            shape = dst.shape
            flat = dst[:, :] if len(shape) == 2 else dst.ap().rearrange(
                "p a b -> p (a b)" if len(shape) == 3 else "p a b c -> p (a b c)")
            nc.sync.dma_start(flat, src[one, :, :].rearrange("l p n -> (l p) n")).then_inc(dma_w[k], 16)
        nc.sync.dma_start(qk_gain[k].ap().rearrange("p a b -> p (a b)"),
                          io["qk_gain"][one, :].broadcast_to([P, 2 * DH])).then_inc(dma_w[k], 16)

    ready.begin()
    for dst, src in ((rot_cos, io["rot_cos"]), (rot_sin, io["rot_sin"])):
        nc.sync.dma_start(dst.ap().rearrange("p a b c -> p (a b c)"), src).then_inc(dma_c, 16)
    nc.sync.dma_start(band.ap().rearrange("p a b -> p (a b)"), io["band"]).then_inc(dma_c, 16)
    nc.sync.wait_ge(dma_c, 48)
    load_layer(0, 0)
    load_layer(1, 1)
    ready.mark("pool", nc.gpsimd.memset(mean_w[:, :], 1.0 / D), "mean_w")
    ready.mark("pool", nc.gpsimd.memset(half[:, :], -0.5), "half")
    ready.mark("pool", nc.gpsimd.memset(x1[:, :], 0.0), "x1_zero")
    ready.mark("pool", nc.gpsimd.memset(xa[:, :], 0.0), "xa_zero")
    ready.mark("dve", nc.vector.tensor_copy(ident_bf[:, :], ident[:, :]), "ident_bf")
    ready.end()
    nc.all_engine_barrier()

    def U(u):
        return slice(u * P, (u + 1) * P)

    def heads(ap, n=2 * GH):
        return ap.rearrange("p (h t d) -> p h t d", t=2, d=DH // 2)

    def project(i, k):
        g, u = divmod(i, NU)
        body.wait_unit("pe", "qk_square", i - 2, UNITS)
        body.wait_unit("pe", "qk_by_sin", i - 2, UNITS)
        for kt in range(KT):
            lhs = xa[:, (1 if kt == 0 else PAD) + u * P:][:, 0:P]
            m = nc.tensor.matmul(ps_qk[i % 2][:, :], lhs, w_qkv[k][:, kt, g, 0:2 * GC],
                                 start=kt == 0, stop=kt == KT - 1)
        body.mark("pe", m, "qk", i)
        body.wait_unit("pe", "v_copied", i - 1, UNITS)
        for kt in range(KT):
            lhs = xa[:, (1 if kt == 0 else PAD) + u * P:][:, 0:P]
            m = nc.tensor.matmul(ps_v[:, 0:GC], lhs, w_qkv[k][:, kt, g, 2 * GC:3 * GC],
                                 start=kt == 0, stop=kt == KT - 1)
        body.mark("pe", m, "v", i)

    def rotate(i, k):
        g, u = divmod(i, NU)
        s = i % 2
        qk = ps_qk[s]
        body.wait("act", "qk", i)
        body.wait_unit("act", "norm2", i - 2, UNITS)
        body.mark("act", nc.scalar.activation(sq[:, s, :], qk[:, :], ACT.Square), "qk_square", i)
        body.wait("act", "v", i)
        body.wait_unit("act", "attn", i - VR, UNITS)
        m = nc.scalar.activation(v_tok[:, i % VR, :], ps_v[:, 0:GC], ACT.Copy)
        if u == 0:
            body.wait_unit("act", "attn", i + 1 - UNITS, UNITS)
            m = nc.scalar.activation(v_shift[WIN:P, g, :], ps_v[WIN:P, 0:GC], ACT.Copy)
        else:
            m = nc.scalar.activation(v_shift[0:WIN, g, :], ps_v[0:WIN, 0:GC], ACT.Copy)
        body.mark("act", m, "v_copied", i)

        body.wait("dve", "qk_square", i)
        body.wait_unit("dve", "turned", i - 2, UNITS)
        shape = [P, 2, GH, DH]
        cs = cos_t[:, u, :, :].unsqueeze(2).broadcast_to(shape)
        body.mark("dve", nc.vector.tensor_tensor(
            by_cos[:, s, :].rearrange("p (a h d) -> p a h d", a=2, h=GH),
            qk[:, :].rearrange("p (a h d) -> p a h d", a=2, h=GH), cs, ALU.mult), "qk_by_cos", i)
        for a in range(2):
            sn = sin_t[:, u, a, :].rearrange("p (t d) -> p t d", t=2).unsqueeze(1)
            cut = slice(a * GC, (a + 1) * GC)
            m = nc.vector.tensor_tensor(heads(by_sin[:, s, cut]), heads(qk[:, cut])[:, :, ::-1, :],
                                        sn.broadcast_to([P, GH, 2, DH // 2]), ALU.mult)
        body.mark("dve", m, "qk_by_sin", i)
        body.wait("dve", "qk_square", i)
        body.wait_unit("dve", "rnorm", i - 2, UNITS)
        body.mark("dve", nc.vector.tensor_reduce(norm2[:, s, :], sq[:, s, :].rearrange(
            "p (h d) -> p h d", d=DH), AX.X, ALU.add), "norm2", i)
        body.wait("dve", "norm2", i)
        body.mark("dve", nc.vector.tensor_scalar(norm2[:, s, :], norm2[:, s, :], 1e-24, None, ALU.max),
                  "norm2_floor", i)

        body.wait("pool", "norm2_floor", i)
        body.wait_unit("pool", "ebias", i - 2, UNITS)
        body.mark("pool", nc.gpsimd.tensor_tensor(rnorm[:, s, :], norm2[:, s, :], half[:, :], ALU.pow),
                  "rnorm", i)
        body.wait("pool", "qk_by_sin", i)
        body.wait_unit("pool", "turned_t", i - 2, UNITS)
        m = nc.gpsimd.tensor_tensor(turned[:, s, :], by_cos[:, s, :], by_sin[:, s, :], ALU.add)
        body.mark("pool", m, "turned", i)
        body.wait("pool", "turned", i)
        kk = turned[:, s, GC:].rearrange("p (h d) -> p h d", d=DH)
        m = nc.gpsimd.tensor_tensor(kk, kk, rnorm[:, s, GH:].unsqueeze(2).broadcast_to([P, GH, DH]), ALU.mult)
        body.mark("pool", m, "k_unit", i)

    def flip_qk(i):
        body.wait("pe", "k_unit", i)
        body.wait_unit("pe", "qk_t", i - 1, UNITS)
        for c in range(4):
            m = nc.tensor.transpose(ps_t[:, U(c)], turned[:, i % 2, U(c)], ident[:, :])
        body.mark("pe", m, "turned_t", i)
        body.wait("act", "turned_t", i)
        body.wait_unit("act", "scores", i - 3, UNITS)
        body.mark("act", nc.scalar.activation(qk_t[:, i % 4, :, :].rearrange("p a b -> p (a b)"),
                                              ps_t[:, :], ACT.Copy), "qk_t", i)

    def half_bank(odd, i):
        return ps_s[odd][:, 0:2 * P]

    def score(i):
        u, s = i % NU, i % 2
        body.wait("pe", "qk_t", i)
        body.wait_unit("pe", "prob", i - 1, UNITS)
        for odd in range(2):
            nc.tensor.matmul(half_bank(odd, i).rearrange("p (h k) -> p h k", h=2), ident_bf[:, :],
                             band[:, u, :].unsqueeze(1).broadcast_to([P, 2, P]), start=True, stop=False,
                             skip_group_check=True)
        for h in range(GH):
            r, c = slice(DH * (h % 2), DH * (h % 2) + DH), h // 2
            q, kk, before = qk_t[r, i % 4, c, :], qk_t[r, i % 4, 2 + c, :], qk_t[r, (i - 1) % 4, 2 + c, :]
            o = half_bank(h % 2, i)[:, U(h // 2)]
            m = nc.tensor.matmul(o[:, 0:WIN], q, kk[:, 0:WIN], start=False, stop=True, skip_group_check=True)
            m = nc.tensor.matmul(o[WIN:P, WIN:P], q[:, WIN:P], kk[:, WIN:P], start=False, stop=True,
                                 skip_group_check=True)
            if u:
                m = nc.tensor.matmul(o[0:WIN, WIN:P], q[:, 0:WIN], before[:, WIN:P], start=False, stop=True,
                                     skip_group_check=True)
        body.mark("pe", m, "scores", i)

    def soften(i):
        s = i % 2
        body.wait("dve", "scores", i)
        body.wait_unit("dve", "ebias", i - 2, UNITS)
        for odd in range(2):
            m = nc.vector.tensor_reduce(negmax[:, s, odd::2], half_bank(odd, i).rearrange(
                "p (h k) -> p h k", h=2), AX.X, ALU.max, negate=True)
        body.mark("dve", m, "negmax", i)
        body.wait("dve", "rnorm", i)
        body.wait_unit("dve", "prob", i - 2, UNITS)
        body.mark("dve", nc.vector.tensor_scalar(escale[:, s, :], rnorm[:, s, 0:GH], QK_SCALE, None, ALU.mult),
                  "escale", i)
        body.wait("dve", "escale", i)
        body.wait("dve", "negmax", i)
        body.mark("dve", nc.vector.tensor_tensor(ebias[:, s, :], negmax[:, s, :], escale[:, s, :], ALU.mult),
                  "ebias", i)
        body.wait("act", "ebias", i)
        body.wait_unit("act", "prob_t_ps", i - 2, UNITS)
        body.wait_unit("act", "rinv", i - 2, UNITS)
        for h in range(GH):
            m = nc.scalar.activation(prob[:, s, h, :], half_bank(h % 2, i)[:, U(h // 2)], ACT.Exp, bias=ebias[:, s, h:h + 1],
                                     scale=escale[:, s, h:h + 1], accum_out=rsum[:, s, h:h + 1])
        body.mark("act", m, "prob", i)
        body.wait("dve", "prob", i)
        body.wait_unit("dve", "prob_unit", i - 2, UNITS)
        body.mark("dve", nc.vector.reciprocal(rinv[:, s, :], rsum[:, s, :]), "rinv", i)
        body.wait("dve", "rinv", i)
        for h in range(GH):
            m = nc.vector.tensor_scalar(prob[:, s, h, :], prob[:, s, h, :], rinv[:, s, h:h + 1], None, ALU.mult)
        body.mark("dve", m, "prob_unit", i)

    def flip_prob(i):
        body.wait("pe", "prob_unit", i)
        body.wait_unit("pe", "prob_t", i - 1, UNITS)
        if i == 0:
            body.wait("pe", "state", back=1)
        for h in range(GH):
            m = nc.tensor.transpose(ps_pt[:, U(h)], prob[:, i % 2, h, :], ident[:, :])
        body.mark("pe", m, "prob_t_ps", i)
        body.wait("dve", "prob_t_ps", i)
        body.wait_unit("dve", "attn", i - 2, UNITS)
        body.mark("dve", nc.vector.tensor_copy(prob_t[:, i % 2, :, :].rearrange("p a b -> p (a b)"),
                                               ps_pt[:, :]), "prob_t", i)

    def attend(i):
        g, u = divmod(i, NU)
        body.wait("pe", "prob_t", i)
        body.wait("pe", "v_copied", i)
        body.wait_unit("pe", "attn_t", i - 1, UNITS)
        if i == 0:
            body.wait("pe", "state", back=1)
        for h in range(GH):
            out = ps_av[DH * (h % 2):DH * (h % 2) + DH, P * (h // 2):P * (h // 2) + P]
            vh = slice(h * DH, (h + 1) * DH)
            pt = prob_t[:, i % 2, h, :]
            if u == 0:
                m = nc.tensor.matmul(out, v_tok[:, i % VR, vh], pt, start=True, stop=True)
            else:
                m = nc.tensor.matmul(out[:, 0:WIN], v_shift[:, g, vh], pt[:, 0:WIN], start=True, stop=True)
                m = nc.tensor.matmul(out[:, WIN:P], v_tok[:, i % VR, vh], pt[:, WIN:P], start=True, stop=True)
        body.mark("pe", m, "attn", i)
        body.wait("act", "attn", i)
        if i == 0:
            body.wait("act", "w_o", back=1)
        body.mark("act", nc.scalar.activation(
            attn_t[:, 2 * g:2 * g + 2, U(u)], ps_av[:, 0:GC].rearrange("p (a b) -> p a b", a=2), ACT.Copy),
            "attn_t", i)

    def feed_forward(k, b):
        c = cols[k]
        gain, shift = c[:, 0:KT], c[:, KT:2 * KT]
        b_a, b_g = c[:, 2 * KT:2 * KT + NJ], c[:, 2 * KT + NJ:2 * KT + 2 * NJ]
        b_2 = c[:, 2 * KT + 2 * NJ:]
        whole = lambda t: t[:, :].rearrange("p (k n) -> p k n", k=KT)[:, :, 1:PAD]
        shifted = lambda t: t[:, 1:1 + KT * N].rearrange("p (k n) -> p k n", k=KT)
        body.wait("pe", "attn_t", UNITS - 1)
        body.wait("pe", "state", back=1)
        for mt in range(KT):
            for j in range(INNER // P):
                m = nc.tensor.matmul(ps_f[0][:, mt * N:(mt + 1) * N], w_o[k][:, j, U(mt)], attn_t[:, j, :],
                                     start=j == 0, stop=j == INNER // P - 1)
        body.mark("pe", m, "w_o")
        body.wait("dve", "w_o")
        body.wait("dve", "mean", back=1)
        body.wait("dve", "state", back=1)
        body.mark("dve", nc.vector.tensor_tensor(whole(x1), ps_f[0][:, :].rearrange("p (k n) -> p k n", k=KT),
                                                 whole(xa), ALU.add), "x1")
        body.wait("pe", "x1")
        body.wait("pe", "gated", NJ - 1, back=1)
        for kt in range(KT):
            m = nc.tensor.matmul(ps_f[1][:, 0:N], mean_w[:, :], shifted(x1)[:, kt, :],
                                 start=kt == 0, stop=kt == KT - 1)
        body.mark("pe", m, "mean")
        body.wait("dve", "mean")
        body.wait("dve", "cent2", back=1)
        body.mark("dve", nc.vector.tensor_tensor(cent[:, :, :], shifted(x1),
                                                 ps_f[1][:, 0:N].unsqueeze(1).broadcast_to([P, KT, N]),
                                                 ALU.subtract), "cent")
        body.wait("act", "cent")
        body.wait("act", "var", back=1)
        body.mark("act", nc.scalar.activation(cent2[:, :, :], cent[:, :, :], ACT.Square), "cent2")
        body.wait("pe", "cent2")
        for kt in range(KT):
            m = nc.tensor.matmul(ps_f[1][:, N:2 * N], mean_w[:, :], cent2[:, kt, :],
                                 start=kt == 0, stop=kt == KT - 1)
        body.mark("pe", m, "var")
        body.wait("act", "var")
        body.wait("act", "normed", back=1)
        body.mark("act", nc.scalar.activation(sdev[:, :], ps_f[1][:, N:2 * N], ACT.Sqrt, bias=eps_ln[:, :]),
                  "sdev")
        body.wait("dve", "sdev")
        body.mark("dve", nc.vector.reciprocal(sdev[:, :], sdev[:, :]), "rdev")
        body.wait("dve", "rdev")
        body.mark("dve", nc.vector.tensor_tensor(cent[:, :, :], cent[:, :, :],
                                                 sdev[:, :].unsqueeze(1).broadcast_to([P, KT, N]), ALU.mult),
                  "normed")
        body.wait("dve", "normed")
        body.wait("dve", "hid", NJ - 1, back=1)
        for kt in range(KT):
            m = nc.vector.tensor_scalar(lin_in[:, kt, :], cent[:, kt, :], gain[:, kt:kt + 1],
                                        shift[:, kt:kt + 1], ALU.mult, ALU.add)
        body.mark("dve", m, "lin_in")
        body.wait("pe", "lin_in")
        for j in range(NJ):
            w = min(P, DI - j * P)
            f = ps_f[j % 2]
            if j == 0:
                body.wait("pe", "x1")
            elif j == 1:
                body.wait("pe", "sdev")
            else:
                body.wait("pe", "gated", j - 2)
            for kt in range(KT):
                m = nc.tensor.matmul(f[0:w, 0:N], w_1[k][:, kt, j * P:j * P + w], lin_in[:, kt, :],
                                     start=kt == 0, stop=kt == KT - 1)
            for kt in range(KT):
                m = nc.tensor.matmul(f[0:w, N:2 * N], w_1[k][:, kt, DI + j * P:DI + j * P + w], lin_in[:, kt, :],
                                     start=kt == 0, stop=kt == KT - 1)
            body.mark("pe", m, "hid", j)
            body.wait("act", "hid", j)
            if j >= 2:
                body.wait("act", "gated", j - 2)
            else:
                body.wait("act", "gated", j + NJ - 2, back=1)
            body.mark("act", nc.scalar.activation(gate[0:w, j % 2, :], f[0:w, N:2 * N], ACT.Gelu,
                                                  bias=b_g[0:w, j:j + 1]), "gate", j)
            body.wait("dve", "gate", j)
            if j == 0:
                body.wait("dve", "out", back=1)
            body.mark("dve", nc.vector.scalar_tensor_tensor(
                out=hidden[0:w, j, :], in0=f[0:w, 0:N], scalar=b_a[0:w, j:j + 1], in1=gate[0:w, j % 2, :],
                op0=ALU.add, op1=ALU.mult), "gated", j)
        body.wait("pe", "gated", NJ - 1)
        for mt in range(KT):
            for j in range(NJ):
                w = min(P, DI - j * P)
                m = nc.tensor.matmul(ps_f[0][:, mt * N:(mt + 1) * N], w_2[k][0:w, j, U(mt)], hidden[0:w, j, :],
                                     start=j == 0, stop=j == NJ - 1)
        body.mark("pe", m, "out")
        body.wait("dve", "out")
        for mt in range(KT):
            m = nc.vector.scalar_tensor_tensor(
                out=state[:, bass.ds(b, 1), mt * PAD + 1:(mt + 1) * PAD].rearrange("p o n -> p (o n)"),
                in0=ps_f[0][:, mt * N:(mt + 1) * N], scalar=b_2[:, mt:mt + 1],
                in1=whole(x1)[:, mt, :], op0=ALU.add, op1=ALU.add)
        body.mark("dve", m, "state")

    def one_batch(k, b, step):
        body.begin(step)
        body.wait("pool", "x1", back=1)
        body.wait("pool", "v", UNITS - 1, back=1)
        body.wait("pool", "state", back=1)
        body.mark("pool", nc.gpsimd.tensor_copy(
            xa[:, :], state[:, bass.ds(b, 1), :].rearrange("p o n -> p (o n)")), "xa")
        body.wait("pe", "xa")
        body.wait("dve", "xa")
        stages = (lambda i: (project(i, k), rotate(i, k)), flip_qk, score_soften, flip_prob, attend)
        for t in range(UNITS + len(stages) - 1):
            for s in reversed(range(len(stages))):
                if 0 <= t - s < UNITS:
                    stages[s](t - s)
        feed_forward(k, b)
        body.end()

    def score_soften(i):
        score(i)
        soften(i)

    with nc.Fori(0, DEPTH // 2) as pair:
        for k in range(2):
            step = pair * 2 + k
            sec.begin(step)
            for lane in ("pe", "act", "dve"):
                sec.eng[lane].wait_ge(dma_w[k], (pair + 1) * (16 * W_DMAS))
            sec.carry("pe")
            sec.carry("act")
            nc.vector.wait_ge(body.sem["dve"], (pair * 2 + k) * (B * body.per["dve"]) + body.per["dve"])
            gb = qk_gain[k].ap().unsqueeze(1).broadcast_to([P, NU, 2, DH])
            m = nc.vector.tensor_tensor(cos_t.ap(), rot_cos.ap(), gb, ALU.mult)
            for a in range(2):
                turn = qk_gain[k][:, a, :].rearrange("p (t d) -> p t d", t=2)[:, ::-1, :]
                m = nc.vector.tensor_tensor(
                    sin_t[:, :, a, :].rearrange("p u (t d) -> p u t d", t=2),
                    rot_sin[:, :, a, :].rearrange("p u (t d) -> p u t d", t=2),
                    turn.unsqueeze(1).broadcast_to([P, NU, 2, DH // 2]), ALU.mult)
            sec.mark("dve", m, "tables")
            sec.wait("dve", "tables")
            sec.carry("dve")
            sec.end()
            with nc.Fori(0, B) as b:
                one_batch(k, b, pair * (2 * B) + (k * B + b))
            for lane in ("pe", "act", "dve"):
                nc.sync.wait_ge(body.sem[lane], (pair * 2 + k + 1) * (B * body.per[lane]) + body.per[lane])
            sec.carry("sp")
            with nc.sync.If(pair < DEPTH // 2 - 1):
                load_layer(k, (pair * 2 + (k + 2)) % DEPTH)
    nc.all_engine_barrier()
def build(nc, io, out, counts):
    made = {}
    ctx = ExitStack()
    with ctx:
        state = ctx.enter_context(nc.sbuf_tensor("state", [P, B, KT * PAD], F32))
        resid = ctx.enter_context(nc.sbuf_tensor("resid", [P, B, KT * N], F32))
        ident = ctx.enter_context(nc.sbuf_tensor("ident", [P, P], F32))
        eps_ln = ctx.enter_context(nc.sbuf_tensor("eps_ln", [P, 1], F32))
        begun = ctx.enter_context(nc.semaphore("begun"))
        nc.gpsimd.memset(ident[:, :], 0.0).then_inc(begun, 1)
        nc.gpsimd.memset(eps_ln[:, :], 1e-5).then_inc(begun, 1)
        nc.gpsimd.memset(state[:, :, :], 0.0).then_inc(begun, 1)
        nc.gpsimd.wait_ge(begun, 3)
        nc.gpsimd.affine_select(out=ident[:, :], in_=ident[:, :], compare_op=ALU.not_equal, fill=1.0, base=0,
                                pattern=[[-1, P]], channel_multiplier=1).then_inc(begun, 1)
        nc.gpsimd.wait_ge(begun, 4)
        nc.all_engine_barrier()
        Stretch.made = made
        with ExitStack() as part:
            conditioned_blocks(nc, part, counts, io, ident, eps_ln, state, resid)
        with ExitStack() as part:
            local_layers(nc, part, counts, io, state, ident, eps_ln)
        with ExitStack() as part:
            write_out(nc, part, counts, out, ident, state, resid)
    return made


def shape_tables():
    half = np.arange(0, DH, 2, dtype=np.float64)
    t = np.arange(N, dtype=np.float64)[:, None]
    freqs = t * (1.0 / 10000.0 ** (half / DH))[None, :]
    scale = ((half + 0.4 * DH) / (1.4 * DH))[None, :] ** ((t - N // 2) / (WIN // 2))
    cos, sin = np.cos(freqs), np.sin(freqs)
    c = np.stack([np.concatenate([cos * s, cos * s], 1) for s in (scale, 1 / scale)], 1)
    s = np.stack([np.concatenate([-sin * s, sin * s], 1) for s in (scale, 1 / scale)], 1)
    tile = lambda a: np.ascontiguousarray(a.reshape(NU, P, 2, DH).transpose(1, 0, 2, 3).reshape(P, -1),
                                          dtype=np.float32)
    r, j = np.arange(P)[:, None], np.arange(P)[None, :]
    odd, upper = r >= WIN, j >= WIN
    i, jj = r % WIN, j % WIN
    valid = np.where(odd == upper, jj <= i, jj >= i)
    first = valid & ~(~odd & upper)
    band = np.where(np.concatenate([first, valid], 1), 0.0, -1e30)
    return tile(c), tile(s), band


def lay_out(a):
    cc = np.ascontiguousarray
    rowtile = lambda w: cc(w.reshape(-1, P, w.shape[-1]).transpose(1, 0, 2).reshape(P, -1))
    col = lambda v: v.reshape(-1, P).T

    def slotted(w):
        z = np.zeros((w.shape[0], NH, SLOT), w.dtype)
        z[:, :, :HD] = w.reshape(w.shape[0], NH, HD)
        return z.reshape(w.shape[0], NH * SLOT)

    c, f = "L0_cond_", "L0_ffn_"
    x = {"x": a["x"]}
    ids = np.stack([a["itok_BxS_0_999"], a["itok_BxS_0_4"], a["mask_BxS_ik0"]])
    x["ids"] = cc(ids.reshape(3, B * NU, P).transpose(2, 0, 1).reshape(P, -1))
    x["t_pw"] = np.concatenate([a[c + "pw_g"], a[c + "pw_b"]], 1)
    x["t_ct"] = np.concatenate([a[c + k] for k in ("cp_g", "cp_b", "tm_g", "tm_b")], 1)
    x["t_ms"] = np.concatenate([a[c + "ms_g"], a[c + "ms_b"]], 1)
    x["w_int1"], x["w_int2"] = rowtile(a[c + "int_W1"]), rowtile(a[c + "int_W2"])
    w, bq = a["L0_attn_W_qkv"], a["L0_attn_b_qkv"][None, :]
    x["w_qk"] = rowtile(np.concatenate([slotted(w[:, 0:D]), slotted(w[:, D:2 * D])], 1))
    x["w_v"] = rowtile(w[:, 2 * D:])
    x["w_proj"] = rowtile(a["L0_attn_W_proj"])
    x["k_w"], x["o_w"] = rowtile(a["L0_cond2_k_w"].T), rowtile(a["L0_cond2_o_w"].T)
    x["aff0"], x["aff1"] = cc(a["L0_cond2_k_aff_w"].T), cc(a["L0_cond2_o_aff_w"].T)
    x["fcols"] = cc(np.concatenate(
        [col(a[c + k]) for k in ("mem_b1", "noi_b1", "res_b1", "int_b1")]
        + [col(a["L0_cond2_k_aff_b"]), col(a["L0_cond2_o_aff_b"]), col(a["L0_attn_b_proj"]), col(a["L0_cond2_o_b"])]
        + [col(slotted(bq[:, 0:D])[0]), col(slotted(bq[:, D:2 * D])[0])], 1))
    x["rows"] = np.concatenate([a[c + "int_b2"], a[c + "int_g"], a[c + "int_be"], bq[0, 2 * D:],
                                a["L0_cond2_k_b"]])[None, :]
    x["aw"] = a[c + "aw"][None, :]
    for m, (k, s) in enumerate((("mem", "cond_512"), ("noi", "cond_64"), ("res", "fside_Bx32_0"))):
        x[f"s_t{m}"] = cc(a[s].T)
        x[f"m_w1{m}"] = a[f"{c}{k}_W1"]
        x[f"m_w2{m}"] = rowtile(a[f"{c}{k}_W2"])
    x["m_rows"] = np.concatenate([a[f"{c}{k}_{q}"] for k in ("mem", "noi", "res") for q in ("b2", "g", "be")])[None, :]

    L = DEPTH
    w = a[f + "Wqkv"].reshape(L, KT, P, 3, NG, GC).transpose(0, 2, 1, 4, 3, 5)
    x["w_qkv"] = cc(w.reshape(L, P, -1))
    x["w_o"] = cc(a[f + "Wo"].reshape(L, INNER // P, P, D).transpose(0, 2, 1, 3).reshape(L, P, -1))
    x["w_1"] = cc(a[f + "W1"].reshape(L, KT, P, 2 * DI).transpose(0, 2, 1, 3).reshape(L, P, -1))
    pad = np.zeros((L, NJ * P - DI, D), np.float32)
    x["w_2"] = cc(np.concatenate([a[f + "W2"], pad], 1).reshape(L, NJ, P, D).transpose(0, 2, 1, 3).reshape(L, P, -1))
    cols3 = lambda v: v.reshape(L, -1, P).transpose(0, 2, 1)
    padded = lambda v: np.concatenate([v, np.zeros((L, NJ * P - DI), np.float32)], 1)
    b1 = a[f + "b1"]
    x["cols"] = cc(np.concatenate([cols3(a[f + "ln_g"]), cols3(a[f + "ln_b"]), cols3(padded(b1[:, :DI])),
                                   cols3(padded(b1[:, DI:])), cols3(a[f + "b2"])], 2))
    x["qk_gain"] = np.concatenate([a[f + "q_scale"], a[f + "k_scale"]], 1)
    x["rot_cos"], x["rot_sin"], x["band"] = shape_tables()
    return x


def kernel(**inputs):
    import ml_dtypes
    from concourse import bacc
    from concourse.bass_utils import run_bass_kernel_spmd

    arrays = {k: np.ascontiguousarray(v) for k, v in
              lay_out({k: np.asarray(v) for k, v in inputs.items()}).items()}
    arrays["band"] = arrays["band"].astype(ml_dtypes.bfloat16)
    counts = {}
    for _ in range(2):
        nc = bacc.Bacc("TRN2", target_bir_lowering=False, num_devices=1)
        io = {k: nc.dram_tensor(f"in_{k}", v.shape, mybir.dt.from_np(v.dtype), kind="ExternalInput").ap()
              for k, v in arrays.items()}
        out = nc.dram_tensor("out", (B, N, D), F32, kind="ExternalOutput").ap()
        counts = build(nc, io, out, counts)
    r = run_bass_kernel_spmd(nc, [{f"in_{k}": v for k, v in arrays.items()}], core_ids=[0])
    return r.results[0]["out"]
```

```python
from contextlib import ExitStack

import numpy as np
import concourse.bass as bass
import concourse.mybir as mybir
from concourse.alu_op_type import AluOpType as ALU

F32 = mybir.dt.float32
BF16 = mybir.dt.bfloat16
I32 = mybir.dt.int32
ACT = mybir.ActivationFunctionType
AX = mybir.AxisListType

P = 128
B, N, D = 8, 256, 256
NU = N // P
KT = D // P
LANES = ("pe", "act", "dve", "pool", "sp")


class Stretch:

    def __init__(self, nc, ctx, name, counts, steps):
        self.name, self.steps, self.new = name, steps, {}
        self.old = counts.get(name, {})
        self.eng = dict(zip(LANES, (nc.tensor, nc.scalar, nc.vector, nc.gpsimd, nc.sync)))
        self.carrier = ctx.enter_context(nc.semaphore(f"{name}_carrier"))
        self.sem = {lane: ctx.enter_context(nc.semaphore(f"{name}_{lane}")) for lane in LANES}
        self.per = {lane: self.old.get(("per", lane), 1) for lane in LANES}
        self.base, self.count, self.seen = {}, {}, {}
        if steps:
            for lane in LANES:
                self.eng[lane].sem_inc(self.sem[lane], self.per[lane])

    def begin(self, step=0):
        self.step, self.base, self.seen = step, {}, {}
        self.count = {lane: 0 for lane in LANES}

    def mark(self, lane, instruction, *name):
        self.count[lane] += 1
        assert name not in self.new or self.new[name] == (lane, self.count[lane]), name
        self.new[name] = (lane, self.count[lane])
        instruction.then_inc(self.sem[lane], 1)
        return instruction

    def wait(self, lane, *name, back=0):
        maker, at = self.old.get(name, ("pe", 1))
        at -= back * self.per[maker]
        if self.old and self.seen.get((lane, maker), -10**9) >= at:
            return
        self.seen[lane, maker] = at
        if (lane, maker) not in self.base:
            before = (self.step + 1) * self.per[maker] if self.steps else 0
            self.base[lane, maker] = before if isinstance(before, int) else self.eng[lane].snap(before)
        self.eng[lane].wait_ge(self.sem[maker], self.base[lane, maker] + at)

    def carry(self, lane):
        self.eng[lane].sem_inc(self.carrier, 1)

    def wait_unit(self, lane, name, unit, units):
        if unit < 0:
            if self.steps:
                self.wait(lane, name, unit + units, back=1)
        else:
            self.wait(lane, name, unit)

    def end(self):
        for lane in LANES:
            self.new["per", lane] = max(self.count[lane], 1)
        Stretch.made[self.name] = self.new


NH, HD = 16, 16
NTILE = 4
SLOT = 32
INT_IN = 6
FQ = NTILE * P


def conditioned_blocks(nc, ctx, counts, io, ident, eps_ln, state, resid):
    def sb(name, shape, dt=F32):
        return ctx.enter_context(nc.sbuf_tensor(name, shape, dt))

    banks = [ctx.enter_context(nc.psum_tensor(f"bank{k}", [P, 512], F32)) for k in range(8)]

    ids = sb("ids", [P, 3, NU * B], I32)
    w_int1 = sb("w_int1", [P, 2 * INT_IN, D])
    w_mix = sb("w_mix", [P, 8, D])
    w_int2 = sb("w_int2", [P, KT, D])
    w_qk = sb("w_qk", [P, KT, 2 * FQ])
    w_v = sb("w_v", [P, KT, D])
    w_proj = sb("w_proj", [P, KT, D])
    k_w, o_w = sb("k_w", [P, KT, D]), sb("o_w", [P, KT, D])
    rows = sb("rows", [P, 5, D])
    fcols = sb("fcols", [P, 16 + 2 * NTILE])
    aw = sb("aw", [P, INT_IN])
    s_t = [sb(f"s_t{m}", [w, B]) for m, w in enumerate((128, 64, 32))]
    m_w1 = [sb(f"m_w1{m}", [w, D]) for m, w in enumerate((128, 64, 32))]
    m_w2 = [sb(f"m_w2{m}", [P, KT, D]) for m in range(3)]
    m_rows = sb("m_rows", [B, 3, 3, D])
    aff = [sb(f"aff{m}", [P, D]) for m in range(2)]
    ones = sb("ones", [P, P])
    slots = sb("slots", [P, P // SLOT])
    nhalf = sb("nhalf", [P, NH])
    mix = sb("mix", [P, INT_IN])
    amax, esum, erec = sb("amax", [P, 1]), sb("esum", [P, 1]), sb("erec", [P, 1])
    m_hid = sb("m_hid", [P, KT, B])
    m_out, m_norm = sb("m_out", [B, D]), sb("m_norm", [B, D])
    m_stat, m_mv, m_sd, m_rs = sb("m_stat", [B, 6]), sb("m_mv", [B, 2]), sb("m_sd", [B, 1]), sb("m_rs", [B, 1])
    m_t = sb("m_t", [P, 3, KT, B])
    int_bias = sb("int_bias", [P, KT, B])
    style = sb("style", [P, 4, B])
    k_sq, o_sq = sb("k_sq", [P, KT, D]), sb("o_sq", [P, KT, D])
    eps_mod = sb("eps_mod", [P, 1])

    dma = ctx.enter_context(nc.semaphore("dma_front"))
    pre = Stretch(nc, ctx, "front_setup", counts, 0)
    body = Stretch(nc, ctx, "front", counts, B)

    pre.begin()
    n = 0
    flat = {2: None, 3: "p a b -> p (a b)", 4: "p a b c -> p (a b c)"}
    for dst, src in (
        [(ids, "ids"), (w_int1, "w_int1"), (w_int2, "w_int2"), (w_qk, "w_qk"), (w_v, "w_v"),
         (w_proj, "w_proj"), (k_w, "k_w"), (o_w, "o_w"), (fcols, "fcols")]
        + [(s_t[m], f"s_t{m}") for m in range(3)] + [(m_w1[m], f"m_w1{m}") for m in range(3)]
        + [(m_w2[m], f"m_w2{m}") for m in range(3)] + [(aff[m], f"aff{m}") for m in range(2)]
    ):
        d = dst[:, :] if len(dst.shape) == 2 else dst.ap().rearrange(flat[len(dst.shape)])
        nc.sync.dma_start(d, io[src]).then_inc(dma, 16)
        n += 16
    for dst, src, w in ((rows, "rows", P), (aw, "aw", P), (m_rows, "m_rows", B)):
        d = dst[:, :] if len(dst.shape) == 2 else dst.ap().rearrange(flat[len(dst.shape)])
        nc.scalar.dma_start(d, io[src].broadcast_to([w, io[src].shape[1]])).then_inc(dma, 16)
        n += 16
    pre.mark("pool", nc.gpsimd.memset(ones[:, :], 1.0), "ones")
    pre.mark("pool", nc.gpsimd.memset(nhalf[:, :], -0.5), "nhalf")
    pre.mark("pool", nc.gpsimd.memset(eps_mod[:, :], 1e-8), "eps_mod")
    pre.mark("dve", nc.vector.memset(slots[:, :], 0.0), "slots0")
    pre.wait("dve", "slots0")
    for g in range(P // SLOT):
        m = nc.vector.memset(slots[g * SLOT:(g + 1) * SLOT, g:g + 1], 1.0)
    pre.mark("dve", m, "slots")
    for lane in ("pe", "act", "dve", "pool"):
        pre.eng[lane].wait_ge(dma, n)
    pre.mark("dve", nc.vector.tensor_reduce(amax[:, :], aw[:, :], AX.X, ALU.max, negate=True), "amax")
    pre.wait("act", "amax")
    pre.mark("act", nc.scalar.activation(mix[:, :], aw[:, :], ACT.Exp, bias=amax[:, :], accum_out=esum[:, :]),
             "mix_exp")
    pre.wait("dve", "mix_exp")
    pre.mark("dve", nc.vector.reciprocal(erec[:, :], esum[:, :]), "erec")
    pre.wait("dve", "erec")
    pre.mark("dve", nc.vector.tensor_scalar(mix[:, :], mix[:, :], erec[:, 0:1], None, ALU.mult), "mix")
    pre.wait("dve", "mix")
    for dst, blk in ((0, 0), (2, 1), (6, 5)):
        nc.vector.tensor_scalar(w_mix[:, dst:dst + 2, :], w_int1[:, 2 * blk:2 * blk + 2, :],
                                mix[:, blk:blk + 1], None, ALU.mult)
    pre.mark("dve", nc.vector.tensor_scalar(w_mix[:, 4:6, :], w_int1[:, 4:6, :], mix[:, 2:3], None, ALU.mult),
             "w_mix", 2)
    for blk in (3, 4):
        pre.wait("dve", "w_mix", blk - 1)
        for kt in range(KT):
            m = nc.vector.scalar_tensor_tensor(out=w_mix[:, 4 + kt, :], in0=w_int1[:, 2 * blk + kt, :],
                                               scalar=mix[:, blk:blk + 1], in1=w_mix[:, 4 + kt, :],
                                               op0=ALU.mult, op1=ALU.add)
        pre.mark("dve", m, "w_mix", blk)
    for m3 in range(3):
        if m3:
            pre.wait("pe", "m_hid", m3 - 1)
        for mt in range(KT):
            m = nc.tensor.matmul(banks[0][:, mt * B:(mt + 1) * B], m_w1[m3][:, mt * P:(mt + 1) * P],
                                 s_t[m3][:, :], start=True, stop=True)
        pre.mark("pe", m, "m_h", m3)
        pre.wait("act", "m_h", m3)
        if m3:
            pre.wait("act", "m_o", m3 - 1)
        for mt in range(KT):
            m = nc.scalar.activation(m_hid[:, mt, :], banks[0][:, mt * B:(mt + 1) * B], ACT.Silu,
                                     bias=fcols[:, 2 * m3 + mt:2 * m3 + mt + 1])
        pre.mark("act", m, "m_hid", m3)
        pre.wait("pe", "m_hid", m3)
        if m3:
            pre.wait("pe", "m_out", m3 - 1)
        for kt in range(KT):
            m = nc.tensor.matmul(banks[1][0:B, 0:D], m_hid[:, kt, :], m_w2[m3][:, kt, :],
                                 start=kt == 0, stop=kt == KT - 1)
        pre.mark("pe", m, "m_o", m3)
        pre.wait("dve", "m_o", m3)
        pre.mark("dve", nc.vector.tensor_tensor(m_out[:, :], banks[1][0:B, 0:D], m_rows[:, m3, 0, :], ALU.add),
                 "m_out", m3)
        pre.wait("dve", "m_out", m3)
        pre.mark("dve", nc.vector.bn_stats(m_stat[:, :], m_out[:, :]), "m_stat", m3)
        pre.wait("dve", "m_stat", m3)
        pre.mark("dve", nc.vector.bn_aggr(m_mv[:, :], m_stat[:, :]), "m_mv", m3)
        pre.wait("act", "m_mv", m3)
        pre.mark("act", nc.scalar.activation(m_sd[:, :], m_mv[:, 1:2], ACT.Sqrt, bias=eps_ln[0:B, :]), "m_sd", m3)
        pre.wait("dve", "m_sd", m3)
        pre.mark("dve", nc.vector.reciprocal(m_rs[:, :], m_sd[:, :]), "m_rs", m3)
        pre.wait("dve", "m_rs", m3)
        pre.mark("dve", nc.vector.tensor_scalar(m_norm[:, :], m_out[:, :], m_mv[:, 0:1], m_rs[:, 0:1],
                                                ALU.subtract, ALU.mult), "m_n0", m3)
        pre.wait("dve", "m_n0", m3)
        pre.mark("dve", nc.vector.tensor_tensor(m_norm[:, :], m_norm[:, :], m_rows[:, m3, 1, :], ALU.mult),
                 "m_n1", m3)
        pre.wait("dve", "m_n1", m3)
        pre.mark("dve", nc.vector.tensor_tensor(m_norm[:, :], m_norm[:, :], m_rows[:, m3, 2, :], ALU.add),
                 "m_n2", m3)
        pre.wait("pe", "m_n2", m3)
        if m3:
            pre.wait("pe", "m_t", m3 - 1)
        for kt in range(KT):
            m = nc.tensor.transpose(banks[2][:, kt * B:(kt + 1) * B], m_norm[:, kt * P:(kt + 1) * P],
                                    ident[0:B, 0:B])
        pre.mark("pe", m, "m_tp", m3)
        pre.wait("dve", "m_tp", m3)
        pre.mark("dve", nc.vector.tensor_scalar(m_t[:, m3, :, :].rearrange("p a b -> p (a b)"),
                                                banks[2][:, 0:KT * B], mix[:, 2 + m3:3 + m3], None, ALU.mult),
                 "m_t", m3)
    pre.wait("pe", "m_t", 2)
    for mt in range(KT):
        for m3 in range(3):
            for kt in range(KT):
                m = nc.tensor.matmul(banks[3][:, mt * B:(mt + 1) * B],
                                     w_int1[:, 4 + 2 * m3 + kt, mt * P:(mt + 1) * P], m_t[:, m3, kt, :],
                                     start=m3 + kt == 0, stop=m3 == 2 and kt == KT - 1)
    pre.mark("pe", m, "int_bias_ps")
    pre.wait("dve", "int_bias_ps")
    for mt in range(KT):
        m = nc.vector.tensor_scalar(int_bias[:, mt, :], banks[3][:, mt * B:(mt + 1) * B],
                                    fcols[:, 6 + mt:7 + mt], None, ALU.add)
    pre.mark("dve", m, "int_bias")
    for m2 in range(2):
        for mt in range(KT):
            c = 2 * m2 + mt
            m = nc.tensor.matmul(banks[4][:, c * B:(c + 1) * B], aff[m2][:, mt * P:(mt + 1) * P], s_t[0][:, :],
                                 start=True, stop=True)
    pre.mark("pe", m, "style_ps")
    pre.wait("dve", "style_ps")
    for c in range(4):
        m = nc.vector.tensor_scalar(style[:, c, :], banks[4][:, c * B:(c + 1) * B], fcols[:, 8 + c:9 + c], None,
                                    ALU.add)
    pre.mark("dve", m, "style")
    nc.scalar.activation(k_sq.ap(), k_w.ap(), ACT.Square)
    pre.mark("act", nc.scalar.activation(o_sq.ap(), o_w.ap(), ACT.Square), "w_sq")
    pre.end()
    nc.all_engine_barrier()

    x_tok = sb("x_tok", [P, NU, D])
    idc = sb("idc", [P, 3, NU], I32)
    pw = sb("pw", [P, NU, 2 * D])
    ct = sb("ct", [P, NU, 4 * D])
    ms = sb("ms", [P, NU, 2 * D])
    stat, mv = sb("stat", [P, NU, 6]), sb("mv", [P, NU, 2])
    rs = sb("rs", [P, NU])
    xh, hh, tt, ss = (sb(q, [P, NU, D]) for q in ("xh", "hh", "tt", "ss"))
    cat = sb("cat", [P, 8, N])
    ibc = sb("ibc", [P, KT])
    hid = sb("hid_t", [P, KT, N])
    y, y_t = sb("y", [P, NU, D]), sb("y_t", [P, KT, N])
    q_t, k_t = sb("q_t", [P, NTILE, N]), sb("k_t", [P, NTILE, N])
    v = sb("v_rows", [P, NU, D])
    junk = sb("junk", [P, N])
    qsq, kab, yab = sb("qsq", [P, NTILE]), sb("kab", [P, NTILE]), sb("yab", [P, KT])
    ymax, yinf, yrec = sb("ymax", [P, 1]), sb("yinf", [P, 1]), sb("yrec", [P, 1])
    qmask, fro = sb("qmask", [P, NH]), sb("fro", [P, NH])
    scl = sb("scl", [P, NH])
    rmax, rbias = sb("rmax", [P, 2, 2]), sb("rbias", [P, 2, 2])
    pr, pr_t = sb("pr", [P, 2, 2, N]), sb("pr_t", [P, 2, 2, NU, P])
    psm, pri = sb("psm", [P, NU, NH]), sb("pri", [P, NU, NH])
    o, o_t = sb("o", [P, NU, D]), sb("o_t", [P, KT, N])
    x_t = sb("x_t", [P, KT, N])
    x1 = sb("x1_t", [P, KT, N])
    stc, stc2 = sb("stc", [P, 4]), sb("stc2", [P, 4])
    stw = sb("stw", [P, 4, P])
    dem, demr = sb("dem", [P, 2, D]), sb("demr", [P, 2, D])
    w_m = sb("w_m", [P, 2, KT, D])
    kx = sb("kx", [P, NU, D])
    prod = sb("prod", [P, NH, NH, HD])
    sc, scm, scs, scr = sb("sc", [P, NH, NH]), sb("scm", [P, NH]), sb("scs", [P, NH]), sb("scr", [P, NH])
    o2, o2_t = sb("o2", [P, NU, D]), sb("o2_t", [P, KT, N])
    dma_x = ctx.enter_context(nc.semaphore("dma_x"))
    dma_g = [ctx.enter_context(nc.semaphore(f"dma_g{k}")) for k in range(3)]

    def W(lane, *name, **kw):
        body.wait(lane, *name, **kw)

    def M(lane, m, *name):
        body.mark(lane, m, *name)

    def dve(m, *name):
        M("dve", m, *name)
        W("dve", *name)

    T = lambda a: slice(a * P, (a + 1) * P)
    two = lambda bank: bank[:, :].rearrange("p (a n) -> p a n", a=2)
    V, A, G, E = nc.vector, nc.scalar, nc.gpsimd, nc.tensor
    VT, TS = V.tensor_tensor, V.tensor_scalar

    def flip(src, bank, name, need, free):
        for w in need + free:
            W("pe", *w[:-1], back=w[-1])
        for kt in range(KT):
            for u in range(NU):
                m = E.transpose(bank[:, kt * N + u * P:][:, 0:P], src[:, u, T(kt)], ident[:, :])
        M("pe", m, name)

    def norm_stats(src, name):
        for u in range(NU):
            m = V.bn_stats(stat[:, u, :], src[:, u, :])
        dve(m, name, "stat")
        body.carry("dve")
        for u in range(NU):
            m = V.bn_aggr(mv[:, u, :], stat[:, u, :])
        dve(m, name, "mv")
        dve(TS(mv[:, :, 1], mv[:, :, 1], 1e-5, None, ALU.add), name, "var")
        W("pool", name, "var")
        M("pool", G.tensor_tensor(rs[:, :], mv[:, :, 1], nhalf[:, 0:NU], ALU.pow), name, "rs")
        W("dve", name, "rs")

    def normalise(dst, src, name):
        for u in range(NU):
            m = TS(dst[:, u, :], src[:, u, :], mv[:, u, 0:1], rs[:, u:u + 1], ALU.subtract, ALU.mult)
        M("dve", m, name, "norm")

    with nc.Fori(0, B) as b:
        body.begin(b)
        W("sp", "xflip", back=1)
        W("sp", "xstat", "norm", back=1)
        nc.sync.dma_start(x_tok.ap(), io["x"][bass.ds(b, 1), :, :].rearrange("o (u p) d -> p (o u) d", p=P)
                          ).then_inc(dma_x, 16)
        W("pool", "s_add", back=1)
        W("pool", "h_add", back=1)
        M("pool", G.tensor_copy(idc.ap(), ids[:, :, bass.ds(b * NU, NU)]), "idc")
        W("pool", "idc")
        body.carry("pool")
        for k, (dst, tab) in enumerate(((pw, "t_pw"), (ct, "t_ct"), (ms, "t_ms"))):
            for u in range(NU):
                G.indirect_dma_start(dst[:, u, :], None, io[tab],
                                     bass.IndirectOffsetOnAxis(ap=idc[:, k, u:u + 1], axis=0)
                                     ).then_inc(dma_g[k], 16)
        V.wait_ge(dma_x, (b + 1) * 16)
        W("dve", "xflip", back=1)
        norm_stats(x_tok, "xstat")
        W("dve", "s_mul", back=1)
        normalise(xh, x_tok, "xstat")
        W("dve", "xstat", "norm")
        V.wait_ge(dma_g[0], (b + 1) * (16 * NU))
        W("dve", "hflip", back=1)
        dve(VT(hh.ap(), xh.ap(), pw[:, :, 0:D], ALU.mult), "h_mul0")
        dve(VT(hh.ap(), hh.ap(), pw[:, :, D:2 * D], ALU.add), "h_add0")
        G.wait_ge(dma_g[1], (b + 1) * (16 * NU))
        W("pool", "xstat", "norm")
        W("pool", "tflip", back=1)
        M("pool", G.tensor_tensor(tt.ap(), xh.ap(), ct[:, :, 2 * D:3 * D], ALU.mult), "t_mul")
        W("pool", "t_mul")
        M("pool", G.tensor_tensor(tt.ap(), tt.ap(), ct[:, :, 3 * D:4 * D], ALU.add), "t_add")
        G.wait_ge(dma_g[2], (b + 1) * (16 * NU))
        W("pool", "sflip", back=1)
        M("pool", G.tensor_tensor(ss.ap(), xh.ap(), ms[:, :, 0:D], ALU.mult), "s_mul")
        W("pool", "s_mul")
        M("pool", G.tensor_tensor(ss.ap(), ss.ap(), ms[:, :, D:2 * D], ALU.add), "s_add")
        norm_stats(hh, "hstat")
        normalise(hh, hh, "hstat")
        W("dve", "hstat", "norm")
        V.wait_ge(dma_g[1], (b + 1) * (16 * NU))
        dve(VT(hh.ap(), hh.ap(), ct[:, :, 0:D], ALU.mult), "h_mul")
        M("dve", VT(hh.ap(), hh.ap(), ct[:, :, D:2 * D], ALU.add), "h_add")
        E.wait_ge(dma_x, (b + 1) * 16)
        flip(x_tok, banks[0], "xflip", [], [("o_t", 1)])
        W("act", "xflip")
        W("act", "resid", back=1)
        W("act", "hid_ps", back=1)
        M("act", A.activation(x_t.ap(), two(banks[0]), ACT.Copy), "x_t")
        M("act", A.activation(cat[:, 4:6, :], two(banks[0]), ACT.Copy), "cat_x")
        for n, (src, ready) in enumerate(((tt, "t_add"), (ss, "s_add"), (hh, "h_add"))):
            name, c = ("tflip", "sflip", "hflip")[n], (2, 6, 0)[n]
            flip(src, banks[1 + n], name, [(ready, 0)], [(("x1", "dem", "kx")[n], 1)])
            W("act", name)
            M("act", A.activation(cat[:, c:c + 2, :], two(banks[1 + n]), ACT.Copy), "cat", n)
        W("act", "hid", back=1)
        M("act", A.activation(ibc[:, :], int_bias[:, :, bass.ds(b, 1)].rearrange("p a o -> p (a o)"), ACT.Copy),
          "ibc")
        W("act", "ibc")
        W("pe", "cat", 2)
        W("pe", "cat_x")
        W("pe", "o2_t", back=1)
        for mt in range(KT):
            for c in range(8):
                m = E.matmul(banks[4][:, mt * N:(mt + 1) * N], w_mix[:, c, T(mt)], cat[:, c, :],
                             start=c == 0, stop=c == 7)
        M("pe", m, "hid_ps")
        W("act", "hid_ps")
        W("act", "y_ps", back=1)
        for mt in range(KT):
            m = A.activation(hid[:, mt, :], banks[4][:, mt * N:(mt + 1) * N], ACT.Silu, bias=ibc[:, mt:mt + 1])
        M("act", m, "hid")
        W("pe", "hid")
        W("pe", "y_b", back=1)
        for u in range(NU):
            for kt in range(KT):
                m = E.matmul(banks[5][:, u * D:(u + 1) * D], hid[:, kt, T(u)], w_int2[:, kt, :],
                             start=kt == 0, stop=kt == KT - 1)
        M("pe", m, "y_ps")
        row = lambda r: rows[:, r, :].unsqueeze(1).broadcast_to([P, NU, D])
        W("dve", "y_ps")
        W("dve", "yflip", back=1)
        dve(VT(y.ap(), two(banks[5]), row(0), ALU.add), "y_b")
        norm_stats(y, "ystat")
        normalise(y, y, "ystat")
        W("dve", "ystat", "norm")
        dve(VT(y.ap(), y.ap(), row(1), ALU.mult), "y_g")
        M("dve", VT(y.ap(), y.ap(), row(2), ALU.add), "y")
        flip(y, banks[0], "yflip", [("y", 0)], [("cat_x", 0), ("x_t", 0)])
        W("act", "yflip")
        W("act", "v_ps", back=1)
        W("act", "junk", NTILE + KT - 1, back=1)
        M("act", A.activation(y_t.ap(), two(banks[0]), ACT.Copy), "y_t")
        W("pe", "y_t")
        for half, (dst, nm) in enumerate(((q_t, "q"), (k_t, "k"))):
            for c in range(2):
                bank = banks[1 + 2 * half + c] if half == 0 else banks[(3, 6)[c]]
                if half == 0:
                    W("pe", "cat", c)
                else:
                    W("pe", "cat", 2)
                    W("pe", "o", back=1)
                for t2 in range(2):
                    t = 2 * c + t2
                    for kt in range(KT):
                        m = E.matmul(bank[:, t2 * N:(t2 + 1) * N],
                                     w_qk[:, kt, half * FQ + t * P:][:, 0:P], y_t[:, kt, :],
                                     start=kt == 0, stop=kt == KT - 1)
                M("pe", m, nm + "_ps", c)
                W("act", nm + "_ps", c)
                W("act", "sc_ps", NH - 1, back=1)
                for t2 in range(2):
                    t = 2 * c + t2
                    m = A.activation(dst[:, t, :], bank[:, t2 * N:(t2 + 1) * N], ACT.Identity,
                                     bias=fcols[:, 16 + half * NTILE + t:][:, 0:1])
                M("act", m, nm, c)
        for u in range(NU):
            if u == 0:
                W("pe", "ostate", back=1)
            for kt in range(KT):
                m = E.matmul(banks[7][:, u * D:(u + 1) * D], y_t[:, kt, T(u)], w_v[:, kt, :],
                             start=kt == 0, stop=kt == KT - 1)
        M("pe", m, "v_ps")
        W("dve", "v_ps")
        W("dve", "av", NH - 1, back=1)
        M("dve", VT(v.ap(), two(banks[7]), row(3), ALU.add), "v")
        W("act", "q", 1)
        W("act", "qmask", back=1)
        W("act", "ymax", back=1)
        for t in range(NTILE):
            W("act", "junk", t - 1) if t else W("act", "junk", NTILE + KT - 1, back=1)
            M("act", A.activation(junk[:, :], q_t[:, t, :], ACT.Square, accum_out=qsq[:, t:t + 1]), "junk", t)
        for kt in range(KT):
            W("act", "junk", NTILE + kt - 1)
            M("act", A.activation(junk[:, :], y_t[:, kt, :], ACT.Abs, accum_out=yab[:, kt:kt + 1]),
              "junk", NTILE + kt)
        W("dve", "junk", NTILE + KT - 1)
        W("dve", "yinf", back=1)
        W("dve", "fro_ps", back=1)
        M("dve", V.tensor_reduce(ymax[:, :], yab[:, :], AX.X, ALU.max), "ymax")
        M("dve", VT(qmask[:, :].rearrange("p (t g) -> p t g", g=4), qsq[:, :].unsqueeze(2).broadcast_to([P, 4, 4]),
                    slots[:, :].unsqueeze(1).broadcast_to([P, 4, 4]), ALU.mult), "qmask")
        W("pool", "ymax")
        W("pool", "yrec", back=1)
        body.carry("pool")
        M("pool", G.partition_all_reduce(yinf[:, :], ymax[:, :], P, bass.bass_isa.ReduceOp.max), "yinf")
        W("pe", "qmask")
        W("pe", "v")
        M("pe", E.matmul(banks[7][:, 0:NH], ones[:, :], qmask[:, :], start=True, stop=True), "fro_ps")
        W("dve", "fro_ps")
        W("dve", "yinf")
        W("dve", "scl0", back=1)
        M("dve", V.tensor_copy(fro[:, :], banks[7][:, 0:NH]), "fro")
        dve(V.reciprocal(yrec[:, :], yinf[:, :]), "yrec")
        W("pool", "fro")
        W("pool", "exp", NH - 1, back=1)
        M("pool", G.tensor_tensor(scl[:, :], fro[:, :], nhalf[:, :], ALU.pow), "scl0")
        W("dve", "scl0")
        dve(TS(scl[:, :], scl[:, :], yrec[:, 0:1], 2.0, ALU.mult, ALU.mult), "scl")
        AU = NH
        SB = (banks[1], banks[2])
        PB = (banks[3], banks[4])
        OB = banks[6]

        def head(hp, e):
            return 4 * (2 * (hp // 4) + e) + hp % 4

        def scores(i):
            hp, u = divmod(i, NU)
            W("pe", "q", 1); W("pe", "k", 1)
            if i >= 2:
                W("pe", "exp", i - 2)
                W("pe", "rmax", i - 2)
            for e in range(2):
                h = head(hp, e)
                t, r = h // 4, slice(SLOT * (h % 4), SLOT * (h % 4) + SLOT)
                m = E.matmul(SB[i % 2][:, e * N:(e + 1) * N], q_t[r, t, T(u)], k_t[r, t, :], start=True, stop=True)
            M("pe", m, "sc_ps", i)

        def softmax(i):
            hp, u = divmod(i, NU)
            s = i % 2
            W("dve", "sc_ps", i)
            if i >= 2:
                W("dve", "exp", i - 2)
            elif i == 0:
                W("dve", "exp", NH - 1, back=1)
            M("dve", V.tensor_reduce(rmax[:, s, :], two(SB[s]), AX.X, ALU.max, negate=True), "rmax", i)
            W("dve", "rmax", i)
            W("dve", "scl")
            M("dve", VT(rbias[:, s, :], rmax[:, s, :], scl[:, head(hp, 0):head(hp, 1) + 1:4], ALU.mult), "rbias", i)
            W("act", "rbias", i)
            if i >= 2:
                W("act", "prt_ps", i - 2)
            else:
                W("act", "prt_ps", NH - 2 + i, back=1)
                W("act", "pri", back=1)
            for e in range(2):
                h = head(hp, e)
                m = A.activation(pr[:, s, e, :], SB[s][:, e * N:(e + 1) * N], ACT.Exp, bias=rbias[:, s, e:e + 1],
                                 scale=scl[:, h:h + 1], accum_out=psm[:, u, h:h + 1])
            M("act", m, "exp", i)

        def flip_p(i):
            s = i % 2
            W("pe", "exp", i)
            if i >= 2:
                W("pe", "prt", i - 2)
            else:
                W("pe", "k", 0); W("pe", "hid")
            for e in range(2):
                for c in range(NU):
                    m = E.transpose(PB[s][:, (2 * e + c) * P:][:, 0:P], pr[:, s, e, T(c)], ident[:, :])
            M("pe", m, "prt_ps", i)
            W("act", "prt_ps", i)
            if i >= 2:
                W("act", "av", i - 2)
            else:
                W("act", "av", NH - 2 + i, back=1)
            M("act", A.activation(pr_t[:, s, :, :, :].rearrange("p a b c -> p (a b c)"), PB[s][:, :], ACT.Copy),
              "prt", i)

        def weigh(i):
            hp, u = divmod(i, NU)
            s = i % 2
            W("pe", "prt", i)
            W("pe", "v")
            if i == 0:
                W("pe", "k", 1)
            for e in range(2):
                h = head(hp, e)
                for c in range(NU):
                    m = E.matmul(OB[:, u * D + h * HD:][:, 0:HD], pr_t[:, s, e, c, :], v[:, c, h * HD:(h + 1) * HD],
                                 start=c == 0, stop=c == NU - 1)
            M("pe", m, "av", i)

        stages = (scores, softmax, flip_p, weigh)
        for t in range(AU + 3):
            for s in reversed(range(4)):
                if 0 <= t - s < AU:
                    stages[s](t - s)
        W("dve", "exp", NH - 1)
        W("dve", "o", back=1)
        dve(V.reciprocal(pri.ap(), psm.ap()), "pri")
        W("dve", "av", NH - 1)
        W("dve", "oflip", back=1)
        M("dve", VT(o.ap().rearrange("p u (h d) -> p u h d", d=HD),
                    two(OB).rearrange("p u (h d) -> p u h d", d=HD),
                    pri.ap().unsqueeze(3).broadcast_to([P, NU, NH, HD]), ALU.mult), "o")
        flip(o, banks[0], "oflip", [("o", 0)], [("y_t", 0)])
        W("act", "oflip")
        W("act", "x1_ps", back=1)
        M("act", A.activation(o_t.ap(), two(banks[0]), ACT.Copy), "o_t")
        W("pe", "o_t")
        W("pe", "exp", NH - 1)
        for mt in range(KT):
            for kt in range(KT):
                m = E.matmul(SB[0][:, mt * N:(mt + 1) * N], w_proj[:, kt, T(mt)], o_t[:, kt, :],
                             start=kt == 0, stop=kt == KT - 1)
        M("pe", m, "x1_ps")
        W("dve", "x1_ps")
        W("dve", "x_t")
        W("dve", "kx_ps", back=1)
        W("dve", "resid", back=1)
        for mt in range(KT):
            m = V.scalar_tensor_tensor(out=x1[:, mt, :], in0=SB[0][:, mt * N:(mt + 1) * N],
                                       scalar=fcols[:, 12 + mt:13 + mt], in1=x_t[:, mt, :],
                                       op0=ALU.add, op1=ALU.add)
        M("dve", m, "x1")
        W("act", "x1")
        M("act", A.activation(resid[:, bass.ds(b, 1), :].rearrange("p o n -> p (o n)"),
                              x1.ap().rearrange("p a n -> p (a n)"), ACT.Copy), "resid")
        W("dve", "w_m", back=1)
        dve(V.tensor_copy(stc[:, :], style[:, :, bass.ds(b, 1)].rearrange("p a o -> p (a o)")), "stc")
        dve(VT(stc2[:, :], stc[:, :], stc[:, :], ALU.mult), "stc2")
        W("dve", "dem_ps", back=1)
        for c in range(4):
            m = TS(stw[:, c, :], ones[:, :], stc2[:, c:c + 1], None, ALU.mult)
        M("dve", m, "stw")
        W("pe", "stw")
        W("pe", "exp", NH - 1)
        for m2, w2 in enumerate((k_sq, o_sq)):
            for kt in range(KT):
                m = E.matmul(SB[1][:, m2 * D:(m2 + 1) * D], stw[:, 2 * m2 + kt, :], w2[:, kt, :],
                             start=kt == 0, stop=kt == KT - 1)
        M("pe", m, "dem_ps")
        W("act", "dem_ps")
        W("act", "demr", back=1)
        M("act", A.activation(dem.ap(), two(SB[1]), ACT.Sqrt, bias=eps_mod[:, :]), "dem")
        W("dve", "dem")
        dve(V.reciprocal(demr.ap(), dem.ap()), "demr")
        W("dve", "x2_ps", back=1)
        for m2, w in enumerate((k_w, o_w)):
            for kt in range(KT):
                m = V.scalar_tensor_tensor(out=w_m[:, m2, kt, :], in0=demr[:, m2, :],
                                           scalar=stc[:, 2 * m2 + kt:2 * m2 + kt + 1], in1=w[:, kt, :],
                                           op0=ALU.mult, op1=ALU.mult)
        M("dve", m, "w_m")
        W("pe", "w_m")
        W("pe", "x1")
        W("pe", "prt", NH - 2)
        for u in range(NU):
            for kt in range(KT):
                m = E.matmul(PB[0][:, u * D:(u + 1) * D], x1[:, kt, T(u)], w_m[:, 0, kt, :],
                             start=kt == 0, stop=kt == KT - 1)
        M("pe", m, "kx_ps")
        W("dve", "kx_ps")
        dve(VT(kx.ap(), two(PB[0]), row(4), ALU.add), "kx")
        W("dve", "o2flip", back=1)
        for u in range(NU):
            kh = kx[:, u, :].rearrange("p (h d) -> p h d", d=HD)
            dve(VT(prod.ap(), kh.unsqueeze(2).broadcast_to([P, NH, NH, HD]),
                   kh.unsqueeze(1).broadcast_to([P, NH, NH, HD]), ALU.mult), "hp", u)
            dve(V.tensor_reduce(sc.ap(), prod.ap(), AX.X, ALU.add), "hs", u)
            dve(V.tensor_reduce(scm[:, :], sc.ap(), AX.X, ALU.max), "hm", u)
            dve(VT(sc.ap(), sc.ap(), scm[:, :].unsqueeze(2).broadcast_to([P, NH, NH]), ALU.subtract), "hd", u)
            W("act", "hd", u)
            M("act", A.activation(sc.ap(), sc.ap(), ACT.Exp, scale=float(HD) ** -0.5), "he", u)
            W("dve", "he", u)
            dve(V.tensor_reduce(scs[:, :], sc.ap(), AX.X, ALU.add), "hsum", u)
            dve(V.reciprocal(scr[:, :], scs[:, :]), "hrec", u)
            dve(VT(sc.ap(), sc.ap(), scr[:, :].unsqueeze(2).broadcast_to([P, NH, NH]), ALU.mult), "hw", u)
            kd = kx[:, u, :].rearrange("p (j d) -> p d j", d=HD)
            dve(VT(prod.ap(), sc.ap().unsqueeze(2).broadcast_to([P, NH, HD, NH]),
                   kd.unsqueeze(1).broadcast_to([P, NH, HD, NH]), ALU.mult), "hq", u)
            dve(V.tensor_reduce(o2[:, u, :].rearrange("p (h d) -> p h d", d=HD), prod.ap(), AX.X, ALU.add),
                "ho", u)
        flip(o2, PB[1], "o2flip", [("ho", NU - 1, 0)], [("prt", NH - 1, 0)])
        W("act", "o2flip")
        W("act", "x2_ps", back=1)
        M("act", A.activation(o2_t.ap(), two(PB[1]), ACT.Copy), "o2_t")
        W("pe", "o2_t")
        W("pe", "o")
        for mt in range(KT):
            for kt in range(KT):
                m = E.matmul(banks[7][:, mt * N:(mt + 1) * N], w_m[:, 1, kt, T(mt)], o2_t[:, kt, :],
                             start=kt == 0, stop=kt == KT - 1)
        M("pe", m, "x2_ps")
        W("act", "x2_ps")
        for mt in range(KT):
            m = A.activation(state[:, bass.ds(b, 1), mt * PAD + 1:(mt + 1) * PAD].rearrange("p o n -> p (o n)"),
                             banks[7][:, mt * N:(mt + 1) * N], ACT.Identity, bias=fcols[:, 14 + mt:15 + mt])
        M("act", m, "ostate")
        body.end()
    nc.all_engine_barrier()


def write_out(nc, ctx, counts, out, ident, state, resid):
    def sb(name, shape, dt=F32):
        return ctx.enter_context(nc.sbuf_tensor(name, shape, dt))

    total = sb("total", [P, 2, KT, N])
    rows_out = sb("rows_out", [P, 2, NU, D])
    bank = [ctx.enter_context(nc.psum_tensor(f"out_bank{k}", [P, 512], F32)) for k in range(2)]
    dma_o = [ctx.enter_context(nc.semaphore(f"dma_o{k}")) for k in range(2)]
    last = Stretch(nc, ctx, "write_out", counts, 0)
    last.begin()
    for b in range(B):
        s = b % 2
        if b >= 2:
            last.wait("dve", "flip", b - 2)
        last.mark("dve", nc.vector.tensor_tensor(
            total[:, s, :, :], resid[:, b, :].rearrange("p (k n) -> p k n", k=KT),
            state[:, b, :].rearrange("p (k n) -> p k n", k=KT)[:, :, 1:PAD], ALU.add), "total", b)
        last.wait("pe", "total", b)
        if b >= 2:
            last.wait("pe", "rows", b - 2)
        for u in range(NU):
            for kt in range(KT):
                m = nc.tensor.transpose(bank[s][:, u * D + kt * P:][:, 0:P], total[:, s, kt, u * P:(u + 1) * P],
                                        ident[:, :])
        last.mark("pe", m, "flip", b)
        last.wait("act", "flip", b)
        if b >= 2:
            nc.scalar.wait_ge(dma_o[s], 16 * (b // 2))
        last.mark("act", nc.scalar.activation(rows_out[:, s, :, :].rearrange("p u d -> p (u d)"), bank[s][:, :],
                                              ACT.Copy), "rows", b)
        last.wait("sp", "rows", b)
        nc.sync.dma_start(out[b:b + 1, :, :].rearrange("o (u p) d -> p (o u) d", p=P), rows_out[:, s, :, :]
                          ).then_inc(dma_o[s], 16)
    for s in range(2):
        nc.sync.wait_ge(dma_o[s], 16 * (B // 2))
    last.end()
DEPTH, HEADS, DH, WIN = 6, 16, 64, 64
INNER = HEADS * DH
DI = int(D * 4 * 2 / 3)
NJ = -(-DI // P)
GH = 4
NG = HEADS // GH
UNITS = NG * NU
GC = GH * DH
PAD = N + 1
VR = 6
QK_SCALE = 8.0
NCOL = 2 * KT + 2 * NJ + KT


def local_layers(nc, ctx, counts, io, state, ident, eps_ln):
    def sb(name, shape, dt=F32):
        return ctx.enter_context(nc.sbuf_tensor(name, shape, dt))

    w_qkv = [sb(f"w_qkv{k}", [P, KT, NG, 3 * GC]) for k in range(2)]
    w_o = [sb(f"w_o{k}", [P, INNER // P, D]) for k in range(2)]
    w_1 = [sb(f"w_1{k}", [P, KT, 2 * DI]) for k in range(2)]
    w_2 = [sb(f"w_2{k}", [P, NJ, D]) for k in range(2)]
    cols = [sb(f"cols{k}", [P, NCOL]) for k in range(2)]
    qk_gain = [sb(f"qk_gain{k}", [P, 2, DH]) for k in range(2)]
    rot_cos, rot_sin = sb("rot_cos", [P, NU, 2, DH]), sb("rot_sin", [P, NU, 2, DH])
    cos_t, sin_t = sb("cos_t", [P, NU, 2, DH]), sb("sin_t", [P, NU, 2, DH])
    band = sb("band", [P, NU, P], BF16)
    ident_bf = sb("ident_bf", [P, P], BF16)
    mean_w = sb("mean_w", [P, P])
    half = sb("half", [P, 2 * GH])

    xa = sb("xa", [P, KT * PAD])
    sq = sb("sq", [P, 2, 2 * GC])
    norm2 = sb("norm2", [P, 2, 2 * GH])
    rnorm = sb("rnorm", [P, 2, 2 * GH])
    by_cos, by_sin = sb("by_cos", [P, 2, 2 * GC]), sb("by_sin", [P, 2, 2 * GC])
    turned = sb("turned", [P, 2, 2 * GC])
    qk_t = sb("qk_t", [P, 4, 4, P])
    v_tok = sb("v_tok", [P, VR, GC])
    v_shift = sb("v_shift", [P, NG, GC])
    negmax = sb("negmax", [P, 2, GH])
    escale, ebias = sb("escale", [P, 2, GH]), sb("ebias", [P, 2, GH])
    prob = sb("prob", [P, 2, GH, P])
    rsum, rinv = sb("rsum", [P, 2, GH]), sb("rinv", [P, 2, GH])
    prob_t = sb("prob_t", [P, 2, GH, P])
    attn_t = sb("attn_t", [P, INNER // P, N])
    x1 = sb("x1", [P, KT * PAD])
    cent, cent2 = sb("cent", [P, KT, N]), sb("cent2", [P, KT, N])
    sdev = sb("sdev", [P, N])
    lin_in = sb("lin_in", [P, KT, N])
    gate = sb("gate", [P, 2, N])
    hidden = sb("hidden", [P, NJ, N])

    def ps(name):
        return ctx.enter_context(nc.psum_tensor(name, [P, 512], F32))

    ps_qk = [ps("ps_qk0"), ps("ps_qk1")]
    ps_v = ps("ps_v")
    ps_t = ps("ps_t")
    ps_s = [ps("ps_s0"), ps("ps_s1")]
    ps_f = [ps("ps_f0"), ps("ps_f1")]

    dma_w = [ctx.enter_context(nc.semaphore(f"dma_w{k}")) for k in range(2)]
    dma_c = ctx.enter_context(nc.semaphore("dma_c"))
    ready = Stretch(nc, ctx, "layer_setup", counts, 0)
    sec = Stretch(nc, ctx, "layer", counts, DEPTH)
    attn = Stretch(nc, ctx, "attn", counts, DEPTH * B)
    ffn = Stretch(nc, ctx, "ffn", counts, DEPTH * B)

    W_DMAS = 6

    def load_layer(k, layer):
        one = bass.ds(layer, 1)
        for dst, src in ((w_qkv[k], io["w_qkv"]), (w_o[k], io["w_o"]), (w_1[k], io["w_1"]),
                         (w_2[k], io["w_2"]), (cols[k], io["cols"])):
            shape = dst.shape
            flat = dst[:, :] if len(shape) == 2 else dst.ap().rearrange(
                "p a b -> p (a b)" if len(shape) == 3 else "p a b c -> p (a b c)")
            nc.sync.dma_start(flat, src[one, :, :].rearrange("l p n -> (l p) n")).then_inc(dma_w[k], 16)
        nc.sync.dma_start(qk_gain[k].ap().rearrange("p a b -> p (a b)"),
                          io["qk_gain"][one, :].broadcast_to([P, 2 * DH])).then_inc(dma_w[k], 16)

    ready.begin()
    for dst, src in ((rot_cos, io["rot_cos"]), (rot_sin, io["rot_sin"])):
        nc.sync.dma_start(dst.ap().rearrange("p a b c -> p (a b c)"), src).then_inc(dma_c, 16)
    nc.sync.dma_start(band.ap().rearrange("p a b -> p (a b)"), io["band"]).then_inc(dma_c, 16)
    nc.sync.wait_ge(dma_c, 48)
    load_layer(0, 0)
    load_layer(1, 1)
    ready.mark("pool", nc.gpsimd.memset(mean_w[:, :], 1.0 / D), "mean_w")
    ready.mark("pool", nc.gpsimd.memset(half[:, :], -0.5), "half")
    ready.mark("pool", nc.gpsimd.memset(x1[:, :], 0.0), "x1_zero")
    ready.mark("pool", nc.gpsimd.memset(xa[:, :], 0.0), "xa_zero")
    ready.mark("dve", nc.vector.tensor_copy(ident_bf[:, :], ident[:, :]), "ident_bf")
    ready.end()
    nc.all_engine_barrier()

    def U(u):
        return slice(u * P, (u + 1) * P)

    def heads(ap, n=2 * GH):
        return ap.rearrange("p (h t d) -> p h t d", t=2, d=DH // 2)

    def project(i, k):
        g, u = divmod(i, NU)
        attn.wait_unit("pe", "qk_square", i - 2, UNITS)
        attn.wait_unit("pe", "qk_by_sin", i - 2, UNITS)
        for kt in range(KT):
            lhs = xa[:, (1 if kt == 0 else PAD) + u * P:][:, 0:P]
            m = nc.tensor.matmul(ps_qk[i % 2][:, :], lhs, w_qkv[k][:, kt, g, 0:2 * GC],
                                 start=kt == 0, stop=kt == KT - 1)
        attn.mark("pe", m, "qk", i)
        attn.wait_unit("pe", "v_copied", i - 1, UNITS)
        attn.wait_unit("pe", "attn_t", max(i - 5, -1), UNITS)
        for kt in range(KT):
            lhs = xa[:, (1 if kt == 0 else PAD) + u * P:][:, 0:P]
            m = nc.tensor.matmul(ps_v[:, 0:GC], lhs, w_qkv[k][:, kt, g, 2 * GC:3 * GC],
                                 start=kt == 0, stop=kt == KT - 1)
        attn.mark("pe", m, "v", i)
        s, qk = i % 2, ps_qk[i % 2]
        attn.wait("act", "qk", i)
        attn.wait_unit("act", "norm2", i - 2, UNITS)
        attn.mark("act", nc.scalar.activation(sq[:, s, :], qk[:, :], ACT.Square), "qk_square", i)
        attn.wait("act", "v", i)
        attn.wait_unit("act", "attn", i - VR, UNITS)
        m = nc.scalar.activation(v_tok[:, i % VR, :], ps_v[:, 0:GC], ACT.Copy)
        if u == 0:
            attn.wait_unit("act", "attn", i + 1 - UNITS, UNITS)
            m = nc.scalar.activation(v_shift[WIN:P, g, :], ps_v[WIN:P, 0:GC], ACT.Copy)
        else:
            m = nc.scalar.activation(v_shift[0:WIN, g, :], ps_v[0:WIN, 0:GC], ACT.Copy)
        attn.mark("act", m, "v_copied", i)

    def rotate(i):
        u, s = i % NU, i % 2
        qk = ps_qk[s]
        attn.wait("dve", "qk_square", i)
        attn.wait_unit("dve", "turned", i - 2, UNITS)
        shape = [P, 2, GH, DH]
        cs = cos_t[:, u, :, :].unsqueeze(2).broadcast_to(shape)
        attn.mark("dve", nc.vector.tensor_tensor(
            by_cos[:, s, :].rearrange("p (a h d) -> p a h d", a=2, h=GH),
            qk[:, :].rearrange("p (a h d) -> p a h d", a=2, h=GH), cs, ALU.mult), "qk_by_cos", i)
        for a in range(2):
            sn = sin_t[:, u, a, :].rearrange("p (t d) -> p t d", t=2).unsqueeze(1)
            cut = slice(a * GC, (a + 1) * GC)
            m = nc.vector.tensor_tensor(heads(by_sin[:, s, cut]), heads(qk[:, cut])[:, :, ::-1, :],
                                        sn.broadcast_to([P, GH, 2, DH // 2]), ALU.mult)
        attn.mark("dve", m, "qk_by_sin", i)
        attn.wait("dve", "qk_square", i)
        attn.wait_unit("dve", "rnorm", i - 2, UNITS)
        attn.mark("dve", nc.vector.tensor_reduce(norm2[:, s, :], sq[:, s, :].rearrange(
            "p (h d) -> p h d", d=DH), AX.X, ALU.add), "norm2", i)
        attn.wait("dve", "norm2", i)
        attn.mark("dve", nc.vector.tensor_scalar(norm2[:, s, :], norm2[:, s, :], 1e-24, None, ALU.max),
                  "norm2_floor", i)

        attn.wait("pool", "norm2_floor", i)
        attn.wait_unit("pool", "ebias", i - 2, UNITS)
        attn.mark("pool", nc.gpsimd.tensor_tensor(rnorm[:, s, :], norm2[:, s, :], half[:, :], ALU.pow),
                  "rnorm", i)
        attn.wait("pool", "qk_by_sin", i)
        attn.wait_unit("pool", "turned_t", i - 2, UNITS)
        m = nc.gpsimd.tensor_tensor(turned[:, s, :], by_cos[:, s, :], by_sin[:, s, :], ALU.add)
        attn.mark("pool", m, "turned", i)
        attn.wait("pool", "turned", i)
        kk = turned[:, s, GC:].rearrange("p (h d) -> p h d", d=DH)
        m = nc.gpsimd.tensor_tensor(kk, kk, rnorm[:, s, GH:].unsqueeze(2).broadcast_to([P, GH, DH]), ALU.mult)
        attn.mark("pool", m, "k_unit", i)

    def flip_qk(i):
        attn.wait("pe", "k_unit", i)
        attn.wait_unit("pe", "qk_t", i - 1, UNITS)
        attn.wait_unit("pe", "prob_t", max(i - 2, -1), UNITS)
        for c in range(4):
            m = nc.tensor.transpose(ps_t[:, U(c)], turned[:, i % 2, U(c)], ident[:, :])
        attn.mark("pe", m, "turned_t", i)
        attn.wait("act", "turned_t", i)
        attn.wait_unit("act", "scores", i - 3, UNITS)
        attn.mark("act", nc.scalar.activation(qk_t[:, i % 4, :, :].rearrange("p a b -> p (a b)"),
                                              ps_t[:, :], ACT.Copy), "qk_t", i)

    def half_bank(odd, i):
        return ps_s[odd][:, 0:2 * P]

    def score(i):
        u, s = i % NU, i % 2
        attn.wait("pe", "qk_t", i)
        attn.wait_unit("pe", "prob", i - 1, UNITS)
        for odd in range(2):
            nc.tensor.matmul(half_bank(odd, i).rearrange("p (h k) -> p h k", h=2), ident_bf[:, :],
                             band[:, u, :].unsqueeze(1).broadcast_to([P, 2, P]), start=True, stop=False,
                             skip_group_check=True)
        for h in range(GH):
            r, c = slice(DH * (h % 2), DH * (h % 2) + DH), h // 2
            q, kk, before = qk_t[r, i % 4, c, :], qk_t[r, i % 4, 2 + c, :], qk_t[r, (i - 1) % 4, 2 + c, :]
            o = half_bank(h % 2, i)[:, U(h // 2)]
            m = nc.tensor.matmul(o[:, 0:WIN], q, kk[:, 0:WIN], start=False, stop=True, skip_group_check=True)
            m = nc.tensor.matmul(o[WIN:P, WIN:P], q[:, WIN:P], kk[:, WIN:P], start=False, stop=True,
                                 skip_group_check=True)
            if u:
                m = nc.tensor.matmul(o[0:WIN, WIN:P], q[:, 0:WIN], before[:, WIN:P], start=False, stop=True,
                                     skip_group_check=True)
        attn.mark("pe", m, "scores", i)

    def soften(i):
        s = i % 2
        attn.wait("dve", "scores", i)
        attn.wait_unit("dve", "ebias", i - 2, UNITS)
        for odd in range(2):
            m = nc.vector.tensor_reduce(negmax[:, s, odd::2], half_bank(odd, i).rearrange(
                "p (h k) -> p h k", h=2), AX.X, ALU.max, negate=True)
        attn.mark("dve", m, "negmax", i)
        attn.wait("dve", "rnorm", i)
        attn.wait_unit("dve", "prob", i - 2, UNITS)
        attn.mark("dve", nc.vector.tensor_scalar(escale[:, s, :], rnorm[:, s, 0:GH], QK_SCALE, None, ALU.mult),
                  "escale", i)
        attn.wait("dve", "escale", i)
        attn.wait("dve", "negmax", i)
        attn.mark("dve", nc.vector.tensor_tensor(ebias[:, s, :], negmax[:, s, :], escale[:, s, :], ALU.mult),
                  "ebias", i)
        attn.wait("act", "ebias", i)
        attn.wait_unit("act", "prob_t_ps", i - 2, UNITS)
        attn.wait_unit("act", "rinv", i - 2, UNITS)
        for h in range(GH):
            m = nc.scalar.activation(prob[:, s, h, :], half_bank(h % 2, i)[:, U(h // 2)], ACT.Exp, bias=ebias[:, s, h:h + 1],
                                     scale=escale[:, s, h:h + 1], accum_out=rsum[:, s, h:h + 1])
        attn.mark("act", m, "prob", i)

    def weigh(i):
        s = i % 2
        attn.wait("dve", "prob", i)
        attn.wait_unit("dve", "prob_unit", i - 2, UNITS)
        attn.mark("dve", nc.vector.reciprocal(rinv[:, s, :], rsum[:, s, :]), "rinv", i)
        attn.wait("dve", "rinv", i)
        for h in range(GH):
            m = nc.vector.tensor_scalar(prob[:, s, h, :], prob[:, s, h, :], rinv[:, s, h:h + 1], None, ALU.mult)
        attn.mark("dve", m, "prob_unit", i)

    def flip_prob(i):
        attn.wait("pe", "prob_unit", i)
        attn.wait_unit("pe", "prob_t", i - 1, UNITS)
        attn.wait_unit("pe", "qk_t", min(i + 1, UNITS - 1), UNITS)
        for h in range(GH):
            m = nc.tensor.transpose(ps_t[:, U(h)], prob[:, i % 2, h, :], ident[:, :])
        attn.mark("pe", m, "prob_t_ps", i)
        attn.wait("dve", "prob_t_ps", i)
        attn.wait_unit("dve", "attn", i - 2, UNITS)
        attn.mark("dve", nc.vector.tensor_copy(prob_t[:, i % 2, :, :].rearrange("p a b -> p (a b)"),
                                               ps_t[:, :]), "prob_t", i)

    def attend(i):
        g, u = divmod(i, NU)
        attn.wait("pe", "prob_t", i)
        attn.wait("pe", "v_copied", min(i + 4, UNITS - 1))
        attn.wait_unit("pe", "attn_t", i - 1, UNITS)
        for h in range(GH):
            out = ps_v[DH * (h % 2):DH * (h % 2) + DH, P * (h // 2):P * (h // 2) + P]
            vh = slice(h * DH, (h + 1) * DH)
            pt = prob_t[:, i % 2, h, :]
            if u == 0:
                m = nc.tensor.matmul(out, v_tok[:, i % VR, vh], pt, start=True, stop=True)
            else:
                m = nc.tensor.matmul(out[:, 0:WIN], v_shift[:, g, vh], pt[:, 0:WIN], start=True, stop=True)
                m = nc.tensor.matmul(out[:, WIN:P], v_tok[:, i % VR, vh], pt[:, WIN:P], start=True, stop=True)
        attn.mark("pe", m, "attn", i)
        attn.wait("act", "attn", i)
        if i == 0:
            ffn.wait("act", "w_o")
        attn.mark("act", nc.scalar.activation(
            attn_t[:, 2 * g:2 * g + 2, U(u)], ps_v[:, 0:GC].rearrange("p (a b) -> p a b", a=2), ACT.Copy),
            "attn_t", i)

    def feed_forward(k, b):
        c = cols[k]
        gain, shift = c[:, 0:KT], c[:, KT:2 * KT]
        b_a, b_g = c[:, 2 * KT:2 * KT + NJ], c[:, 2 * KT + NJ:2 * KT + 2 * NJ]
        b_2 = c[:, 2 * KT + 2 * NJ:]
        whole = lambda t: t[:, :].rearrange("p (k n) -> p k n", k=KT)[:, :, 1:PAD]
        shifted = lambda t: t[:, 1:1 + KT * N].rearrange("p (k n) -> p k n", k=KT)
        mine = state[:, bass.ds(b, 1), :].rearrange("p o n -> p (o n)")

        attn.wait("pe", "attn_t", UNITS - 1, back=1)
        ffn.wait("pe", "state", back=1)
        for mt in range(KT):
            for j in range(INNER // P):
                m = nc.tensor.matmul(ps_f[0][:, mt * N:(mt + 1) * N], w_o[k][:, j, U(mt)], attn_t[:, j, :],
                                     start=j == 0, stop=j == INNER // P - 1)
        ffn.mark("pe", m, "w_o")
        ffn.wait("dve", "w_o")
        ffn.wait("dve", "mean", back=1)
        ffn.wait("dve", "state", back=1)
        ffn.mark("dve", nc.vector.tensor_tensor(whole(x1), ps_f[0][:, :].rearrange("p (k n) -> p k n", k=KT),
                                                whole(mine), ALU.add), "x1")
        yield
        ffn.wait("pe", "x1")
        ffn.wait("pe", "gated", NJ - 1, back=1)
        for kt in range(KT):
            m = nc.tensor.matmul(ps_f[1][:, 0:N], mean_w[:, :], shifted(x1)[:, kt, :],
                                 start=kt == 0, stop=kt == KT - 1)
        ffn.mark("pe", m, "mean")
        ffn.wait("dve", "mean")
        ffn.wait("dve", "cent2", back=1)
        ffn.mark("dve", nc.vector.tensor_tensor(cent[:, :, :], shifted(x1),
                                                ps_f[1][:, 0:N].unsqueeze(1).broadcast_to([P, KT, N]),
                                                ALU.subtract), "cent")
        ffn.wait("act", "cent")
        ffn.wait("act", "var", back=1)
        ffn.mark("act", nc.scalar.activation(cent2[:, :, :], cent[:, :, :], ACT.Square), "cent2")
        yield
        ffn.wait("pe", "cent2")
        for kt in range(KT):
            m = nc.tensor.matmul(ps_f[1][:, N:2 * N], mean_w[:, :], cent2[:, kt, :],
                                 start=kt == 0, stop=kt == KT - 1)
        ffn.mark("pe", m, "var")
        ffn.wait("act", "var")
        ffn.wait("act", "normed", back=1)
        ffn.mark("act", nc.scalar.activation(sdev[:, :], ps_f[1][:, N:2 * N], ACT.Sqrt, bias=eps_ln[:, :]),
                 "sdev")
        ffn.wait("dve", "sdev")
        ffn.mark("dve", nc.vector.reciprocal(sdev[:, :], sdev[:, :]), "rdev")
        ffn.wait("dve", "rdev")
        ffn.mark("dve", nc.vector.tensor_tensor(cent[:, :, :], cent[:, :, :],
                                                sdev[:, :].unsqueeze(1).broadcast_to([P, KT, N]), ALU.mult),
                 "normed")
        ffn.wait("dve", "normed")
        ffn.wait("dve", "hid", NJ - 1, back=1)
        for kt in range(KT):
            m = nc.vector.tensor_scalar(lin_in[:, kt, :], cent[:, kt, :], gain[:, kt:kt + 1],
                                        shift[:, kt:kt + 1], ALU.mult, ALU.add)
        ffn.mark("dve", m, "lin_in")
        yield
        for j0 in range(0, NJ, 2):
            for j in (j0, j0 + 1):
                w = min(P, DI - j * P)
                f = ps_f[j % 2]
                ffn.wait("pe", "lin_in")
                if j >= 2:
                    ffn.wait("pe", "gated", j - 2)
                for half, first in enumerate((j * P, DI + j * P)):
                    for kt in range(KT):
                        m = nc.tensor.matmul(f[0:w, half * N:(half + 1) * N], w_1[k][:, kt, first:first + w],
                                             lin_in[:, kt, :], start=kt == 0, stop=kt == KT - 1)
                ffn.mark("pe", m, "hid", j)
            for j in (j0, j0 + 1):
                w = min(P, DI - j * P)
                ffn.wait("act", "hid", j)
                if j >= 2:
                    ffn.wait("act", "gated", j - 2)
                else:
                    ffn.wait("act", "gated", j + NJ - 2, back=1)
                ffn.mark("act", nc.scalar.activation(gate[0:w, j % 2, :], ps_f[j % 2][0:w, N:2 * N], ACT.Gelu,
                                                     bias=b_g[0:w, j:j + 1]), "gate", j)
            for j in (j0, j0 + 1):
                w = min(P, DI - j * P)
                ffn.wait("dve", "gate", j)
                if j == 0:
                    ffn.wait("dve", "out", back=1)
                ffn.mark("dve", nc.vector.scalar_tensor_tensor(
                    out=hidden[0:w, j, :], in0=ps_f[j % 2][0:w, 0:N], scalar=b_a[0:w, j:j + 1],
                    in1=gate[0:w, j % 2, :], op0=ALU.add, op1=ALU.mult), "gated", j)
            yield
        ffn.wait("pe", "gated", NJ - 1)
        for mt in range(KT):
            for j in range(NJ):
                w = min(P, DI - j * P)
                m = nc.tensor.matmul(ps_f[0][:, mt * N:(mt + 1) * N], w_2[k][0:w, j, U(mt)], hidden[0:w, j, :],
                                     start=j == 0, stop=j == NJ - 1)
        ffn.mark("pe", m, "out")
        ffn.wait("dve", "out")
        for mt in range(KT):
            m = nc.vector.scalar_tensor_tensor(
                out=mine[:, mt * PAD + 1:(mt + 1) * PAD],
                in0=ps_f[0][:, mt * N:(mt + 1) * N], scalar=b_2[:, mt:mt + 1],
                in1=whole(x1)[:, mt, :], op0=ALU.add, op1=ALU.add)
        ffn.mark("dve", m, "state")
        yield

    FF_STEPS = (0, 1, 2, 4, 7, 9, 11)

    def attention(k, b):
        attn.wait("pool", "v", UNITS - 1, back=1)
        ffn.wait("pool", "state", back=1)
        attn.carry("pool")
        attn.mark("pool", nc.gpsimd.tensor_copy(
            xa[:, :], state[:, bass.ds(b, 1), :].rearrange("p o n -> p (o n)")), "xa")
        attn.wait("pe", "xa")
        stages = ((attend, 5), (flip_prob, 4), (score, 3), (soften, 3), (rotate, 1), (weigh, 3), (flip_qk, 2),
                  (lambda i: project(i, k), 0))
        for t in range(UNITS + 5):
            for stage, lag in stages:
                if 0 <= t - lag < UNITS:
                    stage(t - lag)
            yield t

    def tables(k, count):
        for lane in ("pe", "act", "dve"):
            sec.eng[lane].wait_ge(dma_w[k], count * (16 * W_DMAS))
            sec.carry(lane)
        attn.wait("dve", "qk_by_sin", UNITS - 1, back=1)
        gb = qk_gain[k].ap().unsqueeze(1).broadcast_to([P, NU, 2, DH])
        m = nc.vector.tensor_tensor(cos_t.ap(), rot_cos.ap(), gb, ALU.mult)
        for a in range(2):
            turn = qk_gain[k][:, a, :].rearrange("p (t d) -> p t d", t=2)[:, ::-1, :]
            m = nc.vector.tensor_tensor(
                sin_t[:, :, a, :].rearrange("p u (t d) -> p u t d", t=2),
                rot_sin[:, :, a, :].rearrange("p u (t d) -> p u t d", t=2),
                turn.unsqueeze(1).broadcast_to([P, NU, 2, DH // 2]), ALU.mult)
        sec.mark("dve", m, "tables")
        sec.wait("dve", "tables")
        sec.carry("dve")

    def both(step, k, b, k_next, b_next, weights=None):
        attn.begin(step + 1)
        ffn.begin(step)
        if weights is not None:
            sec.begin(weights[0])
            tables(k_next, weights[1])
            sec.end()
        parts = feed_forward(k, b)
        for t in attention(k_next, b_next):
            if t in FF_STEPS:
                next(parts)
        attn.end()
        ffn.end()

    attn.begin(0)
    ffn.begin(-1)
    sec.begin(0)
    tables(0, 1)
    sec.end()
    for _ in attention(0, 0):
        pass
    attn.end()

    def layer_pair(pair, final):
        for k in range(2):
            first = pair * (2 * B) + k * B
            with nc.Fori(0, B - 1) as b:
                both(first + b, k, b, k, b + 1)
            if final and k == 1:
                attn.begin(first + B)
                ffn.begin(first + B - 1)
                for _ in feed_forward(k, B - 1):
                    pass
                ffn.end()
                return
            both(first + (B - 1), k, B - 1, 1 - k, 0, (pair * 2 + (k + 1), pair + (k + 1)))
            if not final:
                for lane in ("pe", "act", "dve"):
                    for part, done in ((attn, first + (B + 1)), (ffn, first + B)):
                        nc.sync.wait_ge(part.sem[lane], (done) * part.per[lane] + part.per[lane])
                sec.carry("sp")
                load_layer(k, pair * 2 + (k + 2))

    with nc.Fori(0, DEPTH // 2 - 1) as pair:
        layer_pair(pair, False)
    layer_pair(DEPTH // 2 - 1, True)
    nc.all_engine_barrier()
def build(nc, io, out, counts):
    made = {}
    ctx = ExitStack()
    with ctx:
        state = ctx.enter_context(nc.sbuf_tensor("state", [P, B, KT * PAD], F32))
        resid = ctx.enter_context(nc.sbuf_tensor("resid", [P, B, KT * N], F32))
        ident = ctx.enter_context(nc.sbuf_tensor("ident", [P, P], F32))
        eps_ln = ctx.enter_context(nc.sbuf_tensor("eps_ln", [P, 1], F32))
        begun = ctx.enter_context(nc.semaphore("begun"))
        nc.gpsimd.memset(ident[:, :], 0.0).then_inc(begun, 1)
        nc.gpsimd.memset(eps_ln[:, :], 1e-5).then_inc(begun, 1)
        nc.gpsimd.memset(state[:, :, :], 0.0).then_inc(begun, 1)
        nc.gpsimd.wait_ge(begun, 3)
        nc.gpsimd.affine_select(out=ident[:, :], in_=ident[:, :], compare_op=ALU.not_equal, fill=1.0, base=0,
                                pattern=[[-1, P]], channel_multiplier=1).then_inc(begun, 1)
        nc.gpsimd.wait_ge(begun, 4)
        nc.all_engine_barrier()
        Stretch.made = made
        with ExitStack() as part:
            conditioned_blocks(nc, part, counts, io, ident, eps_ln, state, resid)
        with ExitStack() as part:
            local_layers(nc, part, counts, io, state, ident, eps_ln)
        with ExitStack() as part:
            write_out(nc, part, counts, out, ident, state, resid)
    return made


def shape_tables():
    half = np.arange(0, DH, 2, dtype=np.float64)
    t = np.arange(N, dtype=np.float64)[:, None]
    freqs = t * (1.0 / 10000.0 ** (half / DH))[None, :]
    scale = ((half + 0.4 * DH) / (1.4 * DH))[None, :] ** ((t - N // 2) / (WIN // 2))
    cos, sin = np.cos(freqs), np.sin(freqs)
    c = np.stack([np.concatenate([cos * s, cos * s], 1) for s in (scale, 1 / scale)], 1)
    s = np.stack([np.concatenate([-sin * s, sin * s], 1) for s in (scale, 1 / scale)], 1)
    tile = lambda a: np.ascontiguousarray(a.reshape(NU, P, 2, DH).transpose(1, 0, 2, 3).reshape(P, -1),
                                          dtype=np.float32)
    r, j = np.arange(P)[:, None], np.arange(P)[None, :]
    odd, upper = r >= WIN, j >= WIN
    i, jj = r % WIN, j % WIN
    valid = np.where(odd == upper, jj <= i, jj >= i)
    first = valid & ~(~odd & upper)
    band = np.where(np.concatenate([first, valid], 1), 0.0, -1e30)
    return tile(c), tile(s), band


def lay_out(a):
    cc = np.ascontiguousarray
    rowtile = lambda w: cc(w.reshape(-1, P, w.shape[-1]).transpose(1, 0, 2).reshape(P, -1))
    col = lambda v: v.reshape(-1, P).T

    def slotted(w):
        z = np.zeros((w.shape[0], NH, SLOT), w.dtype)
        z[:, :, :HD] = w.reshape(w.shape[0], NH, HD)
        return z.reshape(w.shape[0], NH * SLOT)

    c, f = "L0_cond_", "L0_ffn_"
    x = {"x": a["x"]}
    ids = np.stack([a["itok_BxS_0_999"], a["itok_BxS_0_4"], a["mask_BxS_ik0"]])
    x["ids"] = cc(ids.reshape(3, B * NU, P).transpose(2, 0, 1).reshape(P, -1))
    x["t_pw"] = np.concatenate([a[c + "pw_g"], a[c + "pw_b"]], 1)
    x["t_ct"] = np.concatenate([a[c + k] for k in ("cp_g", "cp_b", "tm_g", "tm_b")], 1)
    x["t_ms"] = np.concatenate([a[c + "ms_g"], a[c + "ms_b"]], 1)
    x["w_int1"], x["w_int2"] = rowtile(a[c + "int_W1"]), rowtile(a[c + "int_W2"])
    w, bq = a["L0_attn_W_qkv"], a["L0_attn_b_qkv"][None, :]
    x["w_qk"] = rowtile(np.concatenate([slotted(w[:, 0:D]), slotted(w[:, D:2 * D])], 1))
    x["w_v"] = rowtile(w[:, 2 * D:])
    x["w_proj"] = rowtile(a["L0_attn_W_proj"])
    x["k_w"], x["o_w"] = rowtile(a["L0_cond2_k_w"].T), rowtile(a["L0_cond2_o_w"].T)
    x["aff0"], x["aff1"] = cc(a["L0_cond2_k_aff_w"].T), cc(a["L0_cond2_o_aff_w"].T)
    x["fcols"] = cc(np.concatenate(
        [col(a[c + k]) for k in ("mem_b1", "noi_b1", "res_b1", "int_b1")]
        + [col(a["L0_cond2_k_aff_b"]), col(a["L0_cond2_o_aff_b"]), col(a["L0_attn_b_proj"]), col(a["L0_cond2_o_b"])]
        + [col(slotted(bq[:, 0:D])[0]), col(slotted(bq[:, D:2 * D])[0])], 1))
    x["rows"] = np.concatenate([a[c + "int_b2"], a[c + "int_g"], a[c + "int_be"], bq[0, 2 * D:],
                                a["L0_cond2_k_b"]])[None, :]
    x["aw"] = a[c + "aw"][None, :]
    for m, (k, s) in enumerate((("mem", "cond_512"), ("noi", "cond_64"), ("res", "fside_Bx32_0"))):
        x[f"s_t{m}"] = cc(a[s].T)
        x[f"m_w1{m}"] = a[f"{c}{k}_W1"]
        x[f"m_w2{m}"] = rowtile(a[f"{c}{k}_W2"])
    x["m_rows"] = np.concatenate([a[f"{c}{k}_{q}"] for k in ("mem", "noi", "res") for q in ("b2", "g", "be")])[None, :]

    L = DEPTH
    w = a[f + "Wqkv"].reshape(L, KT, P, 3, NG, GC).transpose(0, 2, 1, 4, 3, 5)
    x["w_qkv"] = cc(w.reshape(L, P, -1))
    x["w_o"] = cc(a[f + "Wo"].reshape(L, INNER // P, P, D).transpose(0, 2, 1, 3).reshape(L, P, -1))
    x["w_1"] = cc(a[f + "W1"].reshape(L, KT, P, 2 * DI).transpose(0, 2, 1, 3).reshape(L, P, -1))
    pad = np.zeros((L, NJ * P - DI, D), np.float32)
    x["w_2"] = cc(np.concatenate([a[f + "W2"], pad], 1).reshape(L, NJ, P, D).transpose(0, 2, 1, 3).reshape(L, P, -1))
    cols3 = lambda v: v.reshape(L, -1, P).transpose(0, 2, 1)
    padded = lambda v: np.concatenate([v, np.zeros((L, NJ * P - DI), np.float32)], 1)
    b1 = a[f + "b1"]
    x["cols"] = cc(np.concatenate([cols3(a[f + "ln_g"]), cols3(a[f + "ln_b"]), cols3(padded(b1[:, :DI])),
                                   cols3(padded(b1[:, DI:])), cols3(a[f + "b2"])], 2))
    x["qk_gain"] = np.concatenate([a[f + "q_scale"], a[f + "k_scale"]], 1)
    x["rot_cos"], x["rot_sin"], x["band"] = shape_tables()
    return x


def kernel(**inputs):
    import ml_dtypes
    from concourse import bacc
    from concourse.bass_utils import run_bass_kernel_spmd

    arrays = {k: np.ascontiguousarray(v) for k, v in
              lay_out({k: np.asarray(v) for k, v in inputs.items()}).items()}
    arrays["band"] = arrays["band"].astype(ml_dtypes.bfloat16)
    counts = {}
    for _ in range(2):
        nc = bacc.Bacc("TRN2", target_bir_lowering=False, num_devices=1)
        io = {k: nc.dram_tensor(f"in_{k}", v.shape, mybir.dt.from_np(v.dtype), kind="ExternalInput").ap()
              for k, v in arrays.items()}
        out = nc.dram_tensor("out", (B, N, D), F32, kind="ExternalOutput").ap()
        counts = build(nc, io, out, counts)
    r = run_bass_kernel_spmd(nc, [{f"in_{k}": v for k, v in arrays.items()}], core_ids=[0])
    return r.results[0]["out"]
```

```python
from contextlib import ExitStack
from functools import partial

import numpy as np
import concourse.bass as bass
import concourse.mybir as mybir
from concourse.alu_op_type import AluOpType as ALU

F32 = mybir.dt.float32
BF16 = mybir.dt.bfloat16
F32R = mybir.dt.float32r
I32 = mybir.dt.int32
ACT = mybir.ActivationFunctionType
AX = mybir.AxisListType

P = 128
B, N, D = 8, 256, 256
NU = N // P
KT = D // P
LANES = ("pe", "act", "dve", "pool", "sp")
UNITS = 8
MAX_LAG = 5


class Stretch:

    def __init__(self, nc, ctx, name, counts, steps):
        self.name, self.steps, self.new = name, steps, {}
        self.old = counts.get(name, {})
        self.eng = dict(zip(LANES, (nc.tensor, nc.scalar, nc.vector, nc.gpsimd, nc.sync)))
        self.carrier = ctx.enter_context(nc.semaphore(f"{name}_carrier"))
        self.sem = {lane: ctx.enter_context(nc.semaphore(f"{name}_{lane}")) for lane in LANES}
        self.per = {lane: self.old.get(("per", lane), 1) for lane in LANES}
        self.base, self.count, self.seen = {}, {}, {}
        if steps:
            for lane in LANES:
                self.eng[lane].sem_inc(self.sem[lane], 2 * self.per[lane])

    def begin(self, step=0):
        self.step, self.base, self.seen = step, {}, {}
        self.count = {lane: 0 for lane in LANES}

    def mark(self, lane, instruction, *name):
        self.count[lane] += 1
        assert name not in self.new or self.new[name] == (lane, self.count[lane]), name
        self.new[name] = (lane, self.count[lane])
        instruction.then_inc(self.sem[lane], 1)
        return instruction

    def wait(self, lane, *name, back=0):
        maker, at = self.old.get(name, ("pe", 1))
        at -= back * self.per[maker]
        if self.old and self.seen.get((lane, maker), -10**9) >= at:
            return
        self.seen[lane, maker] = at
        if (lane, maker) not in self.base:
            before = (self.step + 2) * self.per[maker] if self.steps else 0
            self.base[lane, maker] = before if isinstance(before, int) else self.eng[lane].snap(before)
        base = self.base[lane, maker]
        if self.steps and isinstance(base, int) and base + at <= 2 * self.per[maker]:
            return
        self.eng[lane].wait_ge(self.sem[maker], self.base[lane, maker] + at)

    def carry(self, lane):
        self.eng[lane].sem_inc(self.carrier, 1)

    def piece(self, key, func, *args, run=True):
        if run or not self.old:
            had = dict(self.count)
            func(*args)
            self.new["piece", key] = {lane: self.count[lane] - had[lane] for lane in LANES}
        else:
            for lane, more in self.old["piece", key].items():
                if more:
                    self.eng[lane].wait_ge(self.sem[lane], (self.step + 2) * self.per[lane] + self.count[lane])
                    self.count[lane] += more
                    self.eng[lane].sem_inc(self.sem[lane], more)

    def stage(self, func, lag, unit, *args, run=True):
        self.lag = lag
        self.piece(func.__name__, func, unit, *args, run=run)

    def mark_unit(self, lane, instruction, name, unit):
        self.new["lag", name] = self.lag
        return self.mark(lane, instruction, name, unit % UNITS)

    def wait_unit(self, lane, name, unit):
        back = -((unit - MAX_LAG + self.old.get(("lag", name), 0)) // UNITS)
        assert not self.old or back >= 0, (name, unit)
        self.wait(lane, name, unit % UNITS, back=back)

    def mark_batch(self, lane, instruction, *name):
        self.new[("lag",) + name] = self.lag
        return self.mark(lane, instruction, *name)

    def wait_batch(self, lane, *name, back=0):
        passes = back + self.lag - self.old.get(("lag",) + name, self.lag)
        assert passes >= 0, name
        self.wait(lane, *name, back=passes)

    def end(self):
        for lane in LANES:
            self.new["per", lane] = max(self.count[lane], 1)
        Stretch.made[self.name] = self.new


NH, HD = 16, 16
NTILE = 4
SLOT = 32
INT_IN = 6
FRONT_SCHEDULE = (
    "step0 token_k fetch",
    "step1 head_scores00 flip_x",
    "step2 head_scores01",
    "step3 head_scores02",
    "step4 head_scores03 head_exp0 norm_x mix_t_s mix_h",
    "step5 head_weights0 head_out00",
    "step6 head_out01 norm_h mix_h2 flip_t flip_s",
    "step7 head_out02",
    "step8 head_out03 flip_h",
    "step9 head_scores10",
    "step10 head_scores11 mixer_hidden",
    "step11 head_scores12 mixer_silu",
    "step12 head_scores13 head_exp1 mixer_out",
    "step13 head_weights1 mixer_stats",
    "step14 head_out10 norm_y",
    "step15 head_out11",
    "step16 head_out12 flip_y",
    "step17 head_out13 project_q",
    "step18 q_sizes project_k attention_out project_v sizes flip_heads project_out heads_out modulation scales",
    "modulated",
)
FQ = NTILE * P


def conditioned_blocks(nc, ctx, counts, io, ident, eps_ln, state, resid):
    def sb(name, shape, dt=F32):
        return ctx.enter_context(nc.sbuf_tensor(name, shape, dt))

    banks = [ctx.enter_context(nc.psum_tensor(f"bank{k}", [P, 512], F32)) for k in range(8)]

    ids = sb("ids", [P, 3, NU * B], I32)
    w_int1 = sb("w_int1", [P, 2 * INT_IN, D])
    w_mix = sb("w_mix", [P, 8, D])
    w_int2 = sb("w_int2", [P, KT, D])
    w_qk = sb("w_qk", [P, KT, 2 * FQ])
    w_v = sb("w_v", [P, KT, D])
    w_proj = sb("w_proj", [P, KT, D])
    k_w, o_w = sb("k_w", [P, KT, D]), sb("o_w", [P, KT, D])
    rows = sb("rows", [P, 5, D])
    fcols = sb("fcols", [P, 16 + 2 * NTILE])
    aw = sb("aw", [P, INT_IN])
    s_t = [sb(f"s_t{m}", [w, B]) for m, w in enumerate((128, 64, 32))]
    m_w1 = [sb(f"m_w1{m}", [w, D]) for m, w in enumerate((128, 64, 32))]
    m_w2 = [sb(f"m_w2{m}", [P, KT, D]) for m in range(3)]
    m_rows = sb("m_rows", [B, 3, 3, D])
    aff = [sb(f"aff{m}", [P, D]) for m in range(2)]
    ones = sb("ones", [P, P])
    slots = sb("slots", [P, P // SLOT])
    nhalf = sb("nhalf", [P, NH])
    mix = sb("mix", [P, INT_IN])
    amax, esum, erec = sb("amax", [P, 1]), sb("esum", [P, 1]), sb("erec", [P, 1])
    m_hid = sb("m_hid", [P, KT, B])
    m_out, m_norm = sb("m_out", [B, D]), sb("m_norm", [B, D])
    m_stat, m_mv, m_sd, m_rs = sb("m_stat", [B, 6]), sb("m_mv", [B, 2]), sb("m_sd", [B, 1]), sb("m_rs", [B, 1])
    m_t = sb("m_t", [P, 3, KT, B])
    int_bias = sb("int_bias", [P, KT, B])
    style = sb("style", [P, 4, B])
    k_sq, o_sq = sb("k_sq", [P, KT, D]), sb("o_sq", [P, KT, D])
    eps_mod = sb("eps_mod", [P, 1])

    dma = ctx.enter_context(nc.semaphore("dma_front"))
    pre = Stretch(nc, ctx, "front_setup", counts, 0)
    body = Stretch(nc, ctx, "front", counts, B)

    pre.begin()
    n = 0
    flat = {2: None, 3: "p a b -> p (a b)", 4: "p a b c -> p (a b c)"}
    for dst, src in (
        [(ids, "ids"), (w_int1, "w_int1"), (w_int2, "w_int2"), (w_qk, "w_qk"), (w_v, "w_v"),
         (w_proj, "w_proj"), (k_w, "k_w"), (o_w, "o_w"), (fcols, "fcols")]
        + [(s_t[m], f"s_t{m}") for m in range(3)] + [(m_w1[m], f"m_w1{m}") for m in range(3)]
        + [(m_w2[m], f"m_w2{m}") for m in range(3)] + [(aff[m], f"aff{m}") for m in range(2)]
    ):
        d = dst[:, :] if len(dst.shape) == 2 else dst.ap().rearrange(flat[len(dst.shape)])
        nc.sync.dma_start(d, io[src]).then_inc(dma, 16)
        n += 16
    for dst, src, w in ((rows, "rows", P), (aw, "aw", P), (m_rows, "m_rows", B)):
        d = dst[:, :] if len(dst.shape) == 2 else dst.ap().rearrange(flat[len(dst.shape)])
        nc.scalar.dma_start(d, io[src].broadcast_to([w, io[src].shape[1]])).then_inc(dma, 16)
        n += 16
    pre.mark("pool", nc.gpsimd.memset(ones[:, :], 1.0), "ones")
    pre.mark("pool", nc.gpsimd.memset(nhalf[:, :], -0.5), "nhalf")
    pre.mark("pool", nc.gpsimd.memset(eps_mod[:, :], 1e-8), "eps_mod")
    pre.mark("dve", nc.vector.memset(slots[:, :], 0.0), "slots0")
    pre.wait("dve", "slots0")
    for g in range(P // SLOT):
        m = nc.vector.memset(slots[g * SLOT:(g + 1) * SLOT, g:g + 1], 1.0)
    pre.mark("dve", m, "slots")
    for lane in ("pe", "act", "dve", "pool"):
        pre.eng[lane].wait_ge(dma, n)
    pre.mark("dve", nc.vector.tensor_reduce(amax[:, :], aw[:, :], AX.X, ALU.max, negate=True), "amax")
    pre.wait("act", "amax")
    pre.mark("act", nc.scalar.activation(mix[:, :], aw[:, :], ACT.Exp, bias=amax[:, :], accum_out=esum[:, :]),
             "mix_exp")
    pre.wait("dve", "mix_exp")
    pre.mark("dve", nc.vector.reciprocal(erec[:, :], esum[:, :]), "erec")
    pre.wait("dve", "erec")
    pre.mark("dve", nc.vector.tensor_scalar(mix[:, :], mix[:, :], erec[:, 0:1], None, ALU.mult), "mix")
    pre.wait("dve", "mix")
    for dst, blk in ((0, 0), (2, 1), (6, 5)):
        nc.vector.tensor_scalar(w_mix[:, dst:dst + 2, :], w_int1[:, 2 * blk:2 * blk + 2, :],
                                mix[:, blk:blk + 1], None, ALU.mult)
    pre.mark("dve", nc.vector.tensor_scalar(w_mix[:, 4:6, :], w_int1[:, 4:6, :], mix[:, 2:3], None, ALU.mult),
             "w_mix", 2)
    for blk in (3, 4):
        pre.wait("dve", "w_mix", blk - 1)
        for kt in range(KT):
            m = nc.vector.scalar_tensor_tensor(out=w_mix[:, 4 + kt, :], in0=w_int1[:, 2 * blk + kt, :],
                                               scalar=mix[:, blk:blk + 1], in1=w_mix[:, 4 + kt, :],
                                               op0=ALU.mult, op1=ALU.add)
        pre.mark("dve", m, "w_mix", blk)
    for m3 in range(3):
        if m3:
            pre.wait("pe", "m_hid", m3 - 1)
        for mt in range(KT):
            m = nc.tensor.matmul(banks[0][:, mt * B:(mt + 1) * B], m_w1[m3][:, mt * P:(mt + 1) * P],
                                 s_t[m3][:, :], start=True, stop=True)
        pre.mark("pe", m, "m_h", m3)
        pre.wait("act", "m_h", m3)
        if m3:
            pre.wait("act", "m_o", m3 - 1)
        for mt in range(KT):
            m = nc.scalar.activation(m_hid[:, mt, :], banks[0][:, mt * B:(mt + 1) * B], ACT.Silu,
                                     bias=fcols[:, 2 * m3 + mt:2 * m3 + mt + 1])
        pre.mark("act", m, "m_hid", m3)
        pre.wait("pe", "m_hid", m3)
        if m3:
            pre.wait("pe", "m_out", m3 - 1)
        for kt in range(KT):
            m = nc.tensor.matmul(banks[1][0:B, 0:D], m_hid[:, kt, :], m_w2[m3][:, kt, :],
                                 start=kt == 0, stop=kt == KT - 1)
        pre.mark("pe", m, "m_o", m3)
        pre.wait("dve", "m_o", m3)
        pre.mark("dve", nc.vector.tensor_tensor(m_out[:, :], banks[1][0:B, 0:D], m_rows[:, m3, 0, :], ALU.add),
                 "m_out", m3)
        pre.wait("dve", "m_out", m3)
        pre.mark("dve", nc.vector.bn_stats(m_stat[:, :], m_out[:, :]), "m_stat", m3)
        pre.wait("dve", "m_stat", m3)
        pre.mark("dve", nc.vector.bn_aggr(m_mv[:, :], m_stat[:, :]), "m_mv", m3)
        pre.wait("act", "m_mv", m3)
        pre.mark("act", nc.scalar.activation(m_sd[:, :], m_mv[:, 1:2], ACT.Sqrt, bias=eps_ln[0:B, :]), "m_sd", m3)
        pre.wait("dve", "m_sd", m3)
        pre.mark("dve", nc.vector.reciprocal(m_rs[:, :], m_sd[:, :]), "m_rs", m3)
        pre.wait("dve", "m_rs", m3)
        pre.mark("dve", nc.vector.tensor_scalar(m_norm[:, :], m_out[:, :], m_mv[:, 0:1], m_rs[:, 0:1],
                                                ALU.subtract, ALU.mult), "m_n0", m3)
        pre.wait("dve", "m_n0", m3)
        pre.mark("dve", nc.vector.tensor_tensor(m_norm[:, :], m_norm[:, :], m_rows[:, m3, 1, :], ALU.mult),
                 "m_n1", m3)
        pre.wait("dve", "m_n1", m3)
        pre.mark("dve", nc.vector.tensor_tensor(m_norm[:, :], m_norm[:, :], m_rows[:, m3, 2, :], ALU.add),
                 "m_n2", m3)
        pre.wait("pe", "m_n2", m3)
        if m3:
            pre.wait("pe", "m_t", m3 - 1)
        for kt in range(KT):
            m = nc.tensor.transpose(banks[2][:, kt * B:(kt + 1) * B], m_norm[:, kt * P:(kt + 1) * P],
                                    ident[0:B, 0:B])
        pre.mark("pe", m, "m_tp", m3)
        pre.wait("dve", "m_tp", m3)
        pre.mark("dve", nc.vector.tensor_scalar(m_t[:, m3, :, :].rearrange("p a b -> p (a b)"),
                                                banks[2][:, 0:KT * B], mix[:, 2 + m3:3 + m3], None, ALU.mult),
                 "m_t", m3)
    pre.wait("pe", "m_t", 2)
    for mt in range(KT):
        for m3 in range(3):
            for kt in range(KT):
                m = nc.tensor.matmul(banks[3][:, mt * B:(mt + 1) * B],
                                     w_int1[:, 4 + 2 * m3 + kt, mt * P:(mt + 1) * P], m_t[:, m3, kt, :],
                                     start=m3 + kt == 0, stop=m3 == 2 and kt == KT - 1)
    pre.mark("pe", m, "int_bias_ps")
    pre.wait("dve", "int_bias_ps")
    for mt in range(KT):
        m = nc.vector.tensor_scalar(int_bias[:, mt, :], banks[3][:, mt * B:(mt + 1) * B],
                                    fcols[:, 6 + mt:7 + mt], None, ALU.add)
    pre.mark("dve", m, "int_bias")
    for m2 in range(2):
        for mt in range(KT):
            c = 2 * m2 + mt
            m = nc.tensor.matmul(banks[4][:, c * B:(c + 1) * B], aff[m2][:, mt * P:(mt + 1) * P], s_t[0][:, :],
                                 start=True, stop=True)
    pre.mark("pe", m, "style_ps")
    pre.wait("dve", "style_ps")
    for c in range(4):
        m = nc.vector.tensor_scalar(style[:, c, :], banks[4][:, c * B:(c + 1) * B], fcols[:, 8 + c:9 + c], None,
                                    ALU.add)
    pre.mark("dve", m, "style")
    nc.scalar.activation(k_sq.ap(), k_w.ap(), ACT.Square)
    pre.mark("act", nc.scalar.activation(o_sq.ap(), o_w.ap(), ACT.Square), "w_sq")
    pre.end()
    nc.all_engine_barrier()

    x_tok = sb("x_tok", [P, NU, D])
    idc = sb("idc", [P, 3, NU], I32)
    pw = sb("pw", [P, NU, 2 * D])
    ct = sb("ct", [P, NU, 4 * D])
    ms = sb("ms", [P, NU, 2 * D])
    stat, mv = sb("stat", [P, NU, 6]), sb("mv", [P, NU, 2])
    rs = sb("rs", [P, NU])
    xh, hh, tt, ss = (sb(q, [P, NU, D]) for q in ("xh", "hh", "tt", "ss"))
    cat = sb("cat", [P, 8, N])
    ibc = sb("ibc", [P, KT])
    hid = sb("hid_t", [P, KT, N])
    y, y_t = sb("y", [P, NU, D]), sb("y_t", [P, KT, N])
    q_t, k_t = sb("q_t", [P, NTILE, N]), sb("k_t", [P, NTILE, N])
    v = sb("v_rows", [P, NU, D])
    junk = sb("junk", [P, N])
    q_abs = sb("q_abs", [P, NTILE, N])
    qsq, kab, yab = sb("qsq", [P, NTILE]), sb("kab", [P, NTILE]), sb("yab", [P, KT])
    most, peak = sb("most", [P, 2 * NH + 1]), sb("peak", [P, 2 * NH + 1])
    peak2, yrec = sb("peak2", [P, 2 * NH]), sb("yrec", [P, 1])
    offset = sb("offset", [P, NH])
    qmask, fro = sb("qmask", [P, NH]), sb("fro", [P, NH])
    scl = sb("scl", [P, NH])
    rmax, rbias = sb("rmax", [P, 2, 2]), sb("rbias", [P, 2, 2])
    pr, pr_t = sb("pr", [P, 2, 2, N]), sb("pr_t", [P, 2, 2, NU, P])
    psm, pri = sb("psm", [P, NU, NH]), sb("pri", [P, NU, NH])
    o, o_t = sb("o", [P, NU, D]), sb("o_t", [P, KT, N])
    x1 = sb("x1_t", [P, KT, N])
    stc, stc2 = sb("stc", [P, 4]), sb("stc2", [P, 4])
    stw = sb("stw", [P, 4, P])
    dem, demr = sb("dem", [P, 2, D]), sb("demr", [P, 2, D])
    w_m = sb("w_m", [P, 2, KT, D])
    kx = sb("kx", [P, NU, D])
    prod = sb("prod", [P, NH, NH, HD])
    sc, scm, scs, scr = sb("sc", [P, NH, NH]), sb("scm", [P, NH]), sb("scs", [P, NH]), sb("scr", [P, NH])
    o2, o2_t = sb("o2", [P, NU, D]), sb("o2_t", [P, KT, N])
    dma_x = ctx.enter_context(nc.semaphore("dma_x"))
    dma_g = [ctx.enter_context(nc.semaphore(f"dma_g{k}")) for k in range(3)]

    def W(lane, *name, back=0):
        body.wait_batch(lane, *name, back=back)

    def bank_free(*name, back=0):
        body.wait("pe", *name, back=back)

    def M(lane, m, *name):
        body.mark_batch(lane, m, *name)

    def dve(m, *name):
        M("dve", m, *name)
        W("dve", *name)

    T = lambda a: slice(a * P, (a + 1) * P)
    two = lambda bank: bank[:, :].rearrange("p (a n) -> p a n", a=2)
    V, A, G, E = nc.vector, nc.scalar, nc.gpsimd, nc.tensor
    VT, TS = V.tensor_tensor, V.tensor_scalar

    def flip(src, bank, name, need=None):
        if need:
            W("pe", *need)
        for kt in range(KT):
            for u in range(NU):
                m = E.transpose(bank[:, kt * N + u * P:][:, 0:P], src[:, u, T(kt)], ident[:, :])
        M("pe", m, name)

    def norm_stats(src, name):
        for u in range(NU):
            m = V.bn_stats(stat[:, u, :], src[:, u, :])
        dve(m, name, "stat")
        body.carry("dve")
        for u in range(NU):
            m = V.bn_aggr(mv[:, u, :], stat[:, u, :])
        dve(m, name, "mv")
        dve(TS(mv[:, :, 1], mv[:, :, 1], 1e-5, None, ALU.add), name, "var")
        W("pool", name, "var")
        M("pool", G.tensor_tensor(rs[:, :], mv[:, :, 1], nhalf[:, 0:NU], ALU.pow), name, "rs")
        W("dve", name, "rs")

    def normalise(dst, src, name):
        for u in range(NU):
            m = TS(dst[:, u, :], src[:, u, :], mv[:, u, 0:1], rs[:, u:u + 1], ALU.subtract, ALU.mult)
        M("dve", m, name, "norm")

    row = lambda r: rows[:, r, :].unsqueeze(1).broadcast_to([P, NU, D])
    by_slot = lambda cols4: cols4[:, :].unsqueeze(2).broadcast_to([P, NTILE, P // SLOT])
    slot_mask = slots[:, :].unsqueeze(1).broadcast_to([P, NTILE, P // SLOT])
    SB = (banks[1], banks[2])
    PB = (banks[3], banks[4])
    OB = banks[6]

    def fetch(b):
        W("sp", "xflip", back=1)
        W("sp", "xstat", "norm", back=1)
        nc.sync.dma_start(x_tok.ap(), io["x"][bass.ds(b, 1), :, :].rearrange("o (u p) d -> p (o u) d", p=P)
                          ).then_inc(dma_x, 16)
        W("pool", "s_add", back=1)
        W("pool", "h_add", back=1)
        M("pool", G.tensor_copy(idc.ap(), ids[:, :, bass.ds(b * NU, NU)]), "idc")
        W("pool", "idc")
        body.carry("pool")
        for k, (dst, tab) in enumerate(((pw, "t_pw"), (ct, "t_ct"), (ms, "t_ms"))):
            for u in range(NU):
                G.indirect_dma_start(dst[:, u, :], None, io[tab],
                                     bass.IndirectOffsetOnAxis(ap=idc[:, k, u:u + 1], axis=0)
                                     ).then_inc(dma_g[k], 16)

    def norm_x(b):
        V.wait_ge(dma_x, (b + 1) * 16)
        norm_stats(x_tok, "xstat")
        W("dve", "s_mul", back=1)
        normalise(xh, x_tok, "xstat")

    def mix_t_s(b):
        G.wait_ge(dma_g[1], (b + 1) * (16 * NU))
        W("pool", "xstat", "norm")
        W("pool", "tflip", back=1)
        M("pool", G.tensor_tensor(tt.ap(), xh.ap(), ct[:, :, 2 * D:3 * D], ALU.mult), "t_mul")
        W("pool", "t_mul")
        M("pool", G.tensor_tensor(tt.ap(), tt.ap(), ct[:, :, 3 * D:4 * D], ALU.add), "t_add")
        G.wait_ge(dma_g[2], (b + 1) * (16 * NU))
        W("pool", "sflip", back=1)
        M("pool", G.tensor_tensor(ss.ap(), xh.ap(), ms[:, :, 0:D], ALU.mult), "s_mul")
        W("pool", "s_mul")
        M("pool", G.tensor_tensor(ss.ap(), ss.ap(), ms[:, :, D:2 * D], ALU.add), "s_add")

    def mix_h(b):
        W("dve", "xstat", "norm")
        V.wait_ge(dma_g[0], (b + 1) * (16 * NU))
        W("dve", "hflip", back=1)
        dve(VT(hh.ap(), xh.ap(), pw[:, :, 0:D], ALU.mult), "h_mul0")
        dve(VT(hh.ap(), hh.ap(), pw[:, :, D:2 * D], ALU.add), "h_add0")

    def norm_h(b):
        W("dve", "h_add0")
        norm_stats(hh, "hstat")

    def mix_h2(b):
        normalise(hh, hh, "hstat")
        W("dve", "hstat", "norm")
        V.wait_ge(dma_g[1], (b + 1) * (16 * NU))
        dve(VT(hh.ap(), hh.ap(), ct[:, :, 0:D], ALU.mult), "h_mul")
        M("dve", VT(hh.ap(), hh.ap(), ct[:, :, D:2 * D], ALU.add), "h_add")

    def flip_x(b):
        E.wait_ge(dma_x, (b + 1) * 16)
        bank_free("x1", back=1)
        flip(x_tok, banks[0], "xflip")
        W("act", "xflip")
        W("act", "hid_ps", back=1)
        M("act", A.activation(resid[:, bass.ds(b, 1), :].rearrange("p o n -> p (o n)"), banks[0][:, :], ACT.Copy),
          "x_t")
        M("act", A.activation(cat[:, 4:6, :], two(banks[0]), ACT.Copy), "cat_x")

    def flip_mixed(n):
        def run(b):
            src, ready = ((tt, "t_add"), (ss, "s_add"), (hh, "h_add"))[n]
            name, c, bank = ("tflip", "sflip", "hflip")[n], (2, 6, 0)[n], banks[(5, 0, 5)[n]]
            bank_free(*(("kx",), ("cat_x",), ("cat", 0))[n])
            flip(src, bank, name, (ready,))
            W("act", name)
            M("act", A.activation(cat[:, c:c + 2, :], two(bank), ACT.Copy), "cat", n)
        return run

    def mixer_hidden(b):
        W("act", "hid", back=1)
        M("act", A.activation(ibc[:, :], int_bias[:, :, bass.ds(b, 1)].rearrange("p a o -> p (a o)"), ACT.Copy),
          "ibc")
        W("act", "ibc")
        W("pe", "cat", 2)
        for mt in range(KT):
            for c in range(8):
                m = E.matmul(banks[0][:, mt * N:(mt + 1) * N], w_mix[:, c, T(mt)], cat[:, c, :],
                             start=c == 0, stop=c == 7)
        M("pe", m, "hid_ps")

    def mixer_silu(b):
        W("act", "hid_ps")
        W("act", "y_ps", back=1)
        for mt in range(KT):
            m = A.activation(hid[:, mt, :], banks[0][:, mt * N:(mt + 1) * N], ACT.Silu, bias=ibc[:, mt:mt + 1])
        M("act", m, "hid")

    def mixer_out(b):
        W("pe", "hid")
        for u in range(NU):
            for kt in range(KT):
                m = E.matmul(banks[5][:, u * D:(u + 1) * D], hid[:, kt, T(u)], w_int2[:, kt, :],
                             start=kt == 0, stop=kt == KT - 1)
        M("pe", m, "y_ps")

    def mixer_stats(b):
        W("dve", "y_ps")
        W("dve", "yflip", back=1)
        dve(VT(y.ap(), two(banks[5]), row(0), ALU.add), "y_b")
        norm_stats(y, "ystat")

    def norm_y(b):
        normalise(y, y, "ystat")
        W("dve", "ystat", "norm")
        dve(VT(y.ap(), y.ap(), row(1), ALU.mult), "y_g")
        M("dve", VT(y.ap(), y.ap(), row(2), ALU.add), "y")

    def flip_y(b):
        W("pe", "y")
        bank_free("hid")
        flip(y, banks[0], "yflip")
        W("act", "yflip")
        W("act", "v_ps", back=1)
        W("act", "junk", NTILE + KT - 1, back=1)
        M("act", A.activation(y_t.ap(), two(banks[0]), ACT.Copy), "y_t")

    def project_slots(half, dst, nm, pair, freed):
        W("pe", "y_t")
        for c in range(2):
            bank_free(freed, NH - 2 + c)
            for t2 in range(2):
                t = 2 * c + t2
                for kt in range(KT):
                    m = E.matmul(pair[c][:, t2 * N:(t2 + 1) * N],
                                 w_qk[:, kt, half * FQ + t * P:][:, 0:P], y_t[:, kt, :],
                                 start=kt == 0, stop=kt == KT - 1)
            M("pe", m, nm + "_ps", c)
        for c in range(2):
            W("act", nm + "_ps", c)
            W("act", "sc_ps", NH - 1, back=1)
            for t2 in range(2):
                t = 2 * c + t2
                m = A.activation(dst[:, t, :], pair[c][:, t2 * N:(t2 + 1) * N], ACT.Identity,
                                 bias=fcols[:, 16 + half * NTILE + t:][:, 0:1])
            M("act", m, nm, c)

    def project_q(b):
        project_slots(0, q_t, "q", SB, "exp")

    def q_sizes(b):
        W("act", "q", 1)
        W("act", "qmask", back=1)
        W("act", "ymax", back=1)
        for t in range(NTILE):
            W("act", "junk", t - 1) if t else W("act", "kabs", NTILE - 1, back=1)
            M("act", A.activation(junk[:, :], q_t[:, t, :], ACT.Square, accum_out=qsq[:, t:t + 1]), "junk", t)
        for kt in range(KT):
            W("act", "junk", NTILE + kt - 1)
            M("act", A.activation(junk[:, :], y_t[:, kt, :], ACT.Abs, accum_out=yab[:, kt:kt + 1]),
              "junk", NTILE + kt)
        W("act", "fro_ps", back=1)
        M("act", A.activation(q_abs.ap(), q_t.ap(), ACT.Abs), "q_abs")

    def project_k(b):
        project_slots(1, k_t, "k", PB, "prt")
        W("act", "k", 1)
        W("act", "kmask", back=1)
        for t in range(NTILE):
            W("act", "kabs", t - 1) if t else W("act", "junk", NTILE + KT - 1)
            M("act", A.activation(junk[:, :], k_t[:, t, :], ACT.Abs, accum_out=kab[:, t:t + 1]), "kabs", t)

    def project_v(b):
        bank_free("ostate", back=1)
        for u in range(NU):
            for kt in range(KT):
                m = E.matmul(banks[7][:, u * D:(u + 1) * D], y_t[:, kt, T(u)], w_v[:, kt, :],
                             start=kt == 0, stop=kt == KT - 1)
        M("pe", m, "v_ps")
        W("dve", "v_ps")
        W("dve", "av", NH - 1, back=1)
        M("dve", VT(v.ap(), two(banks[7]), row(3), ALU.add), "v")

    def sizes(b):
        W("dve", "junk", NTILE + KT - 1)
        W("dve", "peak", back=1)
        W("dve", "fro_ps", back=1)
        M("dve", V.tensor_reduce(most[:, 2 * NH:], yab[:, :], AX.X, ALU.max), "ymax")
        M("dve", VT(qmask[:, :].rearrange("p (t g) -> p t g", g=4), by_slot(qsq), slot_mask, ALU.mult), "qmask")
        W("dve", "kabs", NTILE - 1)
        M("dve", VT(most[:, NH:2 * NH].rearrange("p (t g) -> p t g", g=4), by_slot(kab), slot_mask, ALU.mult),
          "kmask")
        W("pe", "qmask")
        W("pe", "v")
        W("pe", "q_abs")
        for u in range(NU):
            for t in range(NTILE):
                E.matmul(banks[7][:, NH * (1 + u) + 4 * t:][:, 0:4], q_abs[:, t, T(u)], slots[:, :],
                         start=True, stop=True)
        M("pe", E.matmul(banks[7][:, 0:NH], ones[:, :], qmask[:, :], start=True, stop=True), "fro_ps")
        W("dve", "fro_ps")
        W("dve", "scl0", back=1)
        M("dve", V.tensor_reduce(most[:, 0:NH], banks[7][:, NH:3 * NH].rearrange("p (u h) -> p h u", u=NU), AX.X,
                                 ALU.max), "rowmax")
        M("dve", V.tensor_copy(fro[:, :], banks[7][:, 0:NH]), "fro")
        W("pool", "ymax")
        W("pool", "kmask")
        W("pool", "rowmax")
        W("pool", "yrec", back=1)
        W("pool", "peak2", back=1)
        body.carry("pool")
        M("pool", G.partition_all_reduce(peak[:, :], most[:, :], P, bass.bass_isa.ReduceOp.max), "peak")
        W("pool", "fro")
        W("pool", "exp", NH - 1, back=1)
        M("pool", G.tensor_tensor(scl[:, :], fro[:, :], nhalf[:, :], ALU.pow), "scl0")

    def scales(b):
        W("dve", "peak")
        dve(V.reciprocal(yrec[:, :], peak[:, 2 * NH:]), "yrec")
        dve(VT(peak2[:, :], peak[:, 0:2 * NH], peak[:, 0:2 * NH], ALU.mult), "peak2")
        dve(VT(offset[:, :], peak2[:, 0:NH], peak2[:, NH:], ALU.add), "offset0")
        W("dve", "scl0")
        dve(TS(scl[:, :], scl[:, :], yrec[:, 0:1], 2.0, ALU.mult, ALU.mult), "scl")
        dve(V.scalar_tensor_tensor(out=offset[:, :], in0=offset[:, :], scalar=0.5, in1=scl[:, :], op0=ALU.mult,
                                   op1=ALU.mult), "offset")

    def head(hp, e):
        return 4 * (2 * (hp // 4) + e) + hp % 4

    def scores(i):
        hp, u = divmod(i, NU)
        W("pe", "q", 1)
        W("pe", "k", 1)
        if i >= 2:
            W("pe", "exp", i - 2)
            W("pe", "rmax", i - 2)
        for e in range(2):
            h = head(hp, e)
            t, r = h // 4, slice(SLOT * (h % 4), SLOT * (h % 4) + SLOT)
            m = E.matmul(SB[i % 2][:, e * N:(e + 1) * N], q_t[r, t, T(u)], k_t[r, t, :], start=True, stop=True)
        M("pe", m, "sc_ps", i)

    def softmax(i):
        hp, u = divmod(i, NU)
        s, off = i % 2, offset[:, head(hp, 0):head(hp, 1) + 1:4]
        W("dve", "sc_ps", i)
        if i >= 2:
            W("dve", "exp", i - 2)
        elif i == 0:
            W("dve", "exp", NH - 1, back=1)
        M("dve", V.tensor_reduce(rmax[:, s, :], two(SB[s]), AX.X, ALU.max, negate=True), "rmax", i)
        W("dve", "rmax", i)
        W("dve", "offset")
        dve(VT(rbias[:, s, :], rmax[:, s, :], scl[:, head(hp, 0):head(hp, 1) + 1:4], ALU.mult), "rbias0", i)
        dve(VT(rbias[:, s, :], rbias[:, s, :], off, ALU.add), "rbias1", i)
        M("dve", VT(rbias[:, s, :], rbias[:, s, :], off, ALU.subtract), "rbias", i)
        W("act", "rbias", i)
        if i >= 2:
            W("act", "prt_ps", i - 2)
        else:
            W("act", "prt_ps", NH - 2 + i, back=1)
            W("act", "pri", back=1)
        for e in range(2):
            h = head(hp, e)
            m = A.activation(pr[:, s, e, :], SB[s][:, e * N:(e + 1) * N], ACT.Exp, bias=rbias[:, s, e:e + 1],
                             scale=scl[:, h:h + 1], accum_out=psm[:, u, h:h + 1])
        M("act", m, "exp", i)

    def flip_p(i):
        s = i % 2
        W("pe", "exp", i)
        if i >= 2:
            W("pe", "prt", i - 2)
        for e in range(2):
            for c in range(NU):
                m = E.transpose(PB[s][:, (2 * e + c) * P:][:, 0:P], pr[:, s, e, T(c)], ident[:, :])
        M("pe", m, "prt_ps", i)
        W("act", "prt_ps", i)
        if i >= 2:
            W("act", "av", i - 2)
        else:
            W("act", "av", NH - 2 + i, back=1)
        M("act", A.activation(pr_t[:, s, :, :, :].rearrange("p a b c -> p (a b c)"), PB[s][:, :], ACT.Copy),
          "prt", i)

    def weigh(i):
        hp, u = divmod(i, NU)
        s = i % 2
        W("pe", "prt", i)
        W("pe", "v")
        if i == 0:
            W("pe", "o", back=1)
        for e in range(2):
            h = head(hp, e)
            for c in range(NU):
                m = E.matmul(OB[:, u * D + h * HD:][:, 0:HD], pr_t[:, s, e, c, :], v[:, c, h * HD:(h + 1) * HD],
                             start=c == 0, stop=c == NU - 1)
        M("pe", m, "av", i)

    def attention_step(t):
        def run(b):
            for s, stage in reversed(list(enumerate((scores, softmax, flip_p, weigh)))):
                if 0 <= t - s < NH:
                    stage(t - s)
        return run

    def attention_out(b):
        W("dve", "exp", NH - 1)
        W("dve", "o", back=1)
        dve(V.reciprocal(pri.ap(), psm.ap()), "pri")
        W("dve", "av", NH - 1)
        W("dve", "oflip", back=1)
        M("dve", VT(o.ap().rearrange("p u (h d) -> p u h d", d=HD),
                    two(OB).rearrange("p u (h d) -> p u h d", d=HD),
                    pri.ap().unsqueeze(3).broadcast_to([P, NU, NH, HD]), ALU.mult), "o")
        bank_free("y_b")
        flip(o, banks[5], "oflip", ("o",))
        W("act", "oflip")
        W("act", "x1_ps", back=1)
        M("act", A.activation(o_t.ap(), two(banks[5]), ACT.Copy), "o_t")

    def project_out(b):
        W("pe", "o_t")
        bank_free("y_t")
        for mt in range(KT):
            for kt in range(KT):
                m = E.matmul(banks[0][:, mt * N:(mt + 1) * N], w_proj[:, kt, T(mt)], o_t[:, kt, :],
                             start=kt == 0, stop=kt == KT - 1)
        M("pe", m, "x1_ps")
        W("dve", "x1_ps")
        W("dve", "x_t")
        W("dve", "kx_ps", back=1)
        W("dve", "resid", back=1)
        for mt in range(KT):
            m = V.scalar_tensor_tensor(out=x1[:, mt, :], in0=banks[0][:, mt * N:(mt + 1) * N],
                                       scalar=fcols[:, 12 + mt:13 + mt],
                                       in1=resid[:, bass.ds(b, 1), mt * N:(mt + 1) * N].rearrange("p o n -> p (o n)"),
                                       op0=ALU.add, op1=ALU.add)
        M("dve", m, "x1")
        W("act", "x1")
        M("act", A.activation(resid[:, bass.ds(b, 1), :].rearrange("p o n -> p (o n)"),
                              x1.ap().rearrange("p a n -> p (a n)"), ACT.Copy), "resid")

    def modulation(b):
        W("dve", "w_m", back=1)
        dve(V.tensor_copy(stc[:, :], style[:, :, bass.ds(b, 1)].rearrange("p a o -> p (a o)")), "stc")
        dve(VT(stc2[:, :], stc[:, :], stc[:, :], ALU.mult), "stc2")
        W("dve", "dem_ps", back=1)
        for c in range(4):
            m = TS(stw[:, c, :], ones[:, :], stc2[:, c:c + 1], None, ALU.mult)
        M("dve", m, "stw")
        W("pe", "stw")
        bank_free("o_t")
        for m2, w2 in enumerate((k_sq, o_sq)):
            for kt in range(KT):
                m = E.matmul(banks[5][:, m2 * D:(m2 + 1) * D], stw[:, 2 * m2 + kt, :], w2[:, kt, :],
                             start=kt == 0, stop=kt == KT - 1)
        M("pe", m, "dem_ps")
        W("act", "dem_ps")
        W("act", "demr", back=1)
        M("act", A.activation(dem.ap(), two(banks[5]), ACT.Sqrt, bias=eps_mod[:, :]), "dem")

    def modulated(b):
        W("dve", "dem")
        dve(V.reciprocal(demr.ap(), dem.ap()), "demr")
        W("dve", "x2_ps", back=1)
        for m2, w in enumerate((k_w, o_w)):
            for kt in range(KT):
                m = V.scalar_tensor_tensor(out=w_m[:, m2, kt, :], in0=demr[:, m2, :],
                                           scalar=stc[:, 2 * m2 + kt:2 * m2 + kt + 1], in1=w[:, kt, :],
                                           op0=ALU.mult, op1=ALU.mult)
        M("dve", m, "w_m")

    def token_k(b):
        W("pe", "w_m")
        W("pe", "x1")
        bank_free("dem", back=1)
        for u in range(NU):
            for kt in range(KT):
                m = E.matmul(banks[5][:, u * D:(u + 1) * D], x1[:, kt, T(u)], w_m[:, 0, kt, :],
                             start=kt == 0, stop=kt == KT - 1)
        M("pe", m, "kx_ps")
        W("dve", "kx_ps")
        dve(VT(kx.ap(), two(banks[5]), row(4), ALU.add), "kx")

    def head_scores(u, q):
        def run(b):
            kh, hs = kx[:, u, :].rearrange("p (h d) -> p h d", d=HD), slice(4 * q, 4 * q + 4)
            dve(VT(prod[:, hs, :, :], kh[:, hs, :].unsqueeze(2).broadcast_to([P, 4, NH, HD]),
                   kh.unsqueeze(1).broadcast_to([P, 4, NH, HD]), ALU.mult), "hp", u, q)
            dve(V.tensor_reduce(sc[:, hs, :], prod[:, hs, :, :], AX.X, ALU.add), "hs", u, q)
        return run

    def head_exp(u):
        def run(b):
            dve(V.tensor_reduce(scm[:, :], sc.ap(), AX.X, ALU.max), "hm", u)
            M("dve", VT(sc.ap(), sc.ap(), scm[:, :].unsqueeze(2).broadcast_to([P, NH, NH]), ALU.subtract), "hd", u)
            W("act", "hd", u)
            M("act", A.activation(sc.ap(), sc.ap(), ACT.Exp, scale=float(HD) ** -0.5), "he", u)
        return run

    def head_weights(u):
        def run(b):
            W("dve", "he", u)
            dve(V.tensor_reduce(scs[:, :], sc.ap(), AX.X, ALU.add), "hsum", u)
            dve(V.reciprocal(scr[:, :], scs[:, :]), "hrec", u)
            dve(VT(sc.ap(), sc.ap(), scr[:, :].unsqueeze(2).broadcast_to([P, NH, NH]), ALU.mult), "hw", u)
        return run

    def head_out(u, q):
        def run(b):
            hs = slice(4 * q, 4 * q + 4)
            kd = kx[:, u, :].rearrange("p (j d) -> p d j", d=HD)
            W("dve", "o2flip", back=1)
            dve(VT(prod[:, hs, :, :], sc[:, hs, :].unsqueeze(2).broadcast_to([P, 4, HD, NH]),
                   kd.unsqueeze(1).broadcast_to([P, 4, HD, NH]), ALU.mult), "hq", u, q)
            dve(V.tensor_reduce(o2[:, u, :].rearrange("p (h d) -> p h d", d=HD)[:, hs, :], prod[:, hs, :, :], AX.X,
                                ALU.add), "ho", u, q)
        return run

    def flip_heads(b):
        bank_free("fro")
        flip(o2, banks[7], "o2flip", ("ho", NU - 1, 3))
        W("act", "o2flip")
        W("act", "x2_ps", back=1)
        M("act", A.activation(o2_t.ap(), two(banks[7]), ACT.Copy), "o2_t")

    def heads_out(b):
        W("pe", "o2_t")
        for mt in range(KT):
            for kt in range(KT):
                m = E.matmul(banks[7][:, mt * N:(mt + 1) * N], w_m[:, 1, kt, T(mt)], o2_t[:, kt, :],
                             start=kt == 0, stop=kt == KT - 1)
        M("pe", m, "x2_ps")
        W("act", "x2_ps")
        for mt in range(KT):
            m = A.activation(state[:, bass.ds(b, 1), mt * PAD + 1:(mt + 1) * PAD].rearrange("p o n -> p (o n)"),
                             banks[7][:, mt * N:(mt + 1) * N], ACT.Identity, bias=fcols[:, 14 + mt:15 + mt])
        M("act", m, "ostate")

    pieces = {func.__name__: (0, func) for func in (
        fetch, norm_x, mix_t_s, mix_h, norm_h, mix_h2, flip_x, mixer_hidden, mixer_silu, mixer_out, mixer_stats,
        norm_y, flip_y, project_q, q_sizes, project_k, project_v, sizes, scales)}
    pieces.update(flip_t=(0, flip_mixed(0)), flip_s=(0, flip_mixed(1)), flip_h=(0, flip_mixed(2)))
    pieces.update({func.__name__: (1, func) for func in (attention_out, project_out, modulation, modulated)})
    pieces.update({f"step{t}": (1, attention_step(t)) for t in range(NH + 3)})
    pieces.update({func.__name__: (2, func) for func in (token_k, flip_heads, heads_out)})
    for u in range(NU):
        pieces.update({f"head_exp{u}": (2, head_exp(u)), f"head_weights{u}": (2, head_weights(u))})
        for q in range(4):
            pieces.update({f"head_scores{u}{q}": (2, head_scores(u, q)), f"head_out{u}{q}": (2, head_out(u, q))})
    order = [pieces[name] for name in " ".join(FRONT_SCHEDULE).split()]

    def one_pass(p, first=True, second=True, third=True):
        body.begin(p + 1)
        on, batch = (first, second, third), (p + 1, p, p - 1)
        for n, (part, run) in enumerate(order):
            body.lag = part
            body.piece(n, run, batch[part] if on[part] else 0, run=on[part])
        body.end()

    one_pass(-1, second=False, third=False)
    one_pass(0, third=False)
    with nc.Fori(0, B - 2) as i:
        one_pass(i + 1)
    one_pass(B - 1, first=False)
    one_pass(B, first=False, second=False)
    nc.all_engine_barrier()


def write_out(nc, ctx, counts, out, ident, state, resid):
    def sb(name, shape, dt=F32):
        return ctx.enter_context(nc.sbuf_tensor(name, shape, dt))

    total = sb("total", [P, 2, KT, N])
    rows_out = sb("rows_out", [P, 2, NU, D])
    bank = [ctx.enter_context(nc.psum_tensor(f"out_bank{k}", [P, 512], F32)) for k in range(2)]
    dma_o = [ctx.enter_context(nc.semaphore(f"dma_o{k}")) for k in range(2)]
    last = Stretch(nc, ctx, "write_out", counts, 0)
    last.begin()
    for b in range(B):
        s = b % 2
        if b >= 2:
            last.wait("dve", "flip", b - 2)
        last.mark("dve", nc.vector.tensor_tensor(
            total[:, s, :, :], resid[:, b, :].rearrange("p (k n) -> p k n", k=KT),
            state[:, b, :].rearrange("p (k n) -> p k n", k=KT)[:, :, 1:PAD], ALU.add), "total", b)
        last.wait("pe", "total", b)
        if b >= 2:
            last.wait("pe", "rows", b - 2)
        for u in range(NU):
            for kt in range(KT):
                m = nc.tensor.transpose(bank[s][:, u * D + kt * P:][:, 0:P], total[:, s, kt, u * P:(u + 1) * P],
                                        ident[:, :])
        last.mark("pe", m, "flip", b)
        last.wait("act", "flip", b)
        if b >= 2:
            nc.scalar.wait_ge(dma_o[s], 16 * (b // 2))
        last.mark("act", nc.scalar.activation(rows_out[:, s, :, :].rearrange("p u d -> p (u d)"), bank[s][:, :],
                                              ACT.Copy), "rows", b)
        last.wait("sp", "rows", b)
        nc.sync.dma_start(out[b:b + 1, :, :].rearrange("o (u p) d -> p (o u) d", p=P), rows_out[:, s, :, :]
                          ).then_inc(dma_o[s], 16)
    for s in range(2):
        nc.sync.wait_ge(dma_o[s], 16 * (B // 2))
    last.end()
DEPTH, HEADS, DH, WIN = 6, 16, 64, 64
INNER = HEADS * DH
DI = int(D * 4 * 2 / 3)
NJ = -(-DI // P)
GH = 4
NG = HEADS // GH
assert UNITS == NG * NU
GC = GH * DH
PAD = N + 1
VR = 8
QK_SCALE = 8.0
NCOL = 2 * KT + 2 * NJ + KT


def local_layers(nc, ctx, counts, io, state, ident, eps_ln):
    def sb(name, shape, dt=F32):
        return ctx.enter_context(nc.sbuf_tensor(name, shape, dt))

    w_hi, w_lo = sb("w_hi", [P, KT, NG, 3 * GC]), sb("w_lo", [P, KT, NG, 3 * GC])
    w_raw = sb("w_raw", [P, KT, 3 * GC])
    w_o = sb("w_o", [P, INNER // P, D])
    w_1 = [sb(f"w_1{k}", [P, KT, 2 * DI]) for k in range(2)]
    w_2 = [sb(f"w_2{k}", [P, NJ, D]) for k in range(2)]
    cols = [sb(f"cols{k}", [P, NCOL]) for k in range(2)]
    qk_gain = [sb(f"qk_gain{k}", [P, 2, DH]) for k in range(2)]
    rot_cos, rot_sin = sb("rot_cos", [P, NU, 2, DH]), sb("rot_sin", [P, NU, 2, DH])
    cos_t, sin_t = sb("cos_t", [P, NU, 2, DH]), sb("sin_t", [P, NU, 2, DH])
    band = sb("band", [P, NU, P], BF16)
    ident_bf = sb("ident_bf", [P, P], BF16)
    mean_w = sb("mean_w", [P, P])
    half = sb("half", [P, 2 * GH])

    x_hi, x_lo = sb("x_hi", [P, KT * PAD]), sb("x_lo", [P, KT * PAD])
    sq = sb("sq", [P, 2, 2 * GC])
    norm2 = sb("norm2", [P, 2, 2 * GH])
    rnorm = sb("rnorm", [P, 4, 2 * GH])
    by_cos = sb("by_cos", [P, 2, 2 * GC])
    turned = sb("turned", [P, 2, 2 * GC])
    qk_t = sb("qk_t", [P, 4, 4, P])
    v_tok = sb("v_tok", [P, VR, GC])
    v_shift = sb("v_shift", [P, NG, GC])
    negmax = sb("negmax", [P, 2, GH])
    escale, ebias = sb("escale", [P, 2, GH]), sb("ebias", [P, 2, GH])
    prob = sb("prob", [P, 2, GH, P])
    rsum, rinv = sb("rsum", [P, 2, GH]), sb("rinv", [P, 2, GH])
    prob_t = sb("prob_t", [P, 2, GH, P])
    attn_t = sb("attn_t", [P, INNER // P, N])
    x1 = sb("x1", [P, KT * PAD])
    cent = sb("cent", [P, KT, N])
    sdev = sb("sdev", [P, N])
    lin_in = sb("lin_in", [P, KT, N])
    cent2 = lin_in
    gate = sb("gate", [P, NJ, N])
    hidden = sb("hidden", [P, NJ, N])

    def ps(name):
        return ctx.enter_context(nc.psum_tensor(name, [P, 512], F32))

    ps_qk = [ps("ps_qk0"), ps("ps_qk1")]
    ps_v = ps("ps_v")
    ps_t = ps("ps_t")
    ps_s = [ps("ps_s0"), ps("ps_s1")]
    ps_f = [ps("ps_f0"), ps("ps_f1")]

    dma_w = [ctx.enter_context(nc.semaphore(f"dma_w{k}")) for k in range(2)]
    dma_q = [ctx.enter_context(nc.semaphore(f"dma_q{g}")) for g in range(NG)]
    dma_o = ctx.enter_context(nc.semaphore("dma_wo"))
    dma_c = ctx.enter_context(nc.semaphore("dma_c"))
    ready = Stretch(nc, ctx, "layer_setup", counts, 0)
    sec = Stretch(nc, ctx, "layer", counts, DEPTH)
    attn = Stretch(nc, ctx, "attn", counts, DEPTH * B)
    ffn = Stretch(nc, ctx, "ffn", counts, DEPTH * B)

    W_DMAS = 4

    def load_layer(k, layer):
        one = bass.ds(layer, 1)
        for dst, src in ((w_1[k], io["w_1"]),
                         (w_2[k], io["w_2"]), (cols[k], io["cols"])):
            shape = dst.shape
            flat = dst[:, :] if len(shape) == 2 else dst.ap().rearrange(
                "p a b -> p (a b)" if len(shape) == 3 else "p a b c -> p (a b c)")
            nc.sync.dma_start(flat, src[one, :, :].rearrange("l p n -> (l p) n")).then_inc(dma_w[k], 16)
        nc.sync.dma_start(qk_gain[k].ap().rearrange("p a b -> p (a b)"),
                          io["qk_gain"][one, :].broadcast_to([P, 2 * DH])).then_inc(dma_w[k], 16)

    def split(high, low, whole):
        return (lambda: nc.vector.tensor_copy(high.bitcast(F32R), whole),
                lambda: nc.vector.tensor_tensor(low.bitcast(F32R), whole, high, ALU.subtract))

    def load_w_o(layer):
        nc.sync.dma_start(w_o.ap().rearrange("p a b -> p (a b)"),
                          io["w_o"][bass.ds(layer, 1), :, :].rearrange("l p n -> (l p) n")).then_inc(dma_o, 16)

    ready.begin()
    for dst, src in ((rot_cos, io["rot_cos"]), (rot_sin, io["rot_sin"])):
        nc.sync.dma_start(dst.ap().rearrange("p a b c -> p (a b c)"), src).then_inc(dma_c, 16)
    nc.sync.dma_start(band.ap().rearrange("p a b -> p (a b)"), io["band"]).then_inc(dma_c, 16)
    nc.sync.wait_ge(dma_c, 48)
    load_w_o(0)
    load_layer(0, 0)
    load_layer(1, 1)
    ready.mark("pool", nc.gpsimd.memset(mean_w[:, :], 1.0 / D), "mean_w")
    ready.mark("pool", nc.gpsimd.memset(half[:, :], -0.5), "half")
    ready.mark("pool", nc.gpsimd.memset(x1[:, :], 0.0), "x1_zero")
    ready.mark("pool", nc.gpsimd.memset(gate[:, :, :], 0.0), "gate_zero")
    ready.mark("pool", nc.gpsimd.memset(hidden[:, :, :], 0.0), "hidden_zero")
    ready.mark("dve", nc.vector.tensor_copy(ident_bf[:, :], ident[:, :]), "ident_bf")
    ready.end()
    nc.all_engine_barrier()

    def U(u):
        return slice(u * P, (u + 1) * P)

    def heads(ap, n=2 * GH):
        return ap.rearrange("p (h t d) -> p h t d", t=2, d=DH // 2)

    def times_wqkv(out, g, u, columns):
        terms = [(x, w, kt) for kt in range(KT) for x, w in ((x_hi, w_hi), (x_hi, w_lo), (x_lo, w_hi))]
        for n, (x, w, kt) in enumerate(terms):
            lhs = x[:, (1 if kt == 0 else PAD) + u * P:][:, 0:P]
            m = nc.tensor.matmul(out, lhs.bitcast(F32R), w[:, kt, g, columns].bitcast(F32R),
                                 start=n == 0, stop=n == len(terms) - 1)
        return m

    def project(i):
        g, u = divmod(i % UNITS, NU)
        attn.wait_unit("pe", "qk_square", i - 2)
        attn.wait_unit("pe", "qk_by_sin", i - 2)
        if i == UNITS:
            attn.wait("pe", "xa")
        m = times_wqkv(ps_qk[i % 2][:, :], g, u, slice(0, 2 * GC))
        attn.mark_unit("pe", m, "qk", i)
        attn.wait_unit("pe", "v_copied", i - 1)
        attn.wait_unit("pe", "attn_t", i - 5)
        m = times_wqkv(ps_v[:, 0:GC], g, u, slice(2 * GC, 3 * GC))
        attn.mark_unit("pe", m, "v", i)
        s, qk = i % 2, ps_qk[i % 2]
        attn.wait_unit("act", "qk", i)
        attn.wait_unit("act", "norm2", i - 2)
        attn.mark_unit("act", nc.scalar.activation(sq[:, s, :], qk[:, :], ACT.Square), "qk_square", i)
        attn.wait_unit("act", "v", i)
        attn.wait_unit("act", "attn", i - VR)
        m = nc.scalar.activation(v_tok[:, i % VR, :], ps_v[:, 0:GC], ACT.Copy)
        if u == 0:
            attn.wait_unit("act", "attn", i + 1 - UNITS)
            m = nc.scalar.activation(v_shift[WIN:P, g, :], ps_v[WIN:P, 0:GC], ACT.Copy)
        else:
            m = nc.scalar.activation(v_shift[0:WIN, g, :], ps_v[0:WIN, 0:GC], ACT.Copy)
        attn.mark_unit("act", m, "v_copied", i)

    def rotate(i):
        u, s = i % NU, i % 2
        qk = ps_qk[s]
        attn.wait_unit("dve", "qk_square", i)
        attn.wait_unit("dve", "turned", i - 2)
        attn.wait_unit("dve", "turned_t", i - 2)
        shape = [P, 2, GH, DH]
        cs = cos_t[:, u, :, :].unsqueeze(2).broadcast_to(shape)
        attn.mark_unit("dve", nc.vector.tensor_tensor(
            by_cos[:, s, :].rearrange("p (a h d) -> p a h d", a=2, h=GH),
            qk[:, :].rearrange("p (a h d) -> p a h d", a=2, h=GH), cs, ALU.mult), "qk_by_cos", i)
        for a in range(2):
            sn = sin_t[:, u, a, :].rearrange("p (t d) -> p t d", t=2).unsqueeze(1)
            cut = slice(a * GC, (a + 1) * GC)
            m = nc.vector.tensor_tensor(heads(turned[:, s, cut]), heads(qk[:, cut])[:, :, ::-1, :],
                                        sn.broadcast_to([P, GH, 2, DH // 2]), ALU.mult)
        attn.mark_unit("dve", m, "qk_by_sin", i)
        attn.wait_unit("dve", "qk_square", i)
        attn.wait_unit("dve", "rnorm", i - 2)
        attn.mark_unit("dve", nc.vector.tensor_reduce(norm2[:, s, :], sq[:, s, :].rearrange(
            "p (h d) -> p h d", d=DH), AX.X, ALU.add), "norm2", i)
        attn.wait_unit("dve", "norm2", i)
        attn.mark_unit("dve", nc.vector.tensor_scalar(norm2[:, s, :], norm2[:, s, :], 1e-24, None, ALU.max),
                  "norm2_floor", i)

        attn.wait_unit("pool", "norm2_floor", i)
        attn.wait_unit("pool", "ebias", i - 4)
        attn.mark_unit("pool", nc.gpsimd.tensor_tensor(rnorm[:, i % 4, :], norm2[:, s, :], half[:, :], ALU.pow),
                  "rnorm", i)
        attn.wait_unit("pool", "qk_by_sin", i)
        m = nc.gpsimd.tensor_tensor(turned[:, s, :], by_cos[:, s, :], turned[:, s, :], ALU.add)
        attn.mark_unit("pool", m, "turned", i)
        attn.wait_unit("pool", "turned", i)
        kk = turned[:, s, GC:].rearrange("p (h d) -> p h d", d=DH)
        m = nc.gpsimd.tensor_tensor(kk, kk, rnorm[:, i % 4, GH:].unsqueeze(2).broadcast_to([P, GH, DH]), ALU.mult)
        attn.mark_unit("pool", m, "k_unit", i)

    def flip_qk(i):
        attn.wait_unit("pe", "k_unit", i)
        attn.wait_unit("pe", "qk_t", i - 1)
        attn.wait_unit("pe", "prob_t", i - 2)
        for c in range(4):
            m = nc.tensor.transpose(ps_t[:, U(c)], turned[:, i % 2, U(c)], ident[:, :])
        attn.mark_unit("pe", m, "turned_t", i)
        attn.wait_unit("act", "turned_t", i)
        attn.wait_unit("act", "scores", i - 3)
        attn.mark_unit("act", nc.scalar.activation(qk_t[:, i % 4, :, :].rearrange("p a b -> p (a b)"),
                                              ps_t[:, :], ACT.Copy), "qk_t", i)

    def half_bank(odd, i):
        return ps_s[odd][:, 0:2 * P]

    def score(i):
        u, s = i % NU, i % 2
        attn.wait_unit("pe", "qk_t", i)
        attn.wait_unit("pe", "prob", i - 1)
        for odd in range(2):
            nc.tensor.matmul(half_bank(odd, i).rearrange("p (h k) -> p h k", h=2), ident_bf[:, :],
                             band[:, u, :].unsqueeze(1).broadcast_to([P, 2, P]), start=True, stop=False,
                             skip_group_check=True)
        for h in range(GH):
            r, c = slice(DH * (h % 2), DH * (h % 2) + DH), h // 2
            q, kk, before = qk_t[r, i % 4, c, :], qk_t[r, i % 4, 2 + c, :], qk_t[r, (i - 1) % 4, 2 + c, :]
            o = half_bank(h % 2, i)[:, U(h // 2)]
            m = nc.tensor.matmul(o[:, 0:WIN], q, kk[:, 0:WIN], start=False, stop=True, skip_group_check=True)
            m = nc.tensor.matmul(o[WIN:P, WIN:P], q[:, WIN:P], kk[:, WIN:P], start=False, stop=True,
                                 skip_group_check=True)
            if u:
                m = nc.tensor.matmul(o[0:WIN, WIN:P], q[:, 0:WIN], before[:, WIN:P], start=False, stop=True,
                                     skip_group_check=True)
        attn.mark_unit("pe", m, "scores", i)

    def soften(i):
        s = i % 2
        attn.wait_unit("dve", "scores", i)
        attn.wait_unit("dve", "ebias", i - 2)
        for odd in range(2):
            m = nc.vector.tensor_reduce(negmax[:, s, odd::2], half_bank(odd, i).rearrange(
                "p (h k) -> p h k", h=2), AX.X, ALU.max, negate=True)
        attn.mark_unit("dve", m, "negmax", i)
        attn.wait_unit("dve", "rnorm", i)
        attn.wait_unit("dve", "prob", i - 2)
        attn.mark_unit("dve", nc.vector.tensor_scalar(escale[:, s, :], rnorm[:, i % 4, 0:GH], QK_SCALE, None, ALU.mult),
                  "escale", i)
        attn.wait_unit("dve", "escale", i)
        attn.wait_unit("dve", "negmax", i)
        attn.mark_unit("dve", nc.vector.tensor_tensor(ebias[:, s, :], negmax[:, s, :], escale[:, s, :], ALU.mult),
                  "ebias", i)
        attn.wait_unit("act", "ebias", i)
        attn.wait_unit("act", "prob_t_ps", i - 2)
        attn.wait_unit("act", "rinv", i - 2)
        for h in range(GH):
            m = nc.scalar.activation(prob[:, s, h, :], half_bank(h % 2, i)[:, U(h // 2)], ACT.Exp, bias=ebias[:, s, h:h + 1],
                                     scale=escale[:, s, h:h + 1], accum_out=rsum[:, s, h:h + 1])
        attn.mark_unit("act", m, "prob", i)

    def weigh(i):
        s = i % 2
        attn.wait_unit("dve", "prob", i)
        attn.wait_unit("dve", "prob_unit", i - 2)
        attn.mark_unit("dve", nc.vector.reciprocal(rinv[:, s, :], rsum[:, s, :]), "rinv", i)
        attn.wait_unit("dve", "rinv", i)
        for h in range(GH):
            m = nc.vector.tensor_scalar(prob[:, s, h, :], prob[:, s, h, :], rinv[:, s, h:h + 1], None, ALU.mult)
        attn.mark_unit("dve", m, "prob_unit", i)

    def flip_prob(i):
        attn.wait_unit("pe", "prob_unit", i)
        attn.wait_unit("pe", "prob_t", i - 1)
        attn.wait_unit("pe", "qk_t", i + 1)
        for h in range(GH):
            m = nc.tensor.transpose(ps_t[:, U(h)], prob[:, i % 2, h, :], ident[:, :])
        attn.mark_unit("pe", m, "prob_t_ps", i)
        attn.wait_unit("act", "prob_t_ps", i)
        attn.wait_unit("act", "attn", i - 2)
        attn.mark_unit("act", nc.scalar.activation(prob_t[:, i % 2, :, :].rearrange("p a b -> p (a b)"),
                                                   ps_t[:, :], ACT.Copy), "prob_t", i)

    def attend(i):
        g, u = divmod(i % UNITS, NU)
        attn.wait_unit("pe", "prob_t", i)
        attn.wait_unit("pe", "v_copied", i + 4)
        attn.wait_unit("pe", "attn_t", i - 1)
        for h in range(GH):
            out = ps_v[DH * (h % 2):DH * (h % 2) + DH, P * (h // 2):P * (h // 2) + P]
            vh = slice(h * DH, (h + 1) * DH)
            pt = prob_t[:, i % 2, h, :]
            if u == 0:
                m = nc.tensor.matmul(out, v_tok[:, i % VR, vh], pt, start=True, stop=True)
            else:
                m = nc.tensor.matmul(out[:, 0:WIN], v_shift[:, g, vh], pt[:, 0:WIN], start=True, stop=True)
                m = nc.tensor.matmul(out[:, WIN:P], v_tok[:, i % VR, vh], pt[:, WIN:P], start=True, stop=True)
        attn.mark_unit("pe", m, "attn", i)
        attn.wait_unit("act", "attn", i)
        if i < NU:
            ffn.wait("act", "w_o", i)
        attn.mark_unit("act", nc.scalar.activation(
            attn_t[:, 2 * g:2 * g + 2, U(u)], ps_v[:, 0:GC].rearrange("p (a b) -> p a b", a=2), ACT.Copy),
            "attn_t", i)

    def feed_forward(k, b):
        c = cols[k]
        gain, shift = c[:, 0:KT], c[:, KT:2 * KT]
        b_a, b_g = c[:, 2 * KT:2 * KT + NJ], c[:, 2 * KT + NJ:2 * KT + 2 * NJ]
        b_2 = c[:, 2 * KT + 2 * NJ:]
        whole = lambda t: t[:, :].rearrange("p (k n) -> p k n", k=KT)[:, :, 1:PAD]
        shifted = lambda t: t[:, 1:1 + KT * N].rearrange("p (k n) -> p k n", k=KT)
        mine = state[:, bass.ds(b, 1), :].rearrange("p o n -> p (o n)")
        width = lambda j: min(P, DI - j * P)

        def w_o_mm(u):
            attn.wait_unit("pe", "attn_t", -1)
            ffn.wait("pe", "state", back=1)
            for mt in range(KT):
                for j in range(INNER // P):
                    m = nc.tensor.matmul(ps_f[0][:, mt * N + u * P:][:, 0:P], w_o[:, j, U(mt)],
                                         attn_t[:, j, U(u)], start=j == 0, stop=j == INNER // P - 1)
            ffn.mark("pe", m, "w_o", u)

        def add_x():
            ffn.wait("dve", "w_o", NU - 1)
            ffn.wait("dve", "mean", back=1)
            ffn.wait("dve", "state", back=1)
            ffn.mark("dve", nc.vector.tensor_tensor(whole(x1), ps_f[0][:, :].rearrange("p (k n) -> p k n", k=KT),
                                                    whole(mine), ALU.add), "x1")

        def mean_mm():
            ffn.wait("pe", "x1")
            ffn.wait("pe", "hid_read", NJ - 1, back=1)
            for kt in range(KT):
                m = nc.tensor.matmul(ps_f[1][:, 0:N], mean_w[:, :], shifted(x1)[:, kt, :],
                                     start=kt == 0, stop=kt == KT - 1)
            ffn.mark("pe", m, "mean")

        def center():
            ffn.wait("dve", "mean")
            ffn.wait("dve", "cent2", back=1)
            ffn.mark("dve", nc.vector.tensor_tensor(cent[:, :, :], shifted(x1),
                                                    ps_f[1][:, 0:N].unsqueeze(1).broadcast_to([P, KT, N]),
                                                    ALU.subtract), "cent")

        def square():
            ffn.wait("act", "cent")
            ffn.wait("act", "hid", NJ - 1, back=1)
            ffn.mark("act", nc.scalar.activation(cent2[:, :, :], cent[:, :, :], ACT.Square), "cent2")

        def var_mm():
            ffn.wait("pe", "cent2")
            for kt in range(KT):
                m = nc.tensor.matmul(ps_f[1][:, N:2 * N], mean_w[:, :], cent2[:, kt, :],
                                     start=kt == 0, stop=kt == KT - 1)
            ffn.mark("pe", m, "var")

        def root():
            ffn.wait("act", "var")
            ffn.wait("act", "normed", back=1)
            ffn.mark("act", nc.scalar.activation(sdev[:, :], ps_f[1][:, N:2 * N], ACT.Sqrt, bias=eps_ln[:, :]),
                     "sdev")

        def normalise():
            ffn.wait("dve", "sdev")
            ffn.mark("dve", nc.vector.reciprocal(sdev[:, :], sdev[:, :]), "rdev")
            ffn.wait("dve", "rdev")
            ffn.mark("dve", nc.vector.tensor_tensor(cent[:, :, :], cent[:, :, :],
                                                    sdev[:, :].unsqueeze(1).broadcast_to([P, KT, N]), ALU.mult),
                     "normed")
            ffn.wait("dve", "normed")
            ffn.wait("dve", "hid", NJ - 1, back=1)
            for kt in range(KT):
                m = nc.vector.tensor_scalar(lin_in[:, kt, :], cent[:, kt, :], gain[:, kt:kt + 1],
                                            shift[:, kt:kt + 1], ALU.mult, ALU.add)
            ffn.mark("dve", m, "lin_in")

        def hidden_tile(j):
            w, f = width(j), ps_f[j % 2]
            ffn.wait("pe", "lin_in")
            if j >= 2:
                ffn.wait("pe", "hid_read", j - 2)
            for half, first in enumerate((j * P, DI + j * P)):
                for kt in range(KT):
                    m = nc.tensor.matmul(f[0:w, half * N:(half + 1) * N], w_1[k][:, kt, first:first + w],
                                         lin_in[:, kt, :], start=kt == 0, stop=kt == KT - 1)
            ffn.mark("pe", m, "hid", j)
            lane = READ_BY[j]
            ffn.wait(lane, "hid", j)
            ffn.wait(lane, "out", KT - 1, back=1)
            ffn.wait(lane, "gated", 1, back=1)
            for dst, src, bias in ((hidden[0:w, j, :], f[0:w, 0:N], b_a), (gate[0:w, j, :], f[0:w, N:2 * N], b_g)):
                if lane == "act":
                    m = nc.scalar.activation(dst, src, ACT.Identity, bias=bias[0:w, j:j + 1])
                else:
                    m = nc.vector.tensor_scalar(dst, src, bias[0:w, j:j + 1], None, ALU.add)
            ffn.mark(lane, m, "hid_read", j)

        def gelu():
            for part in range(2):
                for j in reversed(range(part * NJ // 2, (part + 1) * NJ // 2)):
                    ffn.wait("act", "hid_read", j)
                cut = slice(part * NJ // 2, (part + 1) * NJ // 2)
                ffn.mark("act", nc.scalar.activation(gate[:, cut, :], gate[:, cut, :], ACT.Gelu), "gelu", part)

        def gate_value():
            for part in range(2):
                cut = slice(part * NJ // 2, (part + 1) * NJ // 2)
                lane, eng = GATED_BY
                for j in reversed(range(part * NJ // 2, (part + 1) * NJ // 2)):
                    ffn.wait(lane, "hid_read", j)
                ffn.wait(lane, "gelu", part)
                ffn.mark(lane, eng.tensor_tensor(hidden[:, cut, :], hidden[:, cut, :], gate[:, cut, :], ALU.mult),
                         "gated", part)

        def w_2_mm(mt):
            ffn.wait("pe", "gated", 0)
            ffn.wait("pe", "hid_read", NJ - 1)
            ffn.wait("pe", "hid_read", NJ - 2)
            for j in range(NJ):
                if j == NJ // 2:
                    ffn.wait("pe", "gated", 1)
                w = width(j)
                m = nc.tensor.matmul(ps_f[0][:, mt * N:(mt + 1) * N], w_2[k][0:w, j, U(mt)],
                                     hidden[0:w, j, :], start=j == 0, stop=j == NJ - 1)
            ffn.mark("pe", m, "out", mt)

        def new_state():
            ffn.wait("dve", "out", KT - 1)
            for mt in range(KT):
                m = nc.vector.scalar_tensor_tensor(
                    out=mine[:, mt * PAD + 1:(mt + 1) * PAD],
                    in0=ps_f[0][:, mt * N:(mt + 1) * N], scalar=b_2[:, mt:mt + 1],
                    in1=whole(x1)[:, mt, :], op0=ALU.add, op1=ALU.add)
            ffn.mark("dve", m, "state")

        parts = {func.__name__: func for func in (add_x, mean_mm, center, square, var_mm, root, normalise, gelu,
                                                  gate_value, new_state)}
        for name, func, count in (("w_o", w_o_mm, NU), ("hidden", hidden_tile, NJ), ("w_2_", w_2_mm, KT)):
            parts.update({f"{name}{n}": partial(func, n) for n in range(count)})
        return parts

    READ_BY = ("act", "act", "act", "dve", "dve", "dve")
    GATED_BY = ("dve", nc.vector)

    def take_x(b):
        attn.wait_unit("dve", "v", UNITS - 1)
        ffn.wait("dve", "state", back=1)
        mine = state[:, bass.ds(b, 1), :].rearrange("p o n -> p (o n)")
        high, low = split(x_hi[:, :], x_lo[:, :], mine)
        attn.mark("dve", high(), "x_hi")
        attn.wait("dve", "x_hi")
        attn.mark("dve", low(), "xa")

    def fetch_wqkv(layer):
        for g in range(NG):
            sec.wait("sp", "w_lo", (g - 1) % NG, back=int(g == 0))
            sec.carry("sp")
            nc.sync.dma_start(w_raw.ap(), io["w_qkv"][bass.ds(layer, 1), :, :].rearrange(
                "l p (k g n) -> (l p) k g n", k=KT, g=NG)[:, :, g, :]).then_inc(dma_q[g], 16)

    def split_wqkv(layer, g):
        nc.vector.wait_ge(dma_q[g], (layer + 1) * 16)
        sec.carry("dve")
        attn.wait_unit("dve", "v", 2 * g + 1)
        high, low = split(w_hi[:, :, g, :], w_lo[:, :, g, :], w_raw.ap())
        sec.mark("dve", high(), "w_hi", g)
        sec.wait("dve", "w_hi", g)
        sec.mark("dve", low(), "w_lo", g)

    SPLIT_AT = (2, 4, 6, 7)
    LAGS = {"attend": 5, "flip_prob": 4, "score": 3, "soften": 3, "rotate": 1, "weigh": 3, "flip_qk": 2,
            "project": 0}
    STAGES = {func.__name__: func for func in (attend, flip_prob, score, soften, rotate, weigh, flip_qk, project)}
    SCHEDULE = (
        "w_o0 w_o1 add_x score flip_prob mean_mm soften center rotate attend weigh flip_qk project square",
        "score flip_prob var_mm soften root rotate attend weigh flip_qk project normalise",
        "score flip_prob soften rotate attend weigh hidden0 flip_qk hidden1 project",
        "score flip_prob take_x soften rotate attend weigh hidden2 flip_qk project",
        "score flip_prob soften rotate hidden3 attend weigh flip_qk project",
        "score flip_prob soften rotate hidden4 attend weigh flip_qk hidden5 gelu project gate_value",
        "score flip_prob soften rotate attend w_2_0 weigh flip_qk project",
        "w_2_1 new_state score flip_prob soften rotate attend weigh flip_qk project",
    )

    def tables(k):
        attn.wait_unit("dve", "qk_by_sin", UNITS - 1)
        gb = qk_gain[k].ap().unsqueeze(1).broadcast_to([P, NU, 2, DH])
        m = nc.vector.tensor_tensor(cos_t.ap(), rot_cos.ap(), gb, ALU.mult)
        for a in range(2):
            turn = qk_gain[k][:, a, :].rearrange("p (t d) -> p t d", t=2)[:, ::-1, :]
            m = nc.vector.tensor_tensor(
                sin_t[:, :, a, :].rearrange("p u (t d) -> p u t d", t=2),
                rot_sin[:, :, a, :].rearrange("p u (t d) -> p u t d", t=2),
                turn.unsqueeze(1).broadcast_to([P, NU, 2, DH // 2]), ALU.mult)
        sec.mark("dve", m, "tables")
        sec.wait("dve", "tables")
        sec.carry("dve")

    def one_pass(step, k=None, b=None, tail=True, front=None, weights=None, next_w_o=None):
        attn.begin(step + 2)
        ffn.begin(step)
        if weights is not None:
            sec.begin(weights[0])
            fetch_wqkv(weights[0])
        if next_w_o is not None:
            ffn.wait("sp", "w_o", NU - 1)
            sec.carry("sp")
            load_w_o(next_w_o)
        parts = feed_forward(k, b) if k is not None else {}
        k_front, b_front = front or (0, 0)
        for t, names in enumerate(SCHEDULE):
            if t and weights is not None and t in SPLIT_AT:
                split_wqkv(weights[0], SPLIT_AT.index(t))
            if t == UNITS - MAX_LAG and weights is not None:
                for lane in ("pe", "act", "dve"):
                    sec.eng[lane].wait_ge(dma_w[k_front], weights[1] * (16 * W_DMAS))
                    sec.carry(lane)
            if t == UNITS - MAX_LAG + 1 and weights is not None:
                tables(k_front)
            for name in names.split():
                if name == "take_x":
                    attn.stage(take_x, 0, b_front, run=front is not None)
                elif name in STAGES:
                    unit = t + MAX_LAG - LAGS[name]
                    if name == "project" and weights is not None and unit >= UNITS and unit % 2 == 0:
                        sec.wait("pe", "w_lo", unit % UNITS // 2)
                    attn.stage(STAGES[name], LAGS[name], unit,
                               run=tail if unit < UNITS else front is not None)
                elif k is not None:
                    parts[name]()
        if weights is not None:
            sec.wait("pe", "w_lo", NG - 1)
            sec.carry("pe")
            sec.end()
        if next_w_o is not None:
            nc.tensor.wait_ge(dma_o, (next_w_o + 1) * 16)
            sec.carry("pe")
        if k is not None:
            ffn.end()
        attn.end()

    one_pass(-2, tail=False, front=(0, 0), weights=(0, 1))
    one_pass(-1, front=(0, 1))
    nc.tensor.wait_ge(dma_o, 16)
    sec.carry("pe")

    def layer_pair(pair, final):
        for k in range(2):
            first = pair * (2 * B) + k * B
            with nc.Fori(0, B - 2) as b:
                one_pass(first + b, k, b, front=(k, b + 2))
            if final and k == 1:
                one_pass(first + (B - 2), k, B - 2)
                one_pass(first + (B - 1), k, B - 1, tail=False)
                return
            one_pass(first + (B - 2), k, B - 2, front=(1 - k, 0), weights=(pair * 2 + (k + 1), pair + (k + 1)))
            one_pass(first + (B - 1), k, B - 1, front=(1 - k, 1), next_w_o=pair * 2 + (k + 1))
            if not final:
                for part, passes in ((attn, B + 3), (ffn, B + 2)):
                    for lane in ("pe", "act", "dve"):
                        nc.sync.wait_ge(part.sem[lane], (first + passes) * part.per[lane])
                        sec.carry("sp")
                load_layer(k, pair * 2 + (k + 2))

    with nc.Fori(0, DEPTH // 2 - 1) as pair:
        layer_pair(pair, False)
    layer_pair(DEPTH // 2 - 1, True)
    nc.all_engine_barrier()
def build(nc, io, out, counts):
    made = {}
    ctx = ExitStack()
    with ctx:
        state = ctx.enter_context(nc.sbuf_tensor("state", [P, B, KT * PAD], F32))
        resid = ctx.enter_context(nc.sbuf_tensor("resid", [P, B, KT * N], F32))
        ident = ctx.enter_context(nc.sbuf_tensor("ident", [P, P], F32))
        eps_ln = ctx.enter_context(nc.sbuf_tensor("eps_ln", [P, 1], F32))
        begun = ctx.enter_context(nc.semaphore("begun"))
        nc.gpsimd.memset(ident[:, :], 0.0).then_inc(begun, 1)
        nc.gpsimd.memset(eps_ln[:, :], 1e-5).then_inc(begun, 1)
        nc.gpsimd.memset(state[:, :, :], 0.0).then_inc(begun, 1)
        nc.gpsimd.wait_ge(begun, 3)
        nc.gpsimd.affine_select(out=ident[:, :], in_=ident[:, :], compare_op=ALU.not_equal, fill=1.0, base=0,
                                pattern=[[-1, P]], channel_multiplier=1).then_inc(begun, 1)
        nc.gpsimd.wait_ge(begun, 4)
        nc.all_engine_barrier()
        Stretch.made = made
        with ExitStack() as part:
            conditioned_blocks(nc, part, counts, io, ident, eps_ln, state, resid)
        with ExitStack() as part:
            local_layers(nc, part, counts, io, state, ident, eps_ln)
        with ExitStack() as part:
            write_out(nc, part, counts, out, ident, state, resid)
    return made


def shape_tables():
    half = np.arange(0, DH, 2, dtype=np.float64)
    t = np.arange(N, dtype=np.float64)[:, None]
    freqs = t * (1.0 / 10000.0 ** (half / DH))[None, :]
    scale = ((half + 0.4 * DH) / (1.4 * DH))[None, :] ** ((t - N // 2) / (WIN // 2))
    cos, sin = np.cos(freqs), np.sin(freqs)
    c = np.stack([np.concatenate([cos * s, cos * s], 1) for s in (scale, 1 / scale)], 1)
    s = np.stack([np.concatenate([-sin * s, sin * s], 1) for s in (scale, 1 / scale)], 1)
    tile = lambda a: np.ascontiguousarray(a.reshape(NU, P, 2, DH).transpose(1, 0, 2, 3).reshape(P, -1),
                                          dtype=np.float32)
    r, j = np.arange(P)[:, None], np.arange(P)[None, :]
    odd, upper = r >= WIN, j >= WIN
    i, jj = r % WIN, j % WIN
    valid = np.where(odd == upper, jj <= i, jj >= i)
    first = valid & ~(~odd & upper)
    band = np.where(np.concatenate([first, valid], 1), 0.0, -1e30)
    return tile(c), tile(s), band


def lay_out(a):
    cc = np.ascontiguousarray
    rowtile = lambda w: cc(w.reshape(-1, P, w.shape[-1]).transpose(1, 0, 2).reshape(P, -1))
    col = lambda v: v.reshape(-1, P).T

    def slotted(w):
        z = np.zeros((w.shape[0], NH, SLOT), w.dtype)
        z[:, :, :HD] = w.reshape(w.shape[0], NH, HD)
        return z.reshape(w.shape[0], NH * SLOT)

    c, f = "L0_cond_", "L0_ffn_"
    x = {"x": a["x"]}
    ids = np.stack([a["itok_BxS_0_999"], a["itok_BxS_0_4"], a["mask_BxS_ik0"]])
    x["ids"] = cc(ids.reshape(3, B * NU, P).transpose(2, 0, 1).reshape(P, -1))
    x["t_pw"] = np.concatenate([a[c + "pw_g"], a[c + "pw_b"]], 1)
    x["t_ct"] = np.concatenate([a[c + k] for k in ("cp_g", "cp_b", "tm_g", "tm_b")], 1)
    x["t_ms"] = np.concatenate([a[c + "ms_g"], a[c + "ms_b"]], 1)
    x["w_int1"], x["w_int2"] = rowtile(a[c + "int_W1"]), rowtile(a[c + "int_W2"])
    w, bq = a["L0_attn_W_qkv"], a["L0_attn_b_qkv"][None, :]
    x["w_qk"] = rowtile(np.concatenate([slotted(w[:, 0:D]), slotted(w[:, D:2 * D])], 1))
    x["w_v"] = rowtile(w[:, 2 * D:])
    x["w_proj"] = rowtile(a["L0_attn_W_proj"])
    x["k_w"], x["o_w"] = rowtile(a["L0_cond2_k_w"].T), rowtile(a["L0_cond2_o_w"].T)
    x["aff0"], x["aff1"] = cc(a["L0_cond2_k_aff_w"].T), cc(a["L0_cond2_o_aff_w"].T)
    x["fcols"] = cc(np.concatenate(
        [col(a[c + k]) for k in ("mem_b1", "noi_b1", "res_b1", "int_b1")]
        + [col(a["L0_cond2_k_aff_b"]), col(a["L0_cond2_o_aff_b"]), col(a["L0_attn_b_proj"]), col(a["L0_cond2_o_b"])]
        + [col(slotted(bq[:, 0:D])[0]), col(slotted(bq[:, D:2 * D])[0])], 1))
    x["rows"] = np.concatenate([a[c + "int_b2"], a[c + "int_g"], a[c + "int_be"], bq[0, 2 * D:],
                                a["L0_cond2_k_b"]])[None, :]
    x["aw"] = a[c + "aw"][None, :]
    for m, (k, s) in enumerate((("mem", "cond_512"), ("noi", "cond_64"), ("res", "fside_Bx32_0"))):
        x[f"s_t{m}"] = cc(a[s].T)
        x[f"m_w1{m}"] = a[f"{c}{k}_W1"]
        x[f"m_w2{m}"] = rowtile(a[f"{c}{k}_W2"])
    x["m_rows"] = np.concatenate([a[f"{c}{k}_{q}"] for k in ("mem", "noi", "res") for q in ("b2", "g", "be")])[None, :]

    L = DEPTH
    w = a[f + "Wqkv"].reshape(L, KT, P, 3, NG, GC).transpose(0, 2, 1, 4, 3, 5)
    x["w_qkv"] = cc(w.reshape(L, P, -1))
    x["w_o"] = cc(a[f + "Wo"].reshape(L, INNER // P, P, D).transpose(0, 2, 1, 3).reshape(L, P, -1))
    x["w_1"] = cc(a[f + "W1"].reshape(L, KT, P, 2 * DI).transpose(0, 2, 1, 3).reshape(L, P, -1))
    pad = np.zeros((L, NJ * P - DI, D), np.float32)
    x["w_2"] = cc(np.concatenate([a[f + "W2"], pad], 1).reshape(L, NJ, P, D).transpose(0, 2, 1, 3).reshape(L, P, -1))
    cols3 = lambda v: v.reshape(L, -1, P).transpose(0, 2, 1)
    padded = lambda v: np.concatenate([v, np.zeros((L, NJ * P - DI), np.float32)], 1)
    b1 = a[f + "b1"]
    x["cols"] = cc(np.concatenate([cols3(a[f + "ln_g"]), cols3(a[f + "ln_b"]), cols3(padded(b1[:, :DI])),
                                   cols3(padded(b1[:, DI:])), cols3(a[f + "b2"])], 2))
    x["qk_gain"] = np.concatenate([a[f + "q_scale"], a[f + "k_scale"]], 1)
    x["rot_cos"], x["rot_sin"], x["band"] = shape_tables()
    return x


def kernel(**inputs):
    import ml_dtypes
    from concourse import bacc
    from concourse.bass_utils import run_bass_kernel_spmd

    arrays = {k: np.ascontiguousarray(v) for k, v in
              lay_out({k: np.asarray(v) for k, v in inputs.items()}).items()}
    arrays["band"] = arrays["band"].astype(ml_dtypes.bfloat16)
    counts = {}
    for _ in range(2):
        nc = bacc.Bacc("TRN2", target_bir_lowering=False, num_devices=1)
        io = {k: nc.dram_tensor(f"in_{k}", v.shape, mybir.dt.from_np(v.dtype), kind="ExternalInput").ap()
              for k, v in arrays.items()}
        out = nc.dram_tensor("out", (B, N, D), F32, kind="ExternalOutput").ap()
        counts = build(nc, io, out, counts)
    r = run_bass_kernel_spmd(nc, [{f"in_{k}": v for k, v in arrays.items()}], core_ids=[0])
    return r.results[0]["out"]
```
